# Optimizing a Trainium2 kernel written in Bass

```python
import numpy as np
import jax
import jax.numpy as jnp

def _softmax(x, axis=-1):
    return jax.nn.softmax(x, axis=axis)

def _gelu(x):
    return jax.nn.gelu(x, approximate=True)

def _silu(x):
    return jax.nn.silu(x)

def _sigmoid(x):
    return jax.nn.sigmoid(x)

def _layernorm(x, axis=-1, eps=1e-05):
    m = jnp.mean(x, axis=axis, keepdims=True)
    v = jnp.var(x, axis=axis, keepdims=True)
    return (x - m) / jnp.sqrt(v + eps)

def _scatter_add(tgt, idx, src, axis=0):
    return tgt.at[idx].add(src)

def _segment_sum(src, seg, n):
    return jax.ops.segment_sum(src, seg, n)
kernel_name = 'mk_hybrid_d2_jaxref_r8_eae390'

def setup_inputs(seed: int=0):
    np.random.seed(seed)
    _w = jnp.asarray

    def _L0_attn_a_setup():
        import jax, jax.numpy as jnp
        import numpy as np
        H = 16
        D_NOPE = 128
        D_ROPE = 64
        D_QK = 192
        D_V = 128
        THETA = 10000.0
        EPS = 1e-06

        def rmsnorm(x, w):
            x32 = x.astype(jnp.float32)
            x32 = x32 * jax.lax.rsqrt(jnp.mean(x32 * x32, axis=-1, keepdims=True) + EPS)
            return (x32 * w).astype(x.dtype)

        def rope_cos_sin(seq_len, dim, dtype):
            inv_freq = 1.0 / THETA ** (jnp.arange(0, dim, 2, dtype=jnp.float32) / dim)
            t = jnp.arange(seq_len, dtype=jnp.float32)
            freqs = jnp.outer(t, inv_freq)
            return (jnp.cos(freqs).astype(dtype), jnp.sin(freqs).astype(dtype))

        def apply_rope(x, cos, sin):
            d2 = x.shape[-1] // 2
            x1, x2 = (x[..., :d2], x[..., d2:])
            c = cos[None, :, None, :]
            s = sin[None, :, None, :]
            return jnp.concatenate([x1 * c - x2 * s, x2 * c + x1 * s], axis=-1)
        key = jax.random.key(seed)
        ks = jax.random.split(key, 8)
        B, T, D = (2, 256, 256)
        q_lora, kv_lora = (192, 64)

        def w(k, fan_in, fan_out):
            return jax.random.normal(k, (fan_in, fan_out), dtype=jnp.float32) * (1.0 / np.sqrt(fan_in))
        return {'hidden_states': jax.random.normal(ks[0], (B, T, D), dtype=jnp.float32), 'Wq_a': w(ks[1], D, q_lora), 'q_norm_w': jnp.ones((q_lora,), dtype=jnp.float32), 'Wq_b': w(ks[2], q_lora, H * D_QK), 'Wk_rope': w(ks[3], D, D_ROPE), 'Wkv_a': w(ks[4], D, kv_lora), 'kv_norm_w': jnp.ones((kv_lora,), dtype=jnp.float32), 'Wkv_b': w(ks[5], kv_lora, H * (D_NOPE + D_V)), 'Wo': w(ks[6], H * D_V, D)}
    _L0_attn_a_in = _L0_attn_a_setup()

    def _L0_attn_b_setup():
        import jax, jax.numpy as jnp
        import numpy as np
        D_MODEL = 256
        B, S = (2, 256)
        key = jax.random.key(seed)
        kx, kq, kk, kv, ko = jax.random.split(key, 5)
        std = 1.0 / np.sqrt(D_MODEL)
        return {'x': jax.random.normal(kx, (B, S, D_MODEL), dtype=jnp.float32), 'W_q': jax.random.normal(kq, (D_MODEL, D_MODEL), dtype=jnp.float32) * std, 'W_k': jax.random.normal(kk, (D_MODEL, D_MODEL), dtype=jnp.float32) * std, 'W_v': jax.random.normal(kv, (D_MODEL, D_MODEL), dtype=jnp.float32) * std, 'W_o': jax.random.normal(ko, (D_MODEL, D_MODEL), dtype=jnp.float32) * std}
    _L0_attn_b_in = _L0_attn_b_setup()

    def _L0_ffn_setup():
        import jax, jax.numpy as jnp
        import numpy as np
        from jax import lax
        TOP_K = 2
        N_EXPERTS = 8
        key = jax.random.key(seed)
        ks = jax.random.split(key, 7)
        B, S, H, I, E = (4, 256, 256, 176, N_EXPERTS)
        s_h = 1.0 / np.sqrt(H)
        s_i = 1.0 / np.sqrt(I)
        return {'hidden_states': jax.random.normal(ks[0], (B, S, H), jnp.float32), 'gate_w': jax.random.normal(ks[1], (E, H), jnp.float32) * s_h, 'w1': jax.random.normal(ks[2], (E, H, 2 * I), jnp.float32) * s_h, 'w2': jax.random.normal(ks[3], (E, I, H), jnp.float32) * s_i, 'sw1': jax.random.normal(ks[4], (I, H), jnp.float32) * s_h, 'sw2': jax.random.normal(ks[5], (I, H), jnp.float32) * s_h, 'sw3': jax.random.normal(ks[6], (H, I), jnp.float32) * s_i}
    _L0_ffn_in = _L0_ffn_setup()

    def _L1_attn_a_setup():
        import jax, jax.numpy as jnp
        import numpy as np
        HIDDEN = 256
        HEADS = 16
        HEAD_DIM = HIDDEN // HEADS
        NEG = -10000000000.0
        key = jax.random.key(seed)
        k1, k2, k3 = jax.random.split(key, 3)
        x = jax.random.normal(k1, (2, 256, HIDDEN), dtype=jnp.float32)
        w_qkv = jax.random.normal(k2, (HIDDEN, 3 * HIDDEN), dtype=jnp.float32) / np.sqrt(HIDDEN)
        w_out = jax.random.normal(k3, (HIDDEN, HIDDEN), dtype=jnp.float32) / np.sqrt(HIDDEN)
        return {'x': x, 'w_qkv': w_qkv, 'w_out': w_out}
    _L1_attn_a_in = _L1_attn_a_setup()

    def _L1_attn_b_setup():
        import jax, jax.numpy as jnp
        import numpy as np
        from jax import lax
        B, L, D = (4, 256, 256)
        R = 256
        DH = D // 4
        key = jax.random.key(seed)
        ks = jax.random.split(key, 12)
        s = 0.02
        x = jax.random.normal(ks[0], (B, L, D), dtype=jnp.float32)
        Wu = jax.random.normal(ks[1], (R, D), dtype=jnp.float32) * s
        bu = jnp.zeros((R,), dtype=jnp.float32)
        Wv = jax.random.normal(ks[2], (R, D), dtype=jnp.float32) * s
        bv = jnp.zeros((R,), dtype=jnp.float32)
        Wg1 = jax.random.normal(ks[3], (DH, D), dtype=jnp.float32) * s
        bg1 = jnp.zeros((DH,), dtype=jnp.float32)
        Wg2 = jax.random.normal(ks[4], (R, DH), dtype=jnp.float32) * s
        bg2 = jnp.zeros((R,), dtype=jnp.float32)
        conv_w = jax.random.normal(ks[5], (D, 1, 3), dtype=jnp.float32) * s
        conv_b = jnp.zeros((D,), dtype=jnp.float32)
        return {'x': x, 'Wu': Wu, 'bu': bu, 'Wv': Wv, 'bv': bv, 'Wg1': Wg1, 'bg1': bg1, 'Wg2': Wg2, 'bg2': bg2, 'conv_w': conv_w, 'conv_b': conv_b}
    _L1_attn_b_in = _L1_attn_b_setup()

    def _L1_ffn_setup():
        import jax, jax.numpy as jnp
        import numpy as np
        B, S, D, H = (4, 256, 256, 1024)

        def fwht(x):
            orig_shape = x.shape
            n = orig_shape[-1]
            x = x.reshape(-1, n)
            h = 1
            while h < n:
                xb = x.reshape(-1, n // (2 * h), 2, h)
                a = xb[:, :, 0, :]
                b = xb[:, :, 1, :]
                x = jnp.stack([a + b, a - b], axis=2).reshape(-1, n)
                h *= 2
            scale = jnp.asarray(1.0 / np.sqrt(n), dtype=x.dtype)
            return (x * scale).reshape(orig_shape)
        key = jax.random.key(seed)
        kx, k1, k2, k3 = jax.random.split(key, 4)
        x = jax.random.normal(kx, (B, S, D), dtype=jnp.float32)
        W1 = jax.random.normal(k1, (H, D), dtype=jnp.float32) * (1.0 / np.sqrt(D))
        W2 = jax.random.normal(k2, (D, H), dtype=jnp.float32) * (1.0 / np.sqrt(H))
        W3 = jax.random.normal(k3, (H, D), dtype=jnp.float32) * (1.0 / np.sqrt(D))
        return {'x': x, 'W1': W1, 'W2': W2, 'W3': W3}
    _L1_ffn_in = _L1_ffn_setup()
    _d = {'L0_attn_a_hidden_states': _L0_attn_a_in['hidden_states'], 'L0_attn_a_Wq_a': _L0_attn_a_in['Wq_a'], 'L0_attn_a_q_norm_w': _L0_attn_a_in['q_norm_w'], 'L0_attn_a_Wq_b': _L0_attn_a_in['Wq_b'], 'L0_attn_a_Wk_rope': _L0_attn_a_in['Wk_rope'], 'L0_attn_a_Wkv_a': _L0_attn_a_in['Wkv_a'], 'L0_attn_a_kv_norm_w': _L0_attn_a_in['kv_norm_w'], 'L0_attn_a_Wkv_b': _L0_attn_a_in['Wkv_b'], 'L0_attn_a_Wo': _L0_attn_a_in['Wo'], 'L0_attn_b_W_q': _L0_attn_b_in['W_q'], 'L0_attn_b_W_k': _L0_attn_b_in['W_k'], 'L0_attn_b_W_v': _L0_attn_b_in['W_v'], 'L0_attn_b_W_o': _L0_attn_b_in['W_o'], 'L0_ffn_gate_w': _L0_ffn_in['gate_w'], 'L0_ffn_w1': _L0_ffn_in['w1'], 'L0_ffn_w2': _L0_ffn_in['w2'], 'L0_ffn_sw1': _L0_ffn_in['sw1'], 'L0_ffn_sw2': _L0_ffn_in['sw2'], 'L0_ffn_sw3': _L0_ffn_in['sw3'], 'L1_attn_a_w_qkv': _L1_attn_a_in['w_qkv'], 'L1_attn_a_w_out': _L1_attn_a_in['w_out'], 'L1_attn_b_Wu': _L1_attn_b_in['Wu'], 'L1_attn_b_bu': _L1_attn_b_in['bu'], 'L1_attn_b_Wv': _L1_attn_b_in['Wv'], 'L1_attn_b_bv': _L1_attn_b_in['bv'], 'L1_attn_b_Wg1': _L1_attn_b_in['Wg1'], 'L1_attn_b_bg1': _L1_attn_b_in['bg1'], 'L1_attn_b_Wg2': _L1_attn_b_in['Wg2'], 'L1_attn_b_bg2': _L1_attn_b_in['bg2'], 'L1_attn_b_conv_w': _L1_attn_b_in['conv_w'], 'L1_attn_b_conv_b': _L1_attn_b_in['conv_b'], 'L1_ffn_W1': _L1_ffn_in['W1'], 'L1_ffn_W2': _L1_ffn_in['W2'], 'L1_ffn_W3': _L1_ffn_in['W3']}
    _x0 = _d['L0_attn_a_hidden_states']
    _d['L0_attn_a_hidden_states'] = jax.random.normal(jax.random.fold_in(jax.random.key(seed), 1), (1, 1024, 256), dtype=_x0.dtype)
    del _x0
    return _d

def reference(L0_attn_a_hidden_states, L0_attn_a_Wq_a, L0_attn_a_q_norm_w, L0_attn_a_Wq_b, L0_attn_a_Wk_rope, L0_attn_a_Wkv_a, L0_attn_a_kv_norm_w, L0_attn_a_Wkv_b, L0_attn_a_Wo, L0_attn_b_W_q, L0_attn_b_W_k, L0_attn_b_W_v, L0_attn_b_W_o, L0_ffn_gate_w, L0_ffn_w1, L0_ffn_w2, L0_ffn_sw1, L0_ffn_sw2, L0_ffn_sw3, L1_attn_a_w_qkv, L1_attn_a_w_out, L1_attn_b_Wu, L1_attn_b_bu, L1_attn_b_Wv, L1_attn_b_bv, L1_attn_b_Wg1, L1_attn_b_bg1, L1_attn_b_Wg2, L1_attn_b_bg2, L1_attn_b_conv_w, L1_attn_b_conv_b, L1_ffn_W1, L1_ffn_W2, L1_ffn_W3):

    def _L0_attn_a_ref(hidden_states, Wq_a, q_norm_w, Wq_b, Wk_rope, Wkv_a, kv_norm_w, Wkv_b, Wo):
        import jax, jax.numpy as jnp
        import numpy as np
        H = 16
        D_NOPE = 128
        D_ROPE = 64
        D_QK = 192
        D_V = 128
        THETA = 10000.0
        EPS = 1e-06

        def rmsnorm(x, w):
            x32 = x.astype(jnp.float32)
            x32 = x32 * jax.lax.rsqrt(jnp.mean(x32 * x32, axis=-1, keepdims=True) + EPS)
            return (x32 * w).astype(x.dtype)

        def rope_cos_sin(seq_len, dim, dtype):
            inv_freq = 1.0 / THETA ** (jnp.arange(0, dim, 2, dtype=jnp.float32) / dim)
            t = jnp.arange(seq_len, dtype=jnp.float32)
            freqs = jnp.outer(t, inv_freq)
            return (jnp.cos(freqs).astype(dtype), jnp.sin(freqs).astype(dtype))

        def apply_rope(x, cos, sin):
            d2 = x.shape[-1] // 2
            x1, x2 = (x[..., :d2], x[..., d2:])
            c = cos[None, :, None, :]
            s = sin[None, :, None, :]
            return jnp.concatenate([x1 * c - x2 * s, x2 * c + x1 * s], axis=-1)
        B, T, D = hidden_states.shape
        q = rmsnorm(hidden_states @ Wq_a, q_norm_w) @ Wq_b
        q = q.reshape(B, T, H, D_QK)
        q_pass, q_rot = (q[..., :D_NOPE], q[..., D_NOPE:])
        kv = rmsnorm(hidden_states @ Wkv_a, kv_norm_w) @ Wkv_b
        kv = kv.reshape(B, T, H, D_NOPE + D_V)
        k_pass, v = (kv[..., :D_NOPE], kv[..., D_NOPE:])
        k_rot = (hidden_states @ Wk_rope)[:, :, None, :]
        cos, sin = rope_cos_sin(T, D_ROPE, hidden_states.dtype)
        q_rot = apply_rope(q_rot, cos, sin)
        k_rot = apply_rope(k_rot, cos, sin)
        k_rot = jnp.broadcast_to(k_rot, (B, T, H, D_ROPE))
        qf = jnp.concatenate([q_pass, q_rot], axis=-1)
        kf = jnp.concatenate([k_pass, k_rot], axis=-1)
        scale = 1.0 / np.sqrt(D_QK)
        scores = jnp.einsum('bqhd,bkhd->bhqk', qf, kf) * scale
        mask = jnp.tril(jnp.ones((T, T), dtype=bool))
        scores = jnp.where(mask[None, None], scores, jnp.finfo(scores.dtype).min)
        p = jax.nn.softmax(scores, axis=-1)
        o = jnp.einsum('bhqk,bkhd->bqhd', p, v)
        o = o.reshape(B, T, H * D_V) @ Wo
        return o

    def _L0_attn_b_ref(x, W_q, W_k, W_v, W_o):
        import jax, jax.numpy as jnp
        import numpy as np
        D_MODEL = 256
        B, S = (2, 256)
        scale = 1.0 / jnp.sqrt(jnp.asarray(x.shape[-1], x.dtype))
        Q = jnp.einsum('bsd,de->bse', x, W_q)
        K = jnp.einsum('bsd,de->bse', x, W_k)
        V = jnp.einsum('bsd,de->bse', x, W_v)
        scores = jnp.einsum('bqe,bke->bqk', Q, K) * scale
        attn = jax.nn.softmax(scores, axis=-1)
        out = jnp.einsum('bqk,bke->bqe', attn, V)
        return jnp.einsum('bse,ed->bsd', out, W_o)

    def _L0_ffn_ref(hidden_states, gate_w, w1, w2, sw1, sw2, sw3):
        import jax, jax.numpy as jnp
        import numpy as np
        from jax import lax
        TOP_K = 2
        N_EXPERTS = 8
        B, S, H = hidden_states.shape
        x = hidden_states.reshape(-1, H)
        T = x.shape[0]
        logits = jnp.einsum('th,eh->te', x.astype(jnp.float32), gate_w.astype(jnp.float32))
        scores = jax.nn.softmax(logits, axis=-1)
        topk_w, topk_idx = lax.top_k(scores, TOP_K)
        topk_w = topk_w / (topk_w.sum(-1, keepdims=True) + 1e-20)
        topk_w = topk_w.astype(hidden_states.dtype)
        cw = jnp.zeros((T, N_EXPERTS), hidden_states.dtype).at[jnp.arange(T)[:, None], topk_idx].add(topk_w)

        def body(acc, ew):
            w1e, w2e, cwe = ew
            h = x @ w1e
            g, u = jnp.split(h, 2, axis=-1)
            y = jax.nn.silu(g) * u @ w2e
            return (acc + cwe[:, None] * y, None)
        moe, _ = lax.scan(body, jnp.zeros_like(x), (w1, w2, cw.T))
        moe = moe.reshape(B, S, H)
        shared = jnp.einsum('bsi,hi->bsh', jax.nn.silu(jnp.einsum('bsh,ih->bsi', hidden_states, sw1)) * jnp.einsum('bsh,ih->bsi', hidden_states, sw2), sw3)
        return moe + shared

    def _L1_attn_a_ref(x, w_qkv, w_out):
        import jax, jax.numpy as jnp
        import numpy as np
        HIDDEN = 256
        HEADS = 16
        HEAD_DIM = HIDDEN // HEADS
        NEG = -10000000000.0
        b, s, _ = x.shape
        qkv = x @ w_qkv
        qkv = qkv.reshape(b, s, 3, HEADS, HEAD_DIM)
        q, k, v = (qkv[:, :, 0], qkv[:, :, 1], qkv[:, :, 2])
        scale = jnp.sqrt(jnp.float32(HEAD_DIM)).astype(x.dtype)
        q = q / scale
        scores = jnp.einsum('bqhd,bkhd->bhqk', q, k)
        causal_mask = jnp.arange(s)[:, None] >= jnp.arange(s)[None, :]
        scores = jnp.where(causal_mask[None, None], scores, NEG)
        attn = jax.nn.softmax(scores, axis=-1)
        out = jnp.einsum('bhqk,bkhd->bqhd', attn, v).reshape(b, s, HIDDEN)
        return out @ w_out

    def _L1_attn_b_ref(x, Wu, bu, Wv, bv, Wg1, bg1, Wg2, bg2, conv_w, conv_b):
        import jax, jax.numpy as jnp
        import numpy as np
        from jax import lax
        B, L, D = (4, 256, 256)
        R = 256
        DH = D // 4
        xc = jnp.transpose(x, (0, 2, 1))
        t = lax.conv_general_dilated(xc, conv_w, window_strides=(1,), padding=[(1, 1)], dimension_numbers=('NCH', 'OIH', 'NCH'), feature_group_count=D)
        t_out = jnp.transpose(t + conv_b[None, :, None], (0, 2, 1))
        u = jnp.einsum('bld,rd->blr', x, Wu) + bu
        v = jnp.einsum('bld,rd->blr', x, Wv) + bv
        h = jax.nn.relu(jnp.einsum('bld,hd->blh', x, Wg1) + bg1)
        gates = jax.nn.sigmoid(jnp.einsum('blh,rh->blr', h, Wg2) + bg2)
        u_gated = u * gates
        v_gated = v * gates
        k_cumsum = jnp.cumsum(u_gated, axis=1)
        global_out = k_cumsum * v_gated
        uv_term = jnp.einsum('blr,rd->bld', global_out, Wu.T[:R, :])
        return t_out + uv_term

    def _L1_ffn_ref(x, W1, W2, W3):
        import jax, jax.numpy as jnp
        import numpy as np
        B, S, D, H = (4, 256, 256, 1024)

        def fwht(x):
            orig_shape = x.shape
            n = orig_shape[-1]
            x = x.reshape(-1, n)
            h = 1
            while h < n:
                xb = x.reshape(-1, n // (2 * h), 2, h)
                a = xb[:, :, 0, :]
                b = xb[:, :, 1, :]
                x = jnp.stack([a + b, a - b], axis=2).reshape(-1, n)
                h *= 2
            scale = jnp.asarray(1.0 / np.sqrt(n), dtype=x.dtype)
            return (x * scale).reshape(orig_shape)
        up_gate = jnp.einsum('bsd,hd->bsh', x, W1)
        up_lin = jnp.einsum('bsd,hd->bsh', x, W3)
        hidden = jax.nn.silu(up_gate) * up_lin
        hidden = fwht(hidden)
        out = jnp.einsum('bsh,dh->bsd', hidden, W2)
        return out
    x = L0_attn_a_hidden_states
    x = x + _L0_attn_a_ref(_layernorm(x, axis=-1), L0_attn_a_Wq_a, L0_attn_a_q_norm_w, L0_attn_a_Wq_b, L0_attn_a_Wk_rope, L0_attn_a_Wkv_a, L0_attn_a_kv_norm_w, L0_attn_a_Wkv_b, L0_attn_a_Wo)
    x = x + _L0_ffn_ref(_layernorm(x, axis=-1), L0_ffn_gate_w, L0_ffn_w1, L0_ffn_w2, L0_ffn_sw1, L0_ffn_sw2, L0_ffn_sw3)
    x = x + _L0_attn_b_ref(_layernorm(x, axis=-1), L0_attn_b_W_q, L0_attn_b_W_k, L0_attn_b_W_v, L0_attn_b_W_o)
    x = x + _L0_ffn_ref(_layernorm(x, axis=-1), L0_ffn_gate_w, L0_ffn_w1, L0_ffn_w2, L0_ffn_sw1, L0_ffn_sw2, L0_ffn_sw3)
    x = x + _L1_attn_a_ref(_layernorm(x, axis=-1), L1_attn_a_w_qkv, L1_attn_a_w_out)
    x = x + _L1_ffn_ref(_layernorm(x, axis=-1), L1_ffn_W1, L1_ffn_W2, L1_ffn_W3)
    x = x + _L1_attn_b_ref(_layernorm(x, axis=-1), L1_attn_b_Wu, L1_attn_b_bu, L1_attn_b_Wv, L1_attn_b_bv, L1_attn_b_Wg1, L1_attn_b_bg1, L1_attn_b_Wg2, L1_attn_b_bg2, L1_attn_b_conv_w, L1_attn_b_conv_b)
    x = x + _L1_ffn_ref(_layernorm(x, axis=-1), L1_ffn_W1, L1_ffn_W2, L1_ffn_W3)
    return x

_drawn_inputs = setup_inputs


def setup_inputs(seed=0):
    import zlib

    import numpy as np

    out = dict(_drawn_inputs(seed))
    spreads = {'L0_attn_a_q_norm_w': (1.0, 0.2),
     'L0_attn_a_kv_norm_w': (1.0, 0.2),
     'L1_attn_b_bu': (0.0, 0.1),
     'L1_attn_b_bv': (0.0, 0.1),
     'L1_attn_b_bg1': (0.0, 0.8),
     'L1_attn_b_bg2': (0.0, 0.1),
     'L1_attn_b_conv_b': (0.0, 0.1)}
    factors = {'L1_attn_b_Wg1': 5.322, 'L1_attn_b_Wg2': 3.125, 'L1_attn_b_conv_w': 4.107}
    for name, (base, spread) in spreads.items():
        noise = np.random.default_rng([zlib.crc32(name.encode()), seed]).standard_normal(out[name].shape)
        drawn = base * np.exp(spread * noise) if base else spread * noise
        out[name] = jnp.asarray(drawn.astype(out[name].dtype))
    for name, factor in factors.items():
        out[name] = (out[name] * factor).astype(out[name].dtype)
    return out
```

```python
from contextlib import ExitStack

import concourse.bass as bass
from concourse import mybir

ALU = mybir.AluOpType
ACT = mybir.ActivationFunctionType
AX = mybir.AxisListType.X
F32 = mybir.dt.float32
F32R = mybir.dt.float32r
BF16 = mybir.dt.bfloat16

P = 128
T, D = 1024, 256
NT = T // P
KD = D // P
LN_EPS = 1e-5

H = 16
NP = H // 2
QL, KL, DR, DN = 192, 64, 64, 128
QR1 = QL - P
WA_N = QL + KL + DR
RMS_EPS = 1e-6
WH_N = QL + KL + KL + D

NE, FI = 8, 176
BLK = 2 * FI
W1_N = (NE + 1) * BLK + NE
FH = (NE + 1) * FI
NF = (FH + P - 1) // P
FTAIL = FH - (NF - 1) * P

HD = D // H
FF = 1024
NFF = FF // P


def ds(start, size):
    return bass.ds(start, size)


class Bufs:

    def __init__(self, nc, ctx, tag):
        self.nc, self.ctx, self.tag = nc, ctx, tag

    def sb(self, name, shape, dt=F32):
        return self.ctx.enter_context(self.nc.sbuf_tensor(f"{self.tag}_{name}", shape, dt))

    def ps(self, name, shape, dt=F32):
        return self.ctx.enter_context(self.nc.psum_tensor(f"{self.tag}_{name}", shape, dt))

    def sem(self, name):
        return self.ctx.enter_context(self.nc.semaphore(f"{self.tag}_{name}"))


def split3(pe, out, lhs, rhs, start, stop):
    (lh, ll), (rh, rl) = lhs, rhs
    pe.matmul(out, lh, rh, start=start, stop=False)
    pe.matmul(out, lh, rl, start=False, stop=False)
    return pe.matmul(out, ll, rh, start=False, stop=stop)


def staged(stages, eng, step):
    for i in range(stages):
        step(i, *[s <= i for s in range(stages)], i)
    with eng.Fori(stages, NT) as i:
        step(i, *[True] * stages, stages)
    for i in range(NT, NT + stages - 1):
        step(i, *[s > i - NT for s in range(stages)], i)


class LayerNorm:

    def __init__(self, b, g):
        self.g = g
        self.stats = b.sb("ln_stats", [P, 6])
        self.mean_var = b.sb("ln_mean_var", [P, 2])
        self.var_eps = b.sb("ln_var_eps", [P, 1])
        self.rstd = b.sb("ln_rstd", [P, 1])
        self.xn = b.sb("ln_xn", [P, D])
        self.waiter = b.sb("ln_waiter", [1, 1])
        self.stats_done = b.sem("ln_stats_done")
        self.aggr_done = b.sem("ln_aggr_done")
        self.var_done = b.sem("ln_var_done")
        self.rstd_done = b.sem("ln_rstd_done")
        self.xn_done = b.sem("ln_xn_done")
        self.xn_read = b.sem("ln_xn_read")

    def vector_stats(self, v, t, n):
        v.bn_stats(self.stats[:], self.g.X[:, ds(t * D, D)]).then_inc(self.stats_done, 1)
        v.wait_ge(self.stats_done, n + 1)
        v.memset(self.waiter[:], 0.0)
        v.bn_aggr(self.mean_var[:], self.stats[:]).then_inc(self.aggr_done, 1)
        v.wait_ge(self.aggr_done, n + 1)
        v.tensor_scalar(self.var_eps[:], self.mean_var[:, 1:2], LN_EPS, None, ALU.add).then_inc(self.var_done, 1)

    def gpsimd_power(self, pool, n):
        pool.wait_ge(self.var_done, n + 1)
        pool.tensor_tensor(self.rstd[:], self.var_eps[:], self.g.neg_half[:, 0:1], ALU.pow).then_inc(self.rstd_done, 1)

    def vector_scale(self, v, t, n, first):
        v.wait_ge(self.rstd_done, n + 1)
        if not first:
            v.wait_ge(self.xn_read, n)
        v.tensor_scalar(self.xn[:], self.g.X[:, ds(t * D, D)], self.mean_var[:, 0:1], self.rstd[:, 0:1],
                        ALU.subtract, ALU.mult).then_inc(self.xn_done, 1)

    def tensor_transpose(self, pe, out, n):
        pe.wait_ge(self.xn_done, n + 1)
        for c in range(KD):
            mm = pe.transpose(out[:, c * P:(c + 1) * P], self.xn[:, c * P:(c + 1) * P], self.g.ident[:])
        mm.then_inc(self.xn_read, 1)


def latent_projections(nc, g, dram):
    with ExitStack() as ctx:
        b = Bufs(nc, ctx, "a1")
        ln = LayerNorm(b, g)
        wa_h = b.sb("wa_h", [P, KD, WA_N], F32R)
        wa_l = b.sb("wa_l", [P, KD, WA_N], F32R)
        xt_h = b.sb("xt_h", [P, KD * P], F32R)
        xt_l = b.sb("xt_l", [P, KD * P], F32R)
        square = b.sb("square", [P, QL])
        sumsq = b.sb("sumsq", [P, 2])
        meansq = b.sb("meansq", [P, 2])
        rrms = b.sb("rrms", [P, 2])
        qa = b.sb("qa", [P, QL])
        kck = b.sb("kck", [P, 3, DR])
        krc = b.sb("krc", [P, DR])
        krs = b.sb("krs", [P, DR])
        qat0 = b.sb("qat0", [P, P])
        qat1 = b.sb("qat1", [QR1, P])
        rot = g.u_space[:, 2048:3072].rearrange("p (h c) -> p h c", c=DR)
        rot_s = g.u_space[:, 3072:4096].rearrange("p (h c) -> p h c", c=DR)
        qr = b.sb("qr", [P, H * DR])
        rot_c = qr[:].rearrange("p (h c) -> p h c", c=DR)
        ps_x = b.ps("ps_x", [P, 512])
        ps_a = b.ps("ps_a", [P, 512])
        ps_t = b.ps("ps_t", [P, 512])
        ps_r = b.ps("ps_r", [P, 2, 512])
        ps_q = b.ps("ps_q", [P, 2, 512])
        wa_split = b.sem("wa_split")
        wr_scaled = b.sem("wr_scaled")
        xt_hi = b.sem("xt_hi")
        xt_lo = b.sem("xt_lo")
        proj_done = b.sem("proj_done")
        sumsq_done = b.sem("sumsq_done")
        meansq_done = b.sem("meansq_done")
        rrms_done = b.sem("rrms_done")
        kr_parts = b.sem("kr_parts")
        kr_done = b.sem("kr_done")
        latents_done = b.sem("latents_done")
        key_copied = b.sem("key_copied")
        lat_t_done = b.sem("lat_t_done")
        lat_evac = b.sem("lat_evac")
        key_lo = b.sem("key_lo")
        qat_kept = b.sem("qat_kept")
        rope_mm = b.sem("rope_mm")
        rot_copied = b.sem("rot_copied")
        rot_s_done = b.sem("rot_s_done")
        rot_c_done = b.sem("rot_c_done")
        qr_done = b.sem("qr_done")
        qr_t_done = b.sem("qr_t_done")
        qr_evac = b.sem("qr_evac")
        block = ctx.enter_context(nc.Block())


        @block.tensor
        def _(pe):
            def step(i, one, two, three, least):
                if two:
                    t = i - 1
                    pe.wait_ge(latents_done, 2 * t + 2)
                    pe.wait_ge(key_copied, t + 1)
                    if least >= 2:
                        pe.wait_ge(lat_evac, 3 * t)
                        pe.wait_ge(key_lo, t)
                    pe.transpose(ps_t[:, 0:P], qa[:, 0:P], g.ident[:])
                    pe.transpose(ps_t[0:QR1, P:2 * P], qa[:, P:QL], g.ident[:])
                    pe.transpose(ps_t[:, 2 * P:3 * P], kck[:, 0:2, :], g.ident[:])
                    pe.transpose(ps_t[:, 3 * P:4 * P], kck[:, 1:3, :], g.ident[:]).then_inc(lat_t_done, 1)
                if three:
                    t = i - 2
                    pe.wait_ge(qr_done, t + 1)
                    if least >= 3:
                        pe.wait_ge(qr_evac, 2 * t)
                    for c in range(NP):
                        mm = pe.transpose(ps_q[:, c // 4, (c % 4) * P:(c % 4 + 1) * P], qr[:, c * P:(c + 1) * P],
                                          g.ident[:])
                    mm.then_inc(qr_t_done, 1)
                if two:
                    t = i - 1
                    pe.wait_ge(lat_evac, 3 * t + 2)
                    if least >= 2:
                        pe.wait_ge(rot_copied, t)
                        pe.wait_ge(rot_c_done, t)
                    if least == 1:
                        pe.wait_ge(wr_scaled, 2)
                    for n in range(2):
                        pe.matmul(ps_r[:, n, :], qat0[:], g.wr0[:, n * 512:(n + 1) * 512], start=True, stop=False)
                        mm = pe.matmul(ps_r[:, n, :], qat1[:], g.wr1[:, n * 512:(n + 1) * 512], start=False, stop=True)
                    mm.then_inc(rope_mm, 1)
                if one:
                    if least >= 1:
                        pe.wait_ge(xt_hi, i)
                        pe.wait_ge(xt_lo, i)
                    ln.tensor_transpose(pe, ps_x, i)
                    pe.wait_ge(xt_hi, i + 1)
                    pe.wait_ge(xt_lo, i + 1)
                    if least == 0:
                        pe.wait_ge(wa_split, 2)
                    if least >= 1:
                        pe.wait_ge(latents_done, 2 * i)
                        pe.wait_ge(kr_parts, 2 * i)
                    for c in range(KD):
                        cs = slice(c * P, (c + 1) * P)
                        mm = split3(pe, ps_a[:, 0:WA_N], (xt_h[:, cs], xt_l[:, cs]), (wa_h[:, c, :], wa_l[:, c, :]),
                                    c == 0, c == KD - 1)
                    mm.then_inc(proj_done, 1)

            pe.wait_ge(g.loaded_const, 16 * g.N_CONST)
            staged(3, pe, step)

        @block.scalar
        def _(act):
            def step(i, one, two, three, least):
                if two:
                    t = i - 1
                    act.wait_ge(lat_t_done, t + 1)
                    if least >= 2:
                        act.wait_ge(rope_mm, t)
                        act.wait_ge(qat_kept, 2 * t)
                    act.activation(qat0[:], ps_t[:, 0:P], ACT.Copy).then_inc(lat_evac, 1)
                    act.activation(qat1[:], ps_t[0:QR1, P:2 * P], ACT.Copy).then_inc(lat_evac, 1)
                    act.activation(g.kt_h[:, :, ds(t * P, P)], ps_t[:, 2 * P:4 * P].rearrange("p (a c) -> p a c", a=2),
                                   ACT.Copy).then_inc(lat_evac, 1)
                if three:
                    t = i - 2
                    act.wait_ge(qr_t_done, t + 1)
                    act.activation(g.qrt[:, 0:4, ds(t * P, P)], ps_q[:, 0, :].rearrange("p (a c) -> p a c", a=4),
                                   ACT.Copy).then_inc(qr_evac, 1)
                if two:
                    t = i - 1
                    act.wait_ge(rope_mm, t + 1)
                    if least >= 2:
                        act.wait_ge(rot_s_done, t)
                    act.activation(rot, ps_r[:].rearrange("p a (h c) -> p (a h) c", c=DR),
                                   ACT.Copy).then_inc(rot_copied, 1)
                if one:
                    act.wait_ge(ln.xn_read, i + 1)
                    if least >= 1:
                        act.wait_ge(proj_done, i)
                    act.activation(xt_h[:], ps_x[:, 0:KD * P], ACT.Copy).then_inc(xt_hi, 1)
                    act.wait_ge(proj_done, i + 1)
                    if least >= 1:
                        act.wait_ge(meansq_done, 2 * i)
                    act.activation(square[:], ps_a[:, 0:QL], ACT.Square,
                                   accum_out=sumsq[:, 0:1]).then_inc(sumsq_done, 1)
                    act.wait_ge(sumsq_done, 2 * i + 1)
                    act.activation(square[:, 0:KL], ps_a[:, QL:QL + KL], ACT.Square,
                                   accum_out=sumsq[:, 1:2]).then_inc(sumsq_done, 1)
                    act.wait_ge(kr_done, i + 1)
                    act.activation(kck[:, 2, :], kck[:, 0, :], ACT.Copy).then_inc(key_copied, 1)
            staged(3, act, step)

        @block.vector
        def _(v):
            def step(i, one, two, three, least):
                if one:
                    ln.vector_stats(v, i, i)
                if two:
                    t = i - 1
                    v.wait_ge(lat_evac, 3 * t + 3)
                    v.tensor_tensor(g.kt_l[:, :, ds(t * P, P)], ps_t[:, 2 * P:4 * P].rearrange("p (a c) -> p a c", a=2),
                                    g.kt_h[:, :, ds(t * P, P)].bitcast(F32), ALU.subtract).then_inc(key_lo, 1)
                if one:
                    ln.vector_scale(v, i, i, least == 0)
                if three:
                    t = i - 2
                    v.wait_ge(qr_t_done, t + 1)
                    v.tensor_copy(g.qrt[:, 4:8, ds(t * P, P)],
                                  ps_q[:, 1, :].rearrange("p (a c) -> p a c", a=4)).then_inc(qr_evac, 1)
                if two:
                    t = i - 1
                    v.wait_ge(rope_mm, t + 1)
                    v.wait_ge(rot_copied, t + 1)
                    if least >= 2:
                        v.wait_ge(qr_t_done, t)
                    v.tensor_tensor(rot_c, ps_r[:].rearrange("p a (h c) -> p (a h) c", c=DR),
                                    g.cos_q[:, ds(t, 1), :].broadcast_to([P, H, DR]), ALU.mult).then_inc(rot_c_done, 1)
                if one:
                    v.wait_ge(ln.xn_read, i + 1)
                    v.wait_ge(xt_hi, i + 1)
                    if least >= 1:
                        v.wait_ge(proj_done, i)
                    v.tensor_tensor(xt_l[:], ps_x[:, 0:KD * P], xt_h[:].bitcast(F32), ALU.subtract).then_inc(xt_lo, 1)
                if two:
                    t = i - 1
                    v.wait_ge(rot_c_done, t + 1)
                    v.wait_ge(rot_s_done, t + 1)
                    v.tensor_tensor(qr[:].rearrange("p (h c) -> p h c", c=DR), rot_c, rot_s,
                                    ALU.add).then_inc(qr_done, 1)
                if one:
                    v.wait_ge(sumsq_done, 2 * i + 2)
                    v.tensor_scalar(meansq[:, 0:1], sumsq[:, 0:1], 1.0 / QL, RMS_EPS, ALU.mult,
                                    ALU.add).then_inc(meansq_done, 1)
                    v.tensor_scalar(meansq[:, 1:2], sumsq[:, 1:2], 1.0 / KL, RMS_EPS, ALU.mult,
                                    ALU.add).then_inc(meansq_done, 1)
                    key = ps_a[:, QL + KL:WA_N]
                    v.tensor_tensor(krc[:], key, g.cos_k[:, ds(i, 1), :].squeeze(1), ALU.mult).then_inc(kr_parts, 1)
                    swapped = key.rearrange("p (a c) -> p a c", a=2)[:, ::-1, :]
                    v.tensor_tensor(krs[:].rearrange("p (a c) -> p a c", a=2), swapped,
                                    g.sin_k[:, ds(i, 1), :].rearrange("p o (a c) -> p (o a) c", a=2),
                                    ALU.mult).then_inc(kr_parts, 1)
                    if least >= 1:
                        v.wait_ge(lat_t_done, i)
                        v.wait_ge(key_copied, i)
                        v.wait_ge(g.vext_done, i)
                    v.wait_ge(kr_parts, 2 * i + 2)
                    v.tensor_tensor(kck[:, 0, :], krc[:], krs[:], ALU.add).then_inc(kr_done, 1)
                    v.wait_ge(rrms_done, i + 1)
                    v.tensor_scalar(qa[:], ps_a[:, 0:QL], rrms[:, 0:1], None, ALU.mult).then_inc(latents_done, 1)
                    v.tensor_scalar(kck[:, 1, :], ps_a[:, QL:QL + KL], rrms[:, 1:2], None,
                                    ALU.mult).then_inc(latents_done, 1)
            v.wait_ge(g.loaded_x, 16)
            v.wait_ge(g.loaded_const, 16 * g.N_CONST)
            staged(3, v, step)

        @block.gpsimd
        def _(pool):
            pool.wait_ge(g.neg_half_set, 1)
            pool.wait_ge(g.loaded_wa, 16)
            pool.tensor_copy(wa_h[:], g.wa[:]).then_inc(wa_split, 1)
            pool.wait_ge(wa_split, 1)
            pool.tensor_tensor(wa_l[:], g.wa[:], wa_h[:].bitcast(F32), ALU.subtract).then_inc(wa_split, 1)

            def step(i, one, two, three, least):
                if one:
                    ln.gpsimd_power(pool, i)
                if two:
                    t = i - 1
                    pool.wait_ge(rot_copied, t + 1)
                    if least >= 2:
                        pool.wait_ge(qr_done, t)
                    pool.tensor_tensor(rot_s.rearrange("p h (a c) -> p h a c", a=2),
                                       rot.rearrange("p h (a c) -> p h a c", a=2)[:, :, ::-1, :],
                                       g.sin_q[:, ds(t, 1), :].rearrange("p o (a c) -> p o a c", a=2).broadcast_to([P, H, 2, DR // 2]),
                                       ALU.mult).then_inc(rot_s_done, 1)
                    pool.wait_ge(lat_evac, 3 * t + 2)
                    pool.tensor_copy(g.qat0[:, ds(t * P, P)], qat0[:]).then_inc(qat_kept, 1)
                    pool.tensor_copy(g.qat1[:, ds(t * P, P)], qat1[:]).then_inc(qat_kept, 1)
                if one:
                    pool.wait_ge(meansq_done, 2 * i + 2)
                    if least >= 1:
                        pool.wait_ge(latents_done, 2 * i)
                    pool.tensor_tensor(rrms[:], meansq[:], g.neg_half[:, 0:2], ALU.pow).then_inc(rrms_done, 1)
                    pool.wait_ge(latents_done, 2 * i + 2)
                    pool.tensor_copy(g.vext[:, ds(i, 1), 0:KL].squeeze(1), kck[:, 1, :]).then_inc(g.vext_done, 1)
            pool.wait_ge(g.loaded_wr, 16 * 5)
            pool.tensor_scalar(g.wr0, g.wr0, g.qnw0[:, 0:1], None, ALU.mult).then_inc(wr_scaled, 1)
            pool.tensor_scalar(g.wr1, g.wr1, g.qnw1[:, 0:1], None, ALU.mult).then_inc(wr_scaled, 1)
            staged(3, pool, step)


class CausalAttention:

    UNITS = [(0, q) for q in range(NT)] + [(1, q) for q in reversed(range(NT))]
    NU = len(UNITS)

    def __init__(self, b, g, width):
        self.g, self.width = g, width
        self.p = b.sb("p", [P, 2, T])
        self.pt = b.sb("pt", [P, 2, NT, P])
        self.negmax = b.sb("negmax", [P, 2])
        self.ps_s = b.ps("ps_s", [P, 2, 2, 512])
        self.ps_t = b.ps("ps_t", [P, 2, 512])
        self.ps_u = b.ps("ps_u", [P, 2, 512])
        self.scores_done = b.sem("scores_done")
        self.max_done = b.sem("max_done")
        self.exp_done = b.sem("exp_done")
        self.trans_done = b.sem("trans_done")
        self.pt_by_scalar = b.sem("pt_by_scalar")
        self.pt_by_vector = b.sem("pt_by_vector")
        self.value_done = b.sem("value_done")
        self.u_read = b.sem("u_read")
        self.groups = [(u, k, min(k + 4, q + 1)) for u, (_, q) in enumerate(self.UNITS) for k in range(0, q + 1, 4)]
        self.NG = len(self.groups)
        assert self.NG % 2 == 0

    def of_unit(self, u):
        return [n for n, grp in enumerate(self.groups) if grp[0] == u]

    def scores(self, pe, pair, u, product, first):
        head, q = self.UNITS[u]
        if not (first and u < 2):
            pe.wait_ge(self.exp_done, self.NU * pair + u - 1)
        for n in range(0, q + 1, 4):
            m = min(n + 4, q + 1)
            out = self.ps_s[:, u % 2, n // 4, 0:(m - n) * P]
            product(pe, out, head, q, n, m, m <= q)
            if m == q + 1:
                mm = pe.matmul(out[:, (q - n) * P:(q - n + 1) * P], self.g.ident_b[:], self.g.causal[:],
                               start=False, stop=True)
        mm.then_inc(self.scores_done, 1)

    def transposes(self, pe, pair, u, first):
        pe.wait_ge(self.exp_done, self.NU * pair + u + 1)
        for n in self.of_unit(u):
            _, k0, k1 = self.groups[n]
            if not (first and n < 2):
                read = self.pt_by_scalar if n % 2 == 0 else self.pt_by_vector
                pe.wait_ge(read, self.NG // 2 * pair + n // 2)
            for k in range(k0, k1):
                mm = pe.transpose(self.ps_t[:, n % 2, (k - k0) * P:(k - k0 + 1) * P],
                                  self.p[:, u % 2, k * P:(k + 1) * P], self.g.ident[:])
            mm.then_inc(self.trans_done, 1)

    def values(self, pe, pair, u, value, first):
        _, q = self.UNITS[u]
        if not (first and u < 2):
            pe.wait_ge(self.u_read, self.NU * pair + u - 1)
        for n in self.of_unit(u):
            copied = self.pt_by_scalar if n % 2 == 0 else self.pt_by_vector
            pe.wait_ge(copied, self.NG // 2 * pair + n // 2 + 1)
            _, k0, k1 = self.groups[n]
            for k in range(k0, k1):
                mm = pe.matmul(self.ps_u[:, u % 2, 0:self.width], self.pt[:, u % 2, k, :],
                               value(self.UNITS[u][0], k), start=(k == 0), stop=(k == q))
        mm.then_inc(self.value_done, 1)

    def maximum(self, v, pair, u, first):
        q = self.UNITS[u][1]
        v.wait_ge(self.scores_done, self.NU * pair + u + 1)
        if not (first and u < 2):
            v.wait_ge(self.exp_done, self.NU * pair + u - 1)
        v.tensor_reduce(self.negmax[:, u % 2:u % 2 + 1],
                        self.ps_s[:, u % 2].rearrange("p a c -> p (a c)")[:, 0:(q + 1) * P], AX, ALU.max,
                        negate=True).then_inc(self.max_done, 1)

    def exponential(self, act, pair, u, first):
        q = self.UNITS[u][1]
        act.wait_ge(self.max_done, self.NU * pair + u + 1)
        if not (first and u < 2):
            n = self.of_unit(u - 2)[-1] if u >= 2 else self.of_unit(self.NU - 2 + u)[-1] - self.NG
            act.wait_ge(self.trans_done, self.NG * pair + n + 1)
        act.activation(self.p[:, u % 2, 0:(q + 1) * P],
                       self.ps_s[:, u % 2].rearrange("p a c -> p (a c)")[:, 0:(q + 1) * P], ACT.Exp,
                       bias=self.negmax[:, u % 2:u % 2 + 1]).then_inc(self.exp_done, 1)

    def copies(self, eng, pair, u, first, scalar):
        for n in self.of_unit(u):
            if (n % 2 == 0) != scalar:
                continue
            _, k0, k1 = self.groups[n]
            eng.wait_ge(self.trans_done, self.NG * pair + n + 1)
            if not (first and u < 2):
                eng.wait_ge(self.value_done, self.NU * pair + u - 1)
            src = self.ps_t[:, n % 2, 0:(k1 - k0) * P].rearrange("p (k c) -> p k c", c=P)
            if scalar:
                eng.activation(self.pt[:, u % 2, k0:k1, :], src, ACT.Copy).then_inc(self.pt_by_scalar, 1)
            else:
                eng.tensor_copy(self.pt[:, u % 2, k0:k1, :], src).then_inc(self.pt_by_vector, 1)

    def result(self, v, pair, u, out):
        v.wait_ge(self.value_done, self.NU * pair + u + 1)
        v.tensor_copy(out, self.ps_u[:, u % 2, 0:self.width]).then_inc(self.u_read, 1)

    def tensor_units(self, pe, pair, product, value, first):
        for s in range(self.NU + 2):
            if s < self.NU:
                self.scores(pe, pair, s, product, first)
            if s >= 2:
                self.values(pe, pair, s - 2, value, first)
            if 1 <= s <= self.NU:
                self.transposes(pe, pair, s - 1, first)

    def scalar_units(self, act, pair, first):
        for s in range(self.NU + 1):
            if s < self.NU:
                self.exponential(act, pair, s, first)
            if s >= 1:
                self.copies(act, pair, s - 1, first, True)

    def vector_units(self, v, pair, out, first):
        for s in range(self.NU + 2):
            if s < self.NU:
                self.maximum(v, pair, s, first)
            if 1 <= s <= self.NU:
                self.copies(v, pair, s - 1, first, False)
            if s >= 2:
                self.result(v, pair, s - 2, out(*self.UNITS[s - 2]))


def latent_heads(nc, g, dram):
    with ExitStack() as ctx:
        b = Bufs(nc, ctx, "a2")
        att = CausalAttention(b, g, KL + 1)
        wh = b.sb("wh", [P, 2, WH_N])
        wq0 = b.sb("wq0", [P, 2, KL])
        wq1 = b.sb("wq1", [QR1, 2, KL])
        q_h = b.sb("q_h", [P, 2, T], F32R)
        q_l = b.sb("q_l", [P, 2, T], F32R)
        waiter = b.sb("waiter", [1, 1])
        wh_loaded = b.sem("wh_loaded")
        wq_done = b.sem("wq_done")
        wq_evac = b.sem("wq_evac")
        wvo_done = b.sem("wvo_done")
        wvo_evac = b.sem("wvo_evac")
        qabs_done = b.sem("qabs_done")
        q_hi = b.sem("q_hi")
        q_lo = b.sem("q_lo")
        rope_hi = b.sem("rope_hi")
        rope_lo = b.sem("rope_lo")
        block = ctx.enter_context(nc.Block())

        @block.sync
        def _(sp):
            def load(p, first):
                if not first:
                    sp.wait_ge(wvo_done, p)
                sp.dma_start(wh[:], dram["wh"][ds(p, 1)].squeeze(0)).then_inc(wh_loaded, 16)
            load(0, True)
            sp.dma_start(g.w1_raw[:], dram["w1"]).then_inc(g.loaded_w1, 16)
            with sp.Fori(1, NP) as p:
                load(p, False)

        @block.tensor
        def _(pe):
            def product(pe, out, head, q, n, m, stop):
                cols, rows = slice(n * P, m * P), slice(q * P, (q + 1) * P)
                split3(pe, out, (q_h[:, head, rows], q_l[:, head, rows]),
                       (g.kt_h[:, head, cols], g.kt_l[:, head, cols]), True, stop)

            def pair(p, first):
                pe.wait_ge(wh_loaded, 16 * p + 16)
                if not first:
                    pe.wait_ge(att.u_read, att.NU * p)
                for head in range(2):
                    c = (1 - head) * KL
                    pe.matmul(att.ps_u[:, 0, c:c + KL], wh[:, head, 0:P], wh[:, head, QL:QL + KL],
                              start=True, stop=True)
                    mm = pe.matmul(att.ps_u[0:QR1, 0, P + c:P + c + KL], wh[:, head, P:QL], wh[:, head, QL:QL + KL],
                                   start=True, stop=True)
                mm.then_inc(wq_done, 1)
                for head in range(2):
                    mm = pe.matmul(att.ps_u[head * KL:(head + 1) * KL, 1, 0:D], wh[:, head, QL + KL:QL + 2 * KL],
                                   wh[:, head, QL + 2 * KL:WH_N], start=True, stop=True)
                mm.then_inc(wvo_done, 1)
                pe.wait_ge(wq_evac, 2 * p + 2)
                for n in range(2):
                    cols = slice(n * 512, (n + 1) * 512)
                    pe.matmul(att.ps_s[:, 0, n, :], wq0[:], g.qat0[:, cols], start=True, stop=False)
                    pe.matmul(att.ps_s[:, 0, n, :], wq1[:], g.qat1[:, cols], start=False,
                              stop=True).then_inc(qabs_done, 1)
                pe.wait_ge(q_hi, 4 * p + 4)
                pe.wait_ge(q_lo, 4 * p + 4)
                pe.wait_ge(rope_hi, 2 * p + 2)
                pe.wait_ge(rope_lo, 2 * p + 2)
                if first:
                    pe.wait_ge(g.loaded_const, 16 * g.N_CONST)
                pe.wait_ge(wvo_evac, p + 1)
                att.tensor_units(pe, p, product, lambda head, k: g.vext[:, k, :], first)
            pair(0, True)
            with pe.Fori(1, NP) as p:
                pair(p, False)

        @block.scalar
        def _(act):
            def pair(p, first):
                act.wait_ge(wq_done, p + 1)
                act.activation(wq0[:].rearrange("p a c -> p (a c)"), att.ps_u[:, 0, 0:P], ACT.Copy,
                               scale=g.qnw0[:, 0:1]).then_inc(wq_evac, 1)
                act.activation(wq1[:].rearrange("p a c -> p (a c)"), att.ps_u[0:QR1, 0, P:2 * P], ACT.Copy,
                               scale=g.qnw1[:, 0:1]).then_inc(wq_evac, 1)
                if not first:
                    act.wait_ge(att.value_done, att.NU * p)
                for n in range(2):
                    cols = slice(n * 512, (n + 1) * 512)
                    act.wait_ge(qabs_done, 2 * p + n + 1)
                    act.activation(q_h[KL:P, 0, cols], att.ps_s[KL:P, 0, n, :], ACT.Copy,
                                   scale=g.kvw_s[KL:P, 0:1]).then_inc(q_hi, 1)
                    act.activation(q_h[0:KL, 1, cols], att.ps_s[0:KL, 0, n, :], ACT.Copy,
                                   scale=g.kvw_s[0:KL, 0:1]).then_inc(q_hi, 1)
                att.scalar_units(act, p, first)
            act.wait_ge(g.kvw_scaled, 1)
            pair(0, True)
            with act.Fori(1, NP) as p:
                pair(p, False)

        @block.vector
        def _(v):
            def pair(p, first):
                v.wait_ge(wvo_done, p + 1)
                v.tensor_scalar(g.wvo[:, ds(p, 1), :].squeeze(1), att.ps_u[:, 1, 0:D], g.kvw[:, 0:1], None,
                                ALU.mult).then_inc(wvo_evac, 1)
                for n in range(2):
                    cols = slice(n * 512, (n + 1) * 512)
                    v.wait_ge(q_hi, 4 * p + 2 * n + 2)
                    v.scalar_tensor_tensor(q_l[KL:P, 0, cols], att.ps_s[KL:P, 0, n, :], g.kvw_s[KL:P, 0:1],
                                           q_h[KL:P, 0, cols].bitcast(F32), ALU.mult, ALU.subtract).then_inc(q_lo, 1)
                    v.scalar_tensor_tensor(q_l[0:KL, 1, cols], att.ps_s[0:KL, 0, n, :], g.kvw_s[0:KL, 0:1],
                                           q_h[0:KL, 1, cols].bitcast(F32), ALU.mult, ALU.subtract).then_inc(q_lo, 1)
                att.vector_units(v, p, lambda head, q: g.u[:, q, ds(2 * p + head, 1), :].squeeze(1), first)
            pair(0, True)
            with v.Fori(1, NP) as p:
                pair(p, False)

        @block.gpsimd
        def _(pool):
            def pair(p, first):
                if not first:
                    pool.wait_ge(att.value_done, att.NU * p)
                for head, rows in ((0, slice(0, DR)), (1, slice(DR, P))):
                    pool.tensor_copy(q_h[rows, head, :], g.qrt[rows, ds(p, 1), :].squeeze(1)).then_inc(rope_hi, 1)
                pool.wait_ge(rope_hi, 2 * p + 2)
                pool.tensor_tensor(waiter[:], g.neg_half[0:1, 0:1], g.neg_half[0:1, 0:1], ALU.add)
                for head, rows in ((0, slice(0, DR)), (1, slice(DR, P))):
                    pool.tensor_tensor(q_l[rows, head, :], g.qrt[rows, ds(p, 1), :].squeeze(1),
                                       q_h[rows, head, :].bitcast(F32), ALU.subtract).then_inc(rope_lo, 1)
            pair(0, True)
            with pool.Fori(1, NP) as p:
                pair(p, False)


def latent_output(nc, g):
    with ExitStack() as ctx:
        b = Bufs(nc, ctx, "a3")
        rden = b.sb("rden", [P, H])
        un = b.sb("un", [P, H * KL])
        ut = b.sb("ut", [P, NP, P])
        ps_t = b.ps("ps_t", [P, 2, 512])
        ps_y = b.ps("ps_y", [P, 512])
        rden_done = b.sem("rden_done")
        un_done = b.sem("un_done")
        un_t_done = b.sem("un_t_done")
        ut_by_scalar = b.sem("ut_by_scalar")
        ut_by_vector = b.sem("ut_by_vector")
        y_done = b.sem("y_done")
        y_added = b.sem("y_added")
        block = ctx.enter_context(nc.Block())

        @block.tensor
        def _(pe):
            def step(i, one, two, least):
                if one:
                    pe.wait_ge(un_done, i + 1)
                    if least >= 1:
                        pe.wait_ge(ut_by_scalar, i)
                        pe.wait_ge(ut_by_vector, i)
                    for c in range(NP):
                        mm = pe.transpose(ps_t[:, c // 4, (c % 4) * P:(c % 4 + 1) * P], un[:, c * P:(c + 1) * P],
                                          g.ident[:])
                    mm.then_inc(un_t_done, 1)
                    pe.wait_ge(ut_by_scalar, i + 1)
                    pe.wait_ge(ut_by_vector, i + 1)
                    if least >= 1:
                        pe.wait_ge(y_added, i)
                    for c in range(NP):
                        mm = pe.matmul(ps_y[:, 0:D], ut[:, c, :], g.wvo[:, c, :], start=(c == 0), stop=(c == NP - 1))
                    mm.then_inc(y_done, 1)
            staged(2, pe, step)

        @block.scalar
        def _(act):
            def step(i, one, two, least):
                if one:
                    act.wait_ge(un_t_done, i + 1)
                    if least >= 1:
                        act.wait_ge(y_done, i)
                    act.activation(ut[:, 0:4, :], ps_t[:, 0, :].rearrange("p (k c) -> p k c", c=P),
                                   ACT.Copy).then_inc(ut_by_scalar, 1)
            staged(2, act, step)

        @block.vector
        def _(v):
            def step(i, one, two, least):
                if one:
                    v.reciprocal(rden[:], g.u[:, ds(i, 1), :, KL].squeeze(1)).then_inc(rden_done, 1)
                    v.wait_ge(rden_done, i + 1)
                    if least >= 1:
                        v.wait_ge(un_t_done, i)
                    v.tensor_tensor(un[:].rearrange("p (h c) -> p h c", c=KL), g.u[:, ds(i, 1), :, 0:KL].squeeze(1),
                                    rden[:].unsqueeze(2).broadcast_to([P, H, KL]), ALU.mult).then_inc(un_done, 1)
                if two:
                    t = i - 1
                    v.wait_ge(y_done, t + 1)
                    v.tensor_tensor(g.X[:, ds(t * D, D)], g.X[:, ds(t * D, D)], ps_y[:, 0:D],
                                    ALU.add).then_inc(y_added, 1)
                if one:
                    v.wait_ge(un_t_done, i + 1)
                    v.tensor_copy(ut[:, 4:8, :], ps_t[:, 1, :].rearrange("p (k c) -> p k c", c=P))\
                        .then_inc(ut_by_vector, 1)
            staged(2, v, step)


def split_expert_weights(nc, g, dram):
    with ExitStack() as ctx:
        b = Bufs(nc, ctx, "ws")
        w1_hi = b.sem("w1_hi")
        w1_lo = b.sem("w1_lo")
        block = ctx.enter_context(nc.Block())
        N = 4
        CH = W1_N // N

        @block.sync
        def _(sp):
            sp.dma_start(g.w2[:, 0:NF - 1, :], dram["w2"][0:(NF - 1) * P, :]
                         .rearrange("(k p) d -> p k d", p=P)).then_inc(g.loaded_w2, 16)
            sp.dma_start(g.w2[0:FTAIL, NF - 1, :], dram["w2"][(NF - 1) * P:FH, :]).then_inc(g.loaded_w2, 16)

        @block.scalar
        def _(act):
            act.wait_ge(g.loaded_w1, 16)
            for n in range(N):
                act.activation(g.w1_h[:, :, n * CH:(n + 1) * CH], g.w1_raw[:, :, n * CH:(n + 1) * CH],
                               ACT.Copy).then_inc(w1_hi, 1)

        @block.vector
        def _(v):
            for n in range(N):
                cols = slice(n * CH, (n + 1) * CH)
                v.wait_ge(w1_hi, n + 1)
                v.tensor_tensor(g.w1_l[:, :, cols], g.w1_raw[:, :, cols], g.w1_h[:, :, cols].bitcast(F32),
                                ALU.subtract).then_inc(w1_lo, 1)


def experts(nc, g, tag):
    NBLK = NE + 1
    with ExitStack() as ctx:
        b = Bufs(nc, ctx, tag)
        ln = LayerNorm(b, g)
        xt_h = b.sb("xt_h", [P, KD * P], F32R)
        xt_l = b.sb("xt_l", [P, KD * P], F32R)
        silu = b.sb("silu", [P, 2, FI])
        hid = b.sb("hid", [P, FH])
        hid_t = b.sb("hid_t", [P, NF, P])
        logits = b.sb("logits", [P, NE])
        top = b.sb("top", [P, 8])
        top_at = b.sb("top_at", [P, 8], mybir.dt.uint32)
        top_atf = b.sb("top_atf", [P, 2])
        neg_top = b.sb("neg_top", [P, 1])
        expert_no = b.sb("expert_no", [P, NE])
        expo = b.sb("expo", [P, NE])
        expo_sum = b.sb("expo_sum", [P, 1])
        first_w = b.sb("first_w", [P, NE])
        second_w = b.sb("second_w", [P, NE])
        both_w = b.sb("both_w", [P, NE])
        pair_sum = b.sb("pair_sum", [P, 1])
        den = b.sb("den", [P, 1])
        rden = b.sb("rden", [P, 1])
        comb = b.sb("comb", [P, NE])
        ps_b = b.ps("ps_b", [P, 4, 512])
        ps_x = b.ps("ps_x", [P, 512])
        ps_h = b.ps("ps_h", [P, 2, 512])
        ps_y = b.ps("ps_y", [P, 512])
        numbered = b.sem("numbered")
        xt_hi = b.sem("xt_hi")
        xt_lo = b.sem("xt_lo")
        block_done = b.sem("block_done")
        silu_done = b.sem("silu_done")
        hid_done = b.sem("hid_done")
        hid_t_done = b.sem("hid_t_done")
        even_copied = b.sem("even_copied")
        odd_copied = b.sem("odd_copied")
        y_done = b.sem("y_done")
        y_added = b.sem("y_added")
        logits_done = b.sem("logits_done")
        router = b.sem("router")
        expo_done = b.sem("expo_done")
        den_done = b.sem("den_done")
        comb_done = b.sem("comb_done")
        ROUTER = 8
        block = ctx.enter_context(nc.Block())
        col = lambda k: 0 if k == 0 else BLK + NE + (k - 1) * BLK
        wid = lambda k: BLK + NE if k == 0 else BLK
        groups = [(0, 4), (4, 8), (8, 12), (12, NF)]

        def slot_before(k, slots):
            if k >= slots:
                return k - slots
            return max(j for j in range(NBLK) if j % slots == k % slots) - NBLK

        def tiles(eng, step):
            step(0, True, False)
            with eng.Fori(1, NT - 1) as t:
                step(t, False, False)
            step(NT - 1, False, True)

        @block.tensor
        def _(pe):
            def transposed_input(t, first):
                if not first:
                    pe.wait_ge(xt_hi, t)
                    pe.wait_ge(xt_lo, t)
                ln.tensor_transpose(pe, ps_x, t)

            def transposes(t, n, first):
                k0, k1 = groups[n]
                need = min(NBLK, -(-k1 * P // FI))
                if n < 3:
                    pe.wait_ge(hid_done, NBLK * t + need)
                if n == 2:
                    pe.wait_ge(even_copied, 2 * t + 1)
                    pe.wait_ge(odd_copied, 2 * t + 1)
                elif n < 2 and not first:
                    pe.wait_ge((even_copied, odd_copied)[n % 2], 2 * t)
                for k in range(k0, k1):
                    m = min(P, FH - k * P)
                    mm = pe.transpose(ps_h[0:m, n % 2, (k - k0) * P:(k - k0 + 1) * P], hid[:, k * P:k * P + m], g.ident[:])
                mm.then_inc(hid_t_done, 1)

            def outputs(t, k0, k1):
                for k in range(k0, k1):
                    m = min(P, FH - k * P)
                    mm = pe.matmul(ps_y[:, 0:D], hid_t[0:m, k, :], g.w2[0:m, k, :], start=(k == 0), stop=(k == NF - 1))
                return mm

            def step(t, first, last):
                pe.wait_ge(xt_hi, t + 1)
                pe.wait_ge(xt_lo, t + 1)
                for k in range(NBLK):
                    if not (first and k < 4):
                        pe.wait_ge(hid_done, NBLK * t + slot_before(k, 4) + 1)
                    for c in range(KD):
                        cs, ws = slice(c * P, (c + 1) * P), slice(col(k), col(k) + wid(k))
                        mm = split3(pe, ps_b[:, k % 4, 0:wid(k)], (xt_h[:, cs], xt_l[:, cs]),
                                    (g.w1_h[:, c, ws], g.w1_l[:, c, ws]), c == 0, c == KD - 1)
                    mm.then_inc(block_done, 1)
                    if k == 4:
                        transposes(t, 0, first)
                    if k == 7:
                        transposes(t, 1, first)
                if not last:
                    transposed_input(t + 1, False)
                if first:
                    pe.wait_ge(g.loaded_w2, 32)
                if not first:
                    pe.wait_ge(y_added, t)
                pe.wait_ge(even_copied, 2 * t + 1)
                outputs(t, 0, 4)
                transposes(t, 2, first)
                transposes(t, 3, first)
                pe.wait_ge(odd_copied, 2 * t + 1)
                outputs(t, 4, 8)
                pe.wait_ge(even_copied, 2 * t + 2)
                pe.wait_ge(odd_copied, 2 * t + 2)
                outputs(t, 8, NF).then_inc(y_done, 1)
            transposed_input(0, True)
            tiles(pe, step)

        @block.scalar
        def _(act):
            def transposed_high(t, first):
                act.wait_ge(ln.xn_read, t + 1)
                if not first:
                    act.wait_ge(block_done, NBLK * t)
                act.activation(xt_h[:], ps_x[:, 0:KD * P], ACT.Copy).then_inc(xt_hi, 1)

            def copy_group(t, n, first):
                k0, k1 = groups[n]
                act.wait_ge(hid_t_done, 4 * t + n + 1)
                if not first:
                    act.wait_ge(y_done, t)
                act.activation(hid_t[:, k0:k1, :], ps_h[:, 0, :].rearrange("p (k c) -> p k c", c=P),
                               ACT.Copy).then_inc(even_copied, 1)

            def step(t, first, last):
                for k in range(NBLK):
                    act.wait_ge(block_done, NBLK * t + k + 1)
                    if not (first and k < 2):
                        act.wait_ge(hid_done, NBLK * t + slot_before(k, 2) + 1)
                    act.activation(silu[:, k % 2, :], ps_b[:, k % 4, 0:FI], ACT.Silu).then_inc(silu_done, 1)
                    if k == 0:
                        act.wait_ge(router, ROUTER * t + 3)
                        if not first:
                            act.wait_ge(comb_done, t)
                        act.activation(expo[:], logits[:], ACT.Exp, bias=neg_top[:, 0:1],
                                       accum_out=expo_sum[:]).then_inc(expo_done, 1)
                    if k == 4:
                        copy_group(t, 0, first)
                if not last:
                    transposed_high(t + 1, False)
                copy_group(t, 2, first)
            transposed_high(0, True)
            tiles(act, step)

        @block.vector
        def _(v):
            def transposed_low(t, first):
                v.wait_ge(xt_hi, t + 1)
                v.tensor_tensor(xt_l[:], ps_x[:, 0:KD * P], xt_h[:].bitcast(F32), ALU.subtract).then_inc(xt_lo, 1)

            def gated(t, k, first):
                v.wait_ge(silu_done, NBLK * t + k + 1)
                if k == 0 and not first:
                    v.wait_ge(hid_t_done, 4 * t)
                out, up = hid[:, k * FI:(k + 1) * FI], ps_b[:, k % 4, FI:BLK]
                if k == 0:
                    v.tensor_tensor(out, up, silu[:, 0, :], ALU.mult).then_inc(hid_done, 1)
                else:
                    if k == 1:
                        v.wait_ge(comb_done, t + 1)
                    v.scalar_tensor_tensor(out, up, comb[:, k - 1:k], silu[:, k % 2, :], ALU.mult,
                                           ALU.mult).then_inc(hid_done, 1)

            def copy_group(t, n, first):
                k0, k1 = groups[n]
                m = min(P, FH - k0 * P)
                v.wait_ge(hid_t_done, 4 * t + n + 1)
                if not first:
                    v.wait_ge(y_done, t)
                v.tensor_copy(hid_t[0:m, k0:k1, :], ps_h[0:m, 1, 0:(k1 - k0) * P].rearrange("p (k c) -> p k c", c=P))\
                    .then_inc(odd_copied, 1)

            def route(t):
                def after(n):
                    v.wait_ge(router, ROUTER * t + n)
                v.wait_ge(logits_done, t + 1)
                v.memset(ln.waiter[:], 0.0)
                v.max(top[:], logits[:]).then_inc(router, 1)
                after(1)
                v.memset(ln.waiter[:], 0.0)
                v.max_index(top_at[:], top[:], logits[:]).then_inc(router, 1)
                v.tensor_scalar(neg_top[:], top[:, 0:1], -1.0, None, ALU.mult).then_inc(router, 1)
                after(2)
                v.tensor_copy(top_atf[:], top_at[:, 0:2]).then_inc(router, 1)
                after(4)
                v.wait_ge(expo_done, t + 1)
                v.scalar_tensor_tensor(first_w[:], expert_no[:], top_atf[:, 0:1], expo[:], ALU.is_equal,
                                       ALU.mult).then_inc(router, 1)
                v.scalar_tensor_tensor(second_w[:], expert_no[:], top_atf[:, 1:2], expo[:], ALU.is_equal,
                                       ALU.mult).then_inc(router, 1)
                after(6)
                v.tensor_tensor(both_w[:], first_w[:], second_w[:], ALU.add).then_inc(router, 1)
                after(7)
                v.tensor_reduce(pair_sum[:], both_w[:], AX, ALU.add).then_inc(router, 1)
                after(8)
                v.scalar_tensor_tensor(den[:], expo_sum[:], 1e-20, pair_sum[:], ALU.mult, ALU.add).then_inc(den_done, 1)
                v.wait_ge(den_done, 2 * t + 1)
                v.reciprocal(rden[:], den[:]).then_inc(den_done, 1)
                v.wait_ge(den_done, 2 * t + 2)
                v.tensor_scalar(comb[:], both_w[:], rden[:, 0:1], None, ALU.mult).then_inc(comb_done, 1)

            def step(t, first, last):
                v.wait_ge(block_done, NBLK * t + 1)
                v.wait_ge(silu_done, NBLK * t + 1)
                v.tensor_copy(logits[:], ps_b[:, 0, BLK:BLK + NE]).then_inc(logits_done, 1)
                gated(t, 0, first)
                route(t)
                for k in range(1, NBLK):
                    gated(t, k, first)
                    if not last and k == 2:
                        ln.vector_stats(v, t + 1, t + 1)
                    if not last and k == 4:
                        ln.vector_scale(v, t + 1, t + 1, False)
                    if k == 7:
                        copy_group(t, 1, first)
                if not last:
                    transposed_low(t + 1, False)
                copy_group(t, 3, first)
                v.wait_ge(y_done, t + 1)
                v.tensor_tensor(g.X[:, ds(t * D, D)], g.X[:, ds(t * D, D)], ps_y[:, 0:D], ALU.add).then_inc(y_added, 1)
            v.wait_ge(numbered, 1)
            ln.vector_stats(v, 0, 0)
            ln.vector_scale(v, 0, 0, True)
            transposed_low(0, True)
            tiles(v, step)

        @block.gpsimd
        def _(pool):
            pool.iota(expert_no[:], pattern=[[1, NE]], base=0, channel_multiplier=0,
                      allow_small_or_imprecise_dtypes=True).then_inc(numbered, 1)
            ln.gpsimd_power(pool, 0)
            with pool.Fori(1, NT) as t:
                ln.gpsimd_power(pool, t)


def plain_attention(nc, g, dram):
    with ExitStack() as ctx:
        b = Bufs(nc, ctx, "b")
        xt_h = b.sb("xt_h", [P, KD, T], F32R)
        xt_l = b.sb("xt_l", [P, KD, T], F32R)
        wqk_h = b.sb("wqk_h", [P, KD, D], F32R)
        wqk_l = b.sb("wqk_l", [P, KD, D], F32R)
        wvo_h = b.sb("wvo_h", [P, KD, D], F32R)
        wvo_l = b.sb("wvo_l", [P, KD, D], F32R)
        vo = b.sb("vo", [P, NT, D])
        keys_and_values(nc, g, dram, xt_h, xt_l, wqk_h, wqk_l, wvo_h, wvo_l, vo)
        plain_queries(nc, g, xt_h, xt_l, wqk_h, wqk_l, vo)


def keys_and_values(nc, g, dram, xt_h, xt_l, wqk_h, wqk_l, wvo_h, wvo_l, vo):
    with ExitStack() as ctx:
        b = Bufs(nc, ctx, "bk")
        ln = LayerNorm(b, g)
        w = b.sb("w", [P, 4, KD, D])
        xs_h = b.sb("xs_h", [P, KD, P], F32R)
        xs_l = b.sb("xs_l", [P, KD, P], F32R)
        ps_w = b.ps("ps_w", [P, 2, 512])
        ps_x = b.ps("ps_x", [P, 512])
        ps_v = b.ps("ps_v", [P, 512])
        w_loaded = b.sem("w_loaded")
        w_done = b.sem("w_done")
        w_hi = b.sem("w_hi")
        w_lo = b.sem("w_lo")
        xt_hi = b.sem("xt_hi")
        xt_lo = b.sem("xt_lo")
        xt_kept = b.sem("xt_kept")
        vo_done = b.sem("vo_done")
        vo_copied = b.sem("vo_copied")
        block = ctx.enter_context(nc.Block())

        @block.sync
        def _(sp):
            sp.dma_start(w[:], dram["wb"]).then_inc(w_loaded, 16)

        @block.tensor
        def _(pe):
            pe.wait_ge(w_loaded, 16)
            for n, (left, right) in enumerate(((0, 1), (2, 3))):
                for m in range(KD):
                    for c in range(KD):
                        mm = pe.matmul(ps_w[:, n, m * D:(m + 1) * D], w[:, left, c, m * P:(m + 1) * P],
                                       w[:, right, c, :], start=(c == 0), stop=(c == KD - 1))
                mm.then_inc(w_done, 1)

            def step(t, one, least):
                if least >= 1:
                    pe.wait_ge(xt_lo, t)
                ln.tensor_transpose(pe, ps_x, t)
                pe.wait_ge(xt_hi, t + 1)
                pe.wait_ge(xt_lo, t + 1)
                if least == 0:
                    pe.wait_ge(w_lo, 2)
                else:
                    pe.wait_ge(vo_copied, t)
                for c in range(KD):
                    mm = split3(pe, ps_v[:, 0:D], (xs_h[:, c, :], xs_l[:, c, :]), (wvo_h[:, c, :], wvo_l[:, c, :]),
                                c == 0, c == KD - 1)
                mm.then_inc(vo_done, 1)
            staged(1, pe, step)

        @block.scalar
        def _(act):
            for n, (hi, scale) in enumerate(((wqk_h, D ** -0.5), (wvo_h, 1.0))):
                act.wait_ge(w_done, n + 1)
                act.activation(hi[:], ps_w[:, n, :].rearrange("p (m c) -> p m c", m=KD), ACT.Copy,
                               scale=scale).then_inc(w_hi, 1)

            def step(t, one, least):
                act.wait_ge(ln.xn_read, t + 1)
                if least >= 1:
                    act.wait_ge(vo_done, t)
                    act.wait_ge(xt_kept, 2 * t)
                act.activation(xs_h[:], ps_x[:, 0:KD * P].rearrange("p (m c) -> p m c", m=KD),
                               ACT.Copy).then_inc(xt_hi, 1)
                act.wait_ge(vo_done, t + 1)
                act.activation(vo[:, ds(t, 1), :].squeeze(1), ps_v[:, 0:D], ACT.Copy).then_inc(vo_copied, 1)
            staged(1, act, step)

        @block.vector
        def _(v):
            ln.vector_stats(v, 0, 0)
            ln.vector_scale(v, 0, 0, True)
            for n, (hi, lo, scale) in enumerate(((wqk_h, wqk_l, D ** -0.5), (wvo_h, wvo_l, 1.0))):
                v.wait_ge(w_hi, n + 1)
                v.scalar_tensor_tensor(lo[:], ps_w[:, n, :].rearrange("p (m c) -> p m c", m=KD), scale,
                                       hi[:].bitcast(F32), ALU.mult, ALU.subtract).then_inc(w_lo, 1)

            def low(t):
                v.wait_ge(xt_hi, t + 1)
                v.tensor_tensor(xs_l[:], ps_x[:, 0:KD * P].rearrange("p (m c) -> p m c", m=KD),
                                xs_h[:].bitcast(F32), ALU.subtract).then_inc(xt_lo, 1)

            def step(t):
                ln.vector_stats(v, t + 1, t + 1)
                low(t)
                ln.vector_scale(v, t + 1, t + 1, False)
            step(0)
            with v.Fori(1, NT - 1) as t:
                step(t)
            low(NT - 1)

        @block.gpsimd
        def _(pool):
            def step(t, one, least):
                if least == 0:
                    ln.gpsimd_power(pool, 0)
                    ln.gpsimd_power(pool, 1)
                pool.wait_ge(xt_lo, t + 1)
                pool.tensor_copy(xt_h[:, :, ds(t * P, P)], xs_h[:]).then_inc(xt_kept, 1)
                pool.tensor_copy(xt_l[:, :, ds(t * P, P)], xs_l[:]).then_inc(xt_kept, 1)
            step(0, True, 0)
            with pool.Fori(1, NT - 1) as t:
                ln.gpsimd_power(pool, t + 1)
                step(t, True, 1)
            step(NT - 1, True, 1)


def plain_queries(nc, g, xt_h, xt_l, wqk_h, wqk_l, vo):
    with ExitStack() as ctx:
        b = Bufs(nc, ctx, "bq")
        qt_h = b.sb("qt_h", [P, KD, P], F32R)
        qt_l = b.sb("qt_l", [P, KD, P], F32R)
        negmax = b.sb("negmax", [P, 1])
        wsum = b.sb("wsum", [P, 1])
        rsum = b.sb("rsum", [P, 1])
        p = b.sb("p", [P, T])
        pt = b.sb("pt", [P, NT, P])
        ps_q = b.ps("ps_q", [P, 512])
        ps_s = b.ps("ps_s", [P, 2, 512])
        ps_t = b.ps("ps_t", [P, 2, 512])
        ps_y = b.ps("ps_y", [P, 512])
        q_done = b.sem("q_done")
        q_hi = b.sem("q_hi")
        q_lo = b.sem("q_lo")
        scores_done = b.sem("scores_done")
        max_done = b.sem("max_done")
        exp_done = b.sem("exp_done")
        rsum_done = b.sem("rsum_done")
        p_t_done = b.sem("p_t_done")
        pt_by_scalar = b.sem("pt_by_scalar")
        pt_by_vector = b.sem("pt_by_vector")
        y_done = b.sem("y_done")
        y_added = b.sem("y_added")
        block = ctx.enter_context(nc.Block())

        @block.tensor
        def _(pe):
            def step(i, one, two, least):
                if one:
                    if least >= 1:
                        pe.wait_ge(q_lo, i)
                    for m in range(KD):
                        for c in range(KD):
                            tokens = ds(i * P, P)
                            mm = split3(pe, ps_q[:, m * P:(m + 1) * P],
                                        (wqk_h[:, c, m * P:(m + 1) * P], wqk_l[:, c, m * P:(m + 1) * P]),
                                        (xt_h[:, c, tokens], xt_l[:, c, tokens]), c == 0, c == KD - 1)
                    mm.then_inc(q_done, 1)
                if two:
                    t = i - 1
                    pe.wait_ge(exp_done, t + 1)
                    if least >= 2:
                        pe.wait_ge(pt_by_scalar, t)
                        pe.wait_ge(pt_by_vector, t)
                    for k in range(NT):
                        mm = pe.transpose(ps_t[:, k // 4, (k % 4) * P:(k % 4 + 1) * P], p[:, k * P:(k + 1) * P],
                                          g.ident[:])
                    mm.then_inc(p_t_done, 1)
                if one:
                    pe.wait_ge(q_hi, i + 1)
                    pe.wait_ge(q_lo, i + 1)
                    for n in range(2):
                        cols = slice(n * 512, (n + 1) * 512)
                        for c in range(KD):
                            mm = split3(pe, ps_s[:, n, :], (qt_h[:, c, :], qt_l[:, c, :]),
                                        (xt_h[:, c, cols], xt_l[:, c, cols]), c == 0, c == KD - 1)
                    mm.then_inc(scores_done, 1)
                if two:
                    t = i - 1
                    pe.wait_ge(pt_by_scalar, t + 1)
                    pe.wait_ge(pt_by_vector, t + 1)
                    if least >= 2:
                        pe.wait_ge(y_added, t)
                    for k in range(NT):
                        mm = pe.matmul(ps_y[:, 0:D], pt[:, k, :], vo[:, k, :], start=(k == 0), stop=(k == NT - 1))
                    mm.then_inc(y_done, 1)
            staged(2, pe, step)

        @block.scalar
        def _(act):
            def step(i, one, two, least):
                if one:
                    act.wait_ge(q_done, i + 1)
                    if least >= 1:
                        act.wait_ge(scores_done, i)
                    act.activation(qt_h[:], ps_q[:, 0:KD * P].rearrange("p (m c) -> p m c", m=KD),
                                   ACT.Copy).then_inc(q_hi, 1)
                if two:
                    t = i - 1
                    act.wait_ge(p_t_done, t + 1)
                    if least >= 2:
                        act.wait_ge(y_done, t)
                    act.activation(pt[:, 0:4, :], ps_t[:, 0, :].rearrange("p (k c) -> p k c", c=P),
                                   ACT.Copy).then_inc(pt_by_scalar, 1)
                if one:
                    act.wait_ge(max_done, i + 1)
                    if least >= 1:
                        act.wait_ge(rsum_done, i)
                    act.activation(p[:], ps_s[:].rearrange("p a c -> p (a c)"), ACT.Exp, bias=negmax[:, 0:1],
                                   accum_out=wsum[:]).then_inc(exp_done, 1)
            staged(2, act, step)

        @block.vector
        def _(v):
            def step(i, one, two, least):
                if one:
                    v.wait_ge(q_hi, i + 1)
                    v.tensor_tensor(qt_l[:], ps_q[:, 0:KD * P].rearrange("p (m c) -> p m c", m=KD),
                                    qt_h[:].bitcast(F32), ALU.subtract).then_inc(q_lo, 1)
                if two:
                    t = i - 1
                    v.wait_ge(p_t_done, t + 1)
                    if least >= 2:
                        v.wait_ge(y_done, t)
                    v.tensor_copy(pt[:, 4:8, :], ps_t[:, 1, :].rearrange("p (k c) -> p k c", c=P))\
                        .then_inc(pt_by_vector, 1)
                if one:
                    v.wait_ge(scores_done, i + 1)
                    v.tensor_reduce(negmax[:], ps_s[:].rearrange("p a c -> p (a c)"), AX, ALU.max,
                                    negate=True).then_inc(max_done, 1)
                if two:
                    t = i - 1
                    v.wait_ge(y_done, t + 1)
                    v.scalar_tensor_tensor(g.X[:, ds(t * D, D)], ps_y[:, 0:D], rsum[:, 0:1], g.X[:, ds(t * D, D)],
                                           ALU.mult, ALU.add).then_inc(y_added, 1)
                if one:
                    v.wait_ge(exp_done, i + 1)
                    if least >= 1:
                        v.wait_ge(y_added, i)
                    v.reciprocal(rsum[:], wsum[:]).then_inc(rsum_done, 1)
            staged(2, v, step)


def experts_and_middle(nc, g, dram):
    with ExitStack() as ctx:
        b = Bufs(nc, ctx, "m")
        g.w1_h = b.sb("w1_h", [P, KD, W1_N], F32R)
        g.w1_l = b.sb("w1_l", [P, KD, W1_N], F32R)
        g.w2 = b.sb("w2", [P, NF, D])
        split_expert_weights(nc, g, dram)
        experts(nc, g, "m1")
        plain_attention(nc, g, dram)
        experts(nc, g, "m2")


def heads_projections(nc, g, dram):
    with ExitStack() as ctx:
        b = Bufs(nc, ctx, "c1")
        ln = LayerNorm(b, g)
        w = b.sb("w", [P, KD, 3 * D])
        w_h = b.sb("w_h", [P, KD, 3 * D], F32R)
        w_l = b.sb("w_l", [P, KD, 3 * D], F32R)
        xt_h = b.sb("xt_h", [P, KD * P], F32R)
        xt_l = b.sb("xt_l", [P, KD * P], F32R)
        st = b.sb("st", [P, 2, H, 4, HD], F32R)
        waiter = b.sb("waiter", [1, 1])
        ps_x = b.ps("ps_x", [P, 512])
        ps_qk = b.ps("ps_qk", [P, 512])
        ps_v = b.ps("ps_v", [P, 512])
        ps_t = b.ps("ps_t", [P, 4, 512])
        w_loaded = b.sem("w_loaded")
        w_hi = b.sem("w_hi")
        w_lo = b.sem("w_lo")
        xt_hi = b.sem("xt_hi")
        xt_lo = b.sem("xt_lo")
        qk_done = b.sem("qk_done")
        v_done = b.sem("v_done")
        st_hi = b.sem("st_hi")
        st_lo = b.sem("st_lo")
        v_kept = b.sem("v_kept")
        st_copied = b.sem("st_copied")
        st_t_done = b.sem("st_t_done")
        by_scalar = b.sem("by_scalar")
        by_vector = b.sem("by_vector")
        block = ctx.enter_context(nc.Block())
        qk = ps_qk[:].rearrange("p (a h c) -> p a h c", a=2, c=HD)
        HIGH = ((0, 0), (1, 0))
        HIGH2 = ((0, 1), (1, 2))
        LOW = ((0, 2), (1, 1))
        LOW2 = ((0, 3), (1, 3))
        SCALE = (HD ** -0.5, 1.0)

        @block.sync
        def _(sp):
            sp.dma_start(w[:], dram["wqkv"]).then_inc(w_loaded, 16)

        @block.tensor
        def _(pe):
            def step(i, one, two, least):
                if one:
                    if least >= 1:
                        pe.wait_ge(xt_lo, i)
                    ln.tensor_transpose(pe, ps_x, i)
                if two:
                    t = i - 1
                    pe.wait_ge(st_lo, 2 * t + 2)
                    pe.wait_ge(st_copied, 2 * t + 2)
                    if least >= 2:
                        pe.wait_ge(by_scalar, 2 * t)
                        pe.wait_ge(by_vector, 2 * t)
                    flat = st[:].rearrange("p a h s c -> p (a h s c)").bitcast(F32)
                    for c in range(2 * NP):
                        mm = pe.transpose(ps_t[:, c // 4, (c % 4) * P:(c % 4 + 1) * P], flat[:, c * P:(c + 1) * P],
                                          g.ident[:])
                    mm.then_inc(st_t_done, 1)
                if one:
                    pe.wait_ge(xt_hi, i + 1)
                    pe.wait_ge(xt_lo, i + 1)
                    if least == 0:
                        pe.wait_ge(w_lo, 1)
                    else:
                        pe.wait_ge(st_lo, 2 * i)
                        pe.wait_ge(v_kept, i)
                    for out, cols, sem in ((ps_qk[:], slice(0, 2 * D), qk_done), (ps_v[:, 0:D], slice(2 * D, 3 * D), v_done)):
                        for c in range(KD):
                            cs = slice(c * P, (c + 1) * P)
                            mm = split3(pe, out, (xt_h[:, cs], xt_l[:, cs]), (w_h[:, c, cols], w_l[:, c, cols]),
                                        c == 0, c == KD - 1)
                        mm.then_inc(sem, 1)
            staged(2, pe, step)

        @block.scalar
        def _(act):
            act.wait_ge(w_loaded, 16)
            act.activation(w_h[:], w[:], ACT.Copy).then_inc(w_hi, 1)

            def step(i, one, two, least):
                if one:
                    act.wait_ge(ln.xn_read, i + 1)
                    if least >= 1:
                        act.wait_ge(v_done, i)
                    act.activation(xt_h[:], ps_x[:, 0:KD * P], ACT.Copy).then_inc(xt_hi, 1)
                if two:
                    t = i - 1
                    act.wait_ge(st_t_done, t + 1)
                    for n in range(2):
                        act.activation(g.qks[:, 4 * n:4 * n + 4, ds(t * P, P)],
                                       ps_t[:, n, :].rearrange("p (k c) -> p k c", c=P), ACT.Copy).then_inc(by_scalar, 1)
                if one:
                    act.wait_ge(qk_done, i + 1)
                    if least >= 1:
                        act.wait_ge(st_t_done, i)
                    for n, (a, s) in enumerate(HIGH):
                        act.activation(st[:, a, :, s, :], qk[:, a], ACT.Copy, scale=SCALE[a]).then_inc(st_hi, 1)
                    act.wait_ge(v_done, i + 1)
                    act.activation(g.vh[:, ds(i, 1), :, 0:HD].squeeze(1), ps_v[:, 0:D].rearrange("p (h c) -> p h c", c=HD),
                                   ACT.Copy).then_inc(v_kept, 1)
            staged(2, act, step)

        @block.vector
        def _(v):
            ln.vector_stats(v, 0, 0)
            ln.vector_scale(v, 0, 0, True)
            v.wait_ge(w_hi, 1)
            v.tensor_tensor(w_l[:], w[:], w_h[:].bitcast(F32), ALU.subtract).then_inc(w_lo, 1)

            def low(i):
                v.wait_ge(xt_hi, i + 1)
                v.tensor_tensor(xt_l[:], ps_x[:, 0:KD * P], xt_h[:].bitcast(F32), ALU.subtract).then_inc(xt_lo, 1)

            def copies(t):
                v.wait_ge(st_t_done, t + 1)
                for n in range(2, 4):
                    v.tensor_copy(g.qks[:, 4 * n:4 * n + 4, ds(t * P, P)],
                                  ps_t[:, n, :].rearrange("p (k c) -> p k c", c=P)).then_inc(by_vector, 1)

            def stack_low(i):
                v.wait_ge(st_hi, 2 * i + 2)
                for (a, s), (_, s_hi) in zip(LOW, HIGH):
                    v.scalar_tensor_tensor(st[:, a, :, s, :], qk[:, a], SCALE[a], st[:, a, :, s_hi, :].bitcast(F32),
                                           ALU.mult, ALU.subtract).then_inc(st_lo, 1)

            def step(i, one, two, least):
                if one:
                    low(i)
                    if least < NT - 1:
                        ln.vector_stats(v, i + 1, i + 1)
                if two:
                    copies(i - 1)
                if one:
                    if least < NT - 1:
                        ln.vector_scale(v, i + 1, i + 1, False)
                    stack_low(i)
            step(0, True, False, 0)
            with v.Fori(1, NT - 1) as i:
                step(i, True, True, 1)
            step(NT - 1, True, True, NT - 1)
            step(NT, False, True, NT)

        @block.gpsimd
        def _(pool):
            pool.memset(g.vh[:, :, :, HD:HD + 1], 1.0).then_inc(g.ones_set, 1)
            pool.wait_ge(g.ones_set, 2)

            def step(i, norm_next):
                if norm_next:
                    ln.gpsimd_power(pool, i + 1)
                pool.wait_ge(st_lo, 2 * i + 2)
                pool.tensor_tensor(waiter[:], g.neg_half[0:1, 0:1], g.neg_half[0:1, 0:1], ALU.add)
                for high, high2, low, low2 in zip(HIGH, HIGH2, LOW, LOW2):
                    a = high[0]
                    pool.tensor_copy(st[:, a, :, high2[1], :], st[:, a, :, high[1], :])
                    pool.tensor_copy(st[:, a, :, low2[1], :], st[:, a, :, low[1], :]).then_inc(st_copied, 1)
            ln.gpsimd_power(pool, 0)
            step(0, True)
            with pool.Fori(1, NT - 1) as i:
                step(i, True)
            step(NT - 1, False)


def head_pairs(nc, g):
    with ExitStack() as ctx:
        b = Bufs(nc, ctx, "c2")
        att = CausalAttention(b, g, HD + 1)
        q_s = [b.sb(f"q_s{s}", [P, T], F32R) for s in range(2)]
        k_s = [b.sb(f"k_s{s}", [P, T], F32R) for s in range(2)]
        slot_loaded = [b.sem(f"slot{s}_loaded") for s in range(2)]
        block = ctx.enter_context(nc.Block())

        @block.sync
        def _(sp):
            def load(j, s, first):
                pair = 2 * j + s
                if not first:
                    sp.wait_ge(att.value_done, att.NU * (pair - 1))
                sp.dma_start(q_s[s][:].bitcast(F32), g.qks[:, ds(pair, 1), :].squeeze(1).bitcast(F32)).then_inc(slot_loaded[s], 16)
                sp.dma_start(k_s[s][:].bitcast(F32), g.qks[:, ds(pair + NP, 1), :].squeeze(1).bitcast(F32)).then_inc(slot_loaded[s], 16)
            for s in range(2):
                load(0, s, True)
            with sp.Fori(1, NP // 2) as j:
                for s in range(2):
                    load(j, s, False)

        @block.tensor
        def _(pe):
            def pair(j, s, first):
                n = 2 * j + s

                def product(pe, out, head, q, k0, k1, stop):
                    rows = slice(head * 64, head * 64 + 64)
                    pe.matmul(out, q_s[s][rows, q * P:(q + 1) * P], k_s[s][rows, k0 * P:k1 * P], start=True, stop=stop)
                pe.wait_ge(slot_loaded[s], 32 * j + 32)
                att.tensor_units(pe, n, product, lambda head, k: g.vh[:, k, ds(2 * n + head, 1), :].squeeze(1), first)
            for s in range(2):
                pair(0, s, s == 0)
            with pe.Fori(1, NP // 2) as j:
                for s in range(2):
                    pair(j, s, False)

        @block.scalar
        def _(act):
            for s in range(2):
                att.scalar_units(act, s, s == 0)
            with act.Fori(1, NP // 2) as j:
                for s in range(2):
                    att.scalar_units(act, 2 * j + s, False)

        @block.vector
        def _(v):
            def pair(n, first):
                att.vector_units(v, n, lambda head, q: g.o[:, q, ds(2 * n + head, 1), :].squeeze(1), first)
            for s in range(2):
                pair(s, s == 0)
            with v.Fori(1, NP // 2) as j:
                for s in range(2):
                    pair(2 * j + s, False)


def heads_output(nc, g, dram):
    with ExitStack() as ctx:
        b = Bufs(nc, ctx, "c3")
        w = b.sb("w", [P, KD, D])
        rden = b.sb("rden", [P, H])
        on = b.sb("on", [P, D])
        ot = b.sb("ot", [P, KD, P])
        ps_t = b.ps("ps_t", [P, 512])
        ps_y = b.ps("ps_y", [P, 512])
        w_loaded = b.sem("w_loaded")
        rden_done = b.sem("rden_done")
        on_done = b.sem("on_done")
        on_t_done = b.sem("on_t_done")
        ot_copied = b.sem("ot_copied")
        y_done = b.sem("y_done")
        y_added = b.sem("y_added")
        block = ctx.enter_context(nc.Block())

        @block.sync
        def _(sp):
            sp.dma_start(w[:], dram["wout"]).then_inc(w_loaded, 16)

        @block.tensor
        def _(pe):
            pe.wait_ge(w_loaded, 16)

            def step(i, one, least):
                pe.wait_ge(on_done, i + 1)
                if least >= 1:
                    pe.wait_ge(ot_copied, i)
                for c in range(KD):
                    mm = pe.transpose(ps_t[:, c * P:(c + 1) * P], on[:, c * P:(c + 1) * P], g.ident[:])
                mm.then_inc(on_t_done, 1)
                pe.wait_ge(ot_copied, i + 1)
                if least >= 1:
                    pe.wait_ge(y_added, i)
                for c in range(KD):
                    mm = pe.matmul(ps_y[:, 0:D], ot[:, c, :], w[:, c, :], start=(c == 0), stop=(c == KD - 1))
                mm.then_inc(y_done, 1)
            staged(1, pe, step)

        @block.scalar
        def _(act):
            def step(i, one, least):
                act.wait_ge(on_t_done, i + 1)
                if least >= 1:
                    act.wait_ge(y_done, i)
                act.activation(ot[:], ps_t[:, 0:D].rearrange("p (k c) -> p k c", c=P), ACT.Copy).then_inc(ot_copied, 1)
            staged(1, act, step)

        @block.vector
        def _(v):
            def step(i, one, two, least):
                if one:
                    if least >= 1:
                        v.wait_ge(on_t_done, i)
                    v.reciprocal(rden[:], g.o[:, ds(i, 1), :, HD].squeeze(1)).then_inc(rden_done, 1)
                    v.wait_ge(rden_done, i + 1)
                    v.tensor_tensor(on[:].rearrange("p (h c) -> p h c", c=HD), g.o[:, ds(i, 1), :, 0:HD].squeeze(1),
                                    rden[:].unsqueeze(2).broadcast_to([P, H, HD]), ALU.mult).then_inc(on_done, 1)
                if two:
                    t = i - 1
                    v.wait_ge(y_done, t + 1)
                    v.tensor_tensor(g.X[:, ds(t * D, D)], g.X[:, ds(t * D, D)], ps_y[:, 0:D],
                                    ALU.add).then_inc(y_added, 1)
            staged(2, v, step)


def many_head_attention(nc, g, dram):
    with ExitStack() as ctx:
        b = Bufs(nc, ctx, "c")
        g.o = b.sb("o", [P, NT, H, HD + 1])
        with ExitStack() as hctx:
            h = Bufs(nc, hctx, "ch")
            g.qks = h.sb("qks", [P, 2 * NP, T], F32R)
            g.vh = h.sb("vh", [P, NT, H, HD + 1])
            heads_projections(nc, g, dram)
            head_pairs(nc, g)
        heads_output(nc, g, dram)


HALF = T // 2
HT = NT // 2


def prepare_ffn(nc, g, dram):
    with ExitStack() as ctx:
        b = Bufs(nc, ctx, "fp")
        raw = b.sb("raw", [P, 2, KD, FF])
        w2 = b.sb("w2", [P, NFF, D])
        had = b.sb("had", [P, P])
        fly = b.sb("fly", [P, 2, NFF, D])
        ps = b.ps("ps", [P, NFF, D])
        raw_loaded = b.sem("raw_loaded")
        w2_loaded = b.sem("w2_loaded")
        had_done = b.sem("had_done")
        fly_start = b.sem("fly_start")
        fly_done = b.sem("fly_done")
        w_hi = b.sem("w_hi")
        w_lo = b.sem("w_lo")
        block = ctx.enter_context(nc.Block())

        @block.sync
        def _(sp):
            sp.dma_start(had[:], dram["had"]).then_inc(w2_loaded, 16)
            sp.dma_start(w2[:], dram["w2f"]).then_inc(w2_loaded, 16)
            sp.dma_start(raw[:], dram["w13"]).then_inc(raw_loaded, 16)

        @block.tensor
        def _(pe):
            pe.wait_ge(w2_loaded, 32)
            for k in range(0, NFF, 2):
                for j in range(k, k + 2):
                    mm = pe.matmul(ps[:, j, :], had[:], w2[:, j, :], start=True, stop=True)
                mm.then_inc(had_done, 1)

        @block.scalar
        def _(act):
            for k in range(0, NFF, 2):
                act.wait_ge(had_done, k // 2 + 1)
                act.activation(fly[:, 0, k:k + 2, :], ps[:, k:k + 2, :], ACT.Copy, scale=FF ** -0.5).then_inc(fly_start, 1)
            act.wait_ge(raw_loaded, 16)
            for n in range(2):
                act.activation(g.w13_h[:, n], raw[:, n], ACT.Copy).then_inc(w_hi, 1)

        @block.vector
        def _(v):
            v.wait_ge(fly_start, NFF // 2)
            done = 0
            for stage in range(3):
                src = fly[:, stage % 2].rearrange("p (a two j) d -> p a two j d", two=2, j=1 << stage)
                dst = (g.w2f[:] if stage == 2 else fly[:, 1 - stage % 2])\
                    .rearrange("p (a two j) d -> p a two j d", two=2, j=1 << stage)
                if stage:
                    v.wait_ge(fly_done, done)
                for a in range(src.shape[1]):
                    v.tensor_tensor(dst[:, a, 0], src[:, a, 0], src[:, a, 1], ALU.add).then_inc(fly_done, 1)
                    v.tensor_tensor(dst[:, a, 1], src[:, a, 0], src[:, a, 1], ALU.subtract).then_inc(fly_done, 1)
                    done += 2
            for n in range(2):
                v.wait_ge(w_hi, n + 1)
                v.tensor_tensor(g.w13_l[:, n], raw[:, n], g.w13_h[:, n].bitcast(F32), ALU.subtract).then_inc(w_lo, 1)


def feed_forward(nc, g, tag):
    with ExitStack() as ctx:
        b = Bufs(nc, ctx, tag)
        ln = LayerNorm(b, g)
        xt_h = b.sb("xt_h", [P, 2, KD, HALF], F32R)
        xt_l = b.sb("xt_l", [P, 2, KD, HALF], F32R)
        silu = b.sb("silu", [P, 2, HALF])
        hid = b.sb("hid", [P, NFF, HALF])
        ps_x = b.ps("ps_x", [P, 512])
        ps_g = b.ps("ps_g", [P, 2, 512])
        ps_u = b.ps("ps_u", [P, 2, 512])
        ps_y = b.ps("ps_y", [P, 2, 512])
        xt_hi = b.sem("xt_hi")
        xt_lo = b.sem("xt_lo")
        gate_done = b.sem("gate_done")
        up_done = b.sem("up_done")
        silu_done = b.sem("silu_done")
        hid_done = b.sem("hid_done")
        y_done = b.sem("y_done")
        y_added = b.sem("y_added")
        block = ctx.enter_context(nc.Block())

        @block.tensor
        def _(pe):
            def input_tile(t):
                if t:
                    pe.wait_ge(xt_lo, t)
                ln.tensor_transpose(pe, ps_x, t)

            def features(s):
                half, f = divmod(s, NFF)
                fs = slice(f * P, (f + 1) * P)
                for n, (ps, sem) in enumerate(((ps_g, gate_done), (ps_u, up_done))):
                    if s >= 2:
                        pe.wait_ge(hid_done, s - 1)
                    for c in range(KD):
                        mm = split3(pe, ps[:, s % 2, :], (g.w13_h[:, n, c, fs], g.w13_l[:, n, c, fs]),
                                    (xt_h[:, half, c, :], xt_l[:, half, c, :]), c == 0, c == KD - 1)
                    mm.then_inc(sem, 1)

            def output(t):
                cols = slice(t % HT * P, (t % HT + 1) * P)
                if t >= 2:
                    pe.wait_ge(y_added, t - 1)
                for f in range(NFF):
                    if t % HT == 0:
                        pe.wait_ge(hid_done, t // HT * NFF + f + 1)
                    mm = pe.matmul(ps_y[:, t % 2, 0:D], hid[:, f, cols], g.w2f[:, f, :], start=(f == 0),
                                   stop=(f == NFF - 1))
                mm.then_inc(y_done, 1)

            for t in range(HT):
                input_tile(t)
            pe.wait_ge(xt_hi, HT)
            pe.wait_ge(xt_lo, HT)
            for f in range(NFF):
                features(f)
                if f % 2:
                    input_tile(HT + f // 2)
            for t in range(HT):
                output(t)
            pe.wait_ge(xt_hi, NT)
            pe.wait_ge(xt_lo, NT)
            for f in range(NFF):
                features(NFF + f)
            for t in range(HT, NT):
                output(t)

        @block.scalar
        def _(act):
            def high(t):
                act.wait_ge(ln.xn_read, t + 1)
                act.activation(xt_h[:, t // HT, :, t % HT * P:(t % HT + 1) * P],
                               ps_x[:, 0:D].rearrange("p (c q) -> p c q", c=KD), ACT.Copy).then_inc(xt_hi, 1)

            def gate(s):
                act.wait_ge(gate_done, s + 1)
                if s >= 2:
                    act.wait_ge(hid_done, s - 1)
                act.activation(silu[:, s % 2, :], ps_g[:, s % 2, :], ACT.Silu).then_inc(silu_done, 1)

            for t in range(HT):
                high(t)
            for f in range(NFF):
                gate(f)
                if f % 2:
                    high(HT + f // 2)
            for f in range(NFF):
                gate(NFF + f)

        @block.vector
        def _(v):
            def low(t):
                v.wait_ge(xt_hi, t + 1)
                half, cols = t // HT, slice(t % HT * P, (t % HT + 1) * P)
                v.tensor_tensor(xt_l[:, half, :, cols], ps_x[:, 0:D].rearrange("p (c q) -> p c q", c=KD),
                                xt_h[:, half, :, cols].bitcast(F32), ALU.subtract).then_inc(xt_lo, 1)

            def norm(t):
                ln.vector_stats(v, t, t)
                ln.vector_scale(v, t, t, t == 0)

            def hidden(s):
                half, f = divmod(s, NFF)
                v.wait_ge(silu_done, s + 1)
                v.wait_ge(up_done, s + 1)
                if half:
                    v.wait_ge(y_done, HT)
                v.tensor_tensor(hid[:, f, :], ps_u[:, s % 2, :], silu[:, s % 2, :], ALU.mult).then_inc(hid_done, 1)

            def add(t):
                v.wait_ge(y_done, t + 1)
                v.tensor_tensor(g.X[:, ds(t * D, D)], g.X[:, ds(t * D, D)], ps_y[:, t % 2, 0:D],
                                ALU.add).then_inc(y_added, 1)

            norm(0)
            for t in range(HT):
                norm(t + 1)
                low(t)
            for f in range(NFF):
                hidden(f)
                if f % 2:
                    t = HT + f // 2
                    low(t)
                    if t + 1 < NT:
                        norm(t + 1)
            for t in range(HT):
                add(t)
            for f in range(NFF):
                hidden(NFF + f)
            for t in range(HT, NT):
                add(t)

        @block.gpsimd
        def _(pool):
            for t in range(NT):
                ln.gpsimd_power(pool, t)


def gated_cumsum(nc, g, dram):
    M = KD
    GH = D // 4
    with ExitStack() as ctx:
        b = Bufs(nc, ctx, "d")
        ln = LayerNorm(b, g)
        w = b.sb("w", [P, KD, 2 * D + GH])
        w_h = b.sb("w_h", [P, KD, 2 * D + GH], F32R)
        w_l = b.sb("w_l", [P, KD, 2 * D + GH], F32R)
        wg2 = b.sb("wg2", [GH, D])
        wu = b.sb("wu", [P, M, D])
        bias = b.sb("bias", [P, 3, M])
        bg1 = b.sb("bg1", [GH, 1])
        taps = b.sb("taps", [P, KD, 4])
        xt = b.sb("xt", [P, KD, T + 2])
        xt_h = b.sb("xt_h", [P, KD, T], F32R)
        xt_l = b.sb("xt_l", [P, KD, T], F32R)
        hidden = b.sb("hidden", [GH, T])
        gates = b.sb("gates", [P, M, T])
        ones = b.sb("ones", [P, T])
        ug = b.sb("ug", [P, M, T])
        vg = b.sb("vg", [P, M, T])
        run = b.sb("run", [P, M, T])
        conv = b.sb("conv", [P, KD, T])
        ps_x = b.ps("ps_x", [P, 512])
        ps_h = b.ps("ps_h", [P, 2, 512])
        ps_uv = b.ps("ps_uv", [P, 2, 512])
        ps_y = b.ps("ps_y", [P, 2, 512])
        loaded = b.sem("loaded")
        small_loaded = b.sem("small_loaded")
        ones_set = b.sem("ones_set")
        w_hi = b.sem("w_hi")
        w_lo = b.sem("w_lo")
        xt_full = b.sem("xt_full")
        xt_hi = b.sem("xt_hi")
        xt_lo = b.sem("xt_lo")
        h_done = b.sem("h_done")
        relu_done = b.sem("relu_done")
        g_done = b.sem("g_done")
        gates_done = b.sem("gates_done")
        uv_done = b.sem("uv_done")
        uv_gated = b.sem("uv_gated")
        run_done = b.sem("run_done")
        out_done = b.sem("out_done")
        conv_done = b.sem("conv_done")
        y_done = b.sem("y_done")
        y_added = b.sem("y_added")
        block = ctx.enter_context(nc.Block())
        halves = [slice(n * HALF, (n + 1) * HALF) for n in range(2)]
        jobs = [(a, m, n) for m in range(M) for a in range(2) for n in range(2)]

        @block.sync
        def _(sp):
            sp.dma_start(w[:], dram["wuvg"]).then_inc(loaded, 16)
            sp.dma_start(wg2[:], dram["wg2"]).then_inc(small_loaded, 16)
            sp.dma_start(wu[:], dram["wu"]).then_inc(small_loaded, 16)
            sp.dma_start(bias[:], dram["bias3"]).then_inc(small_loaded, 16)
            sp.dma_start(bg1[:], dram["bg1"]).then_inc(small_loaded, 16)
            sp.dma_start(taps[:], dram["taps"]).then_inc(small_loaded, 16)

        @block.tensor
        def _(pe):
            def input_tile(t, least):
                if least:
                    pe.wait_ge(xt_full, t)
                    pe.wait_ge(xt_hi, t)
                ln.tensor_transpose(pe, ps_x, t)
            input_tile(0, 0)
            with pe.Fori(1, NT) as t:
                input_tile(t, 1)
            pe.wait_ge(xt_lo, NT)
            pe.wait_ge(w_lo, 1)

            def product(out, cols, n):
                for c in range(KD):
                    mm = split3(pe, out, (w_h[:, c, cols], w_l[:, c, cols]), (xt_h[:, c, halves[n]], xt_l[:, c, halves[n]]),
                                c == 0, c == KD - 1)
                return mm
            for n in range(2):
                product(ps_h[0:GH, n, :], slice(2 * D, 2 * D + GH), n).then_inc(h_done, 1)
            pe.wait_ge(small_loaded, 16 * 5)

            def gate(m):
                for n in range(2):
                    if m == 0:
                        pe.wait_ge(relu_done, n + 1)
                    else:
                        pe.wait_ge(gates_done, n + 1)
                    pe.matmul(ps_h[:, n, :], wg2[:, m * P:(m + 1) * P], hidden[:, halves[n]], start=True,
                              stop=True).then_inc(g_done, 1)

            def uv(j):
                a, m, n = jobs[j]
                if j >= 2:
                    pe.wait_ge(uv_gated, j - 1)
                product(ps_uv[:, j % 2, :], slice(a * D + m * P, a * D + (m + 1) * P), n).then_inc(uv_done, 1)
            pe.wait_ge(relu_done, 2)
            gate(0)
            for j in range(4):
                uv(j)
            gate(1)
            for j in range(4, 8):
                uv(j)
            pe.wait_ge(conv_done, 3 * KD)
            for t in range(NT):
                tokens = slice(t * P, (t + 1) * P)
                if t == 0:
                    pe.wait_ge(out_done, M)
                if t >= 2:
                    pe.wait_ge(y_added, t - 1)
                for m in range(M):
                    pe.matmul(ps_y[:, t % 2, 0:D], run[:, m, tokens], wu[:, m, :], start=(m == 0), stop=False)
                for c in range(KD):
                    mm = pe.matmul(ps_y[:, t % 2, c * P:(c + 1) * P], conv[:, c, tokens], g.ident[:], start=False,
                                   stop=(c == KD - 1))
                mm.then_inc(y_done, 1)

        @block.scalar
        def _(act):
            act.wait_ge(loaded, 16)
            act.activation(w_h[:], w[:], ACT.Copy).then_inc(w_hi, 1)

            def full(t):
                act.wait_ge(ln.xn_read, t + 1)
                act.activation(xt[:, :, ds(t * P + 1, P)], ps_x[:, 0:D].rearrange("p (c q) -> p c q", c=KD),
                               ACT.Copy).then_inc(xt_full, 1)
            full(0)
            with act.Fori(1, NT) as t:
                full(t)
            act.wait_ge(small_loaded, 16 * 5)
            for n in range(2):
                act.wait_ge(h_done, n + 1)
                act.activation(hidden[:, halves[n]], ps_h[0:GH, n, :], ACT.Relu, bias=bg1[:, 0:1]).then_inc(relu_done, 1)
            for m in range(M):
                for n in range(2):
                    act.wait_ge(g_done, 2 * m + n + 1)
                    act.activation(gates[:, m, halves[n]], ps_h[:, n, :], ACT.Sigmoid,
                                   bias=bias[:, 2, m:m + 1]).then_inc(gates_done, 1)

        @block.vector
        def _(v):
            ln.vector_stats(v, 0, 0)
            ln.vector_scale(v, 0, 0, True)
            v.wait_ge(w_hi, 1)
            v.tensor_tensor(w_l[:], w[:], w_h[:].bitcast(F32), ALU.subtract).then_inc(w_lo, 1)

            def high(t):
                v.wait_ge(xt_full, t + 1)
                v.tensor_copy(xt_h[:, :, ds(t * P, P)], ps_x[:, 0:D].rearrange("p (c q) -> p c q", c=KD)).then_inc(xt_hi, 1)

            def step(t):
                ln.vector_stats(v, t + 1, t + 1)
                high(t)
                ln.vector_scale(v, t + 1, t + 1, False)
            step(0)
            with v.Fori(1, NT - 1) as t:
                step(t)
            high(NT - 1)
            v.wait_ge(small_loaded, 16 * 5)

            def gated(j):
                a, m, n = jobs[j]
                v.wait_ge(uv_done, j + 1)
                v.wait_ge(gates_done, 2 * m + n + 1)
                v.scalar_tensor_tensor((ug, vg)[a][:, m, halves[n]], ps_uv[:, j % 2, :], bias[:, a, m:m + 1],
                                       gates[:, m, halves[n]], ALU.add, ALU.mult).then_inc(uv_gated, 1)

            def convolve(c):
                v.wait_ge(ones_set, 2)
                v.tensor_scalar(conv[:, c, :], xt[:, c, 1:T + 1], taps[:, c, 1:2], taps[:, c, 3:4], ALU.mult,
                                ALU.add).then_inc(conv_done, 1)
                for n, tap in enumerate((0, 2)):
                    v.wait_ge(conv_done, 3 * c + n + 1)
                    v.scalar_tensor_tensor(conv[:, c, :], xt[:, c, tap:tap + T], taps[:, c, tap:tap + 1], conv[:, c, :],
                                           ALU.mult, ALU.add).then_inc(conv_done, 1)
            convolve(0)
            for m in range(M):
                for j in range(4 * m, 4 * m + 4):
                    gated(j)
                if m == 0:
                    convolve(1)
                v.wait_ge(uv_gated, 4 * m + 2)
                v.tensor_tensor_scan(run[:, m, :], ones[:], ug[:, m, :], 0.0, ALU.mult, ALU.add).then_inc(run_done, 1)
                v.wait_ge(run_done, m + 1)
                v.wait_ge(uv_gated, 4 * m + 4)
                v.tensor_tensor(run[:, m, :], run[:, m, :], vg[:, m, :], ALU.mult).then_inc(out_done, 1)
            for t in range(NT):
                v.wait_ge(y_done, t + 1)
                v.tensor_tensor(g.X[:, ds(t * D, D)], g.X[:, ds(t * D, D)], ps_y[:, t % 2, 0:D],
                                ALU.add).then_inc(y_added, 1)

        @block.gpsimd
        def _(pool):
            pool.memset(ones[:], 1.0).then_inc(ones_set, 1)
            pool.memset(xt[:, :, 0:T + 2:T + 1], 0.0).then_inc(ones_set, 1)
            ln.gpsimd_power(pool, 0)

            def low(t):
                tokens = ds(t * P, P)
                pool.wait_ge(xt_hi, t + 1)
                pool.tensor_tensor(xt_l[:, :, tokens], xt[:, :, ds(t * P + 1, P)], xt_h[:, :, tokens].bitcast(F32),
                                   ALU.subtract).then_inc(xt_lo, 1)

            def step(t):
                ln.gpsimd_power(pool, t + 1)
                low(t)
            step(0)
            with pool.Fori(1, NT - 1) as t:
                step(t)
            low(NT - 1)


class Persistent:
    pass


def clear_released_semaphores(nc):
    done = sorted(nc.released_uncleared_semaphores)
    runs = []
    for n in done:
        if runs and runs[-1][1] == n:
            runs[-1][1] = n + 1
        else:
            runs.append([n, n + 1])
    with nc.Block() as block:
        @block.gpsimd
        def _(pool):
            for start, end in runs:
                pool.sem_clear(range(start, end))


def build(nc, dram, out):
    with ExitStack() as ctx:
        g = Persistent()
        b = Bufs(nc, ctx, "g")
        X = b.sb("X", [P, NT * D])
        g.X = X
        g.ident = b.sb("ident", [P, P])
        g.ident_b = b.sb("ident_b", [P, P], BF16)
        g.causal = b.sb("causal", [P, P], BF16)
        g.neg_half = b.sb("neg_half", [P, 8])
        g.qnw0 = b.sb("qnw0", [P, 1])
        g.qnw1 = b.sb("qnw1", [QR1, 1])
        g.kvw = b.sb("kvw", [P, 1])
        g.kvw_s = b.sb("kvw_s", [P, 1])
        g.w1_raw = b.sb("w1_raw", [P, KD, W1_N])
        g.loaded_x = b.sem("loaded_x")
        g.loaded_const = b.sem("loaded_const")
        g.loaded_wa = b.sem("loaded_wa")
        g.loaded_wr = b.sem("loaded_wr")
        g.loaded_w1 = b.sem("loaded_w1")
        g.loaded_w2 = b.sem("loaded_w2")
        g.neg_half_set = b.sem("neg_half_set")
        g.vext_done = b.sem("vext_done")
        g.kvw_scaled = b.sem("kvw_scaled")
        g.ones_set = b.sem("ones_set")
        stored = b.sem("stored")
        g.N_CONST = 7

        with ExitStack() as actx:
            a = Bufs(nc, actx, "a")
            g.wvo = a.sb("wvo", [P, NP, D])
            g.u_space = a.sb("u", [P, NT * H * (KL + 1)])
            g.u = g.u_space[:].rearrange("p (t h c) -> p t h c", h=H, c=KL + 1)
            with ExitStack() as hctx:
                h = Bufs(nc, hctx, "h")
                g.kt_h = h.sb("kt_h", [P, 2, T], F32R)
                g.kt_l = h.sb("kt_l", [P, 2, T], F32R)
                g.vext = h.sb("vext", [P, NT, KL + 1])
                g.qrt = h.sb("qrt", [P, NP, T])
                g.qat0 = h.sb("qat0", [P, T])
                g.qat1 = h.sb("qat1", [QR1, T])
                with ExitStack() as wctx:
                    w = Bufs(nc, wctx, "w")
                    g.cos_q = w.sb("cos_q", [P, NT, DR])
                    g.sin_q = w.sb("sin_q", [P, NT, DR])
                    g.cos_k = w.sb("cos_k", [P, NT, DR])
                    g.sin_k = w.sb("sin_k", [P, NT, DR])
                    g.wa = w.sb("wa", [P, KD, WA_N])
                    g.wr0 = g.u_space[:, 0:H * DR]
                    g.wr1 = g.u_space[0:QR1, H * DR:2 * H * DR]
                    with nc.Block() as block:
                        @block.sync
                        def _(sp):
                            sp.dma_start(X[:].rearrange("p (t d) -> p t d", d=D), dram["x"]).then_inc(g.loaded_x, 16)
                            sp.dma_start(g.ident[:], dram["ident"]).then_inc(g.loaded_const, 16)
                            sp.dma_start(g.wa[:], dram["wa"]).then_inc(g.loaded_wa, 16)
                            sp.dma_start(g.wr0, dram["wr"][0:P, :]).then_inc(g.loaded_wr, 16)
                            sp.dma_start(g.wr1, dram["wr"][P:QL, :]).then_inc(g.loaded_wr, 16)

                        @block.scalar
                        def _(act):
                            act.dma_start(g.cos_k[:], dram["cos_k"]).then_inc(g.loaded_const, 16)
                            act.dma_start(g.sin_k[:], dram["sin_k"]).then_inc(g.loaded_const, 16)
                            act.dma_start(g.cos_q[:], dram["cos_q"]).then_inc(g.loaded_const, 16)
                            act.dma_start(g.sin_q[:], dram["sin_q"]).then_inc(g.loaded_const, 16)
                            act.dma_start(g.qnw0[:], dram["qnw"][0:P, :]).then_inc(g.loaded_wr, 16)
                            act.dma_start(g.qnw1[:], dram["qnw"][P:QL, :]).then_inc(g.loaded_wr, 16)
                            act.dma_start(g.kvw[:], dram["kvw"]).then_inc(g.loaded_wr, 16)
                            act.dma_start(g.causal[:], dram["causal"]).then_inc(g.loaded_const, 16)
                            act.dma_start(g.ident_b[:], dram["ident_b"]).then_inc(g.loaded_const, 16)

                        @block.gpsimd
                        def _(pool):
                            pool.memset(g.neg_half[:], -0.5).then_inc(g.neg_half_set, 1)
                            pool.memset(g.vext[:], 1.0).then_inc(g.ones_set, 1)
                            pool.wait_ge(g.loaded_wr, 16 * 5)
                            pool.tensor_scalar(g.kvw_s[:], g.kvw[:], float((DN + DR) ** -0.5), None,
                                               ALU.mult).then_inc(g.kvw_scaled, 1)
                            pool.wait_ge(g.ones_set, 1)
                    latent_projections(nc, g, dram)
                latent_heads(nc, g, dram)
            latent_output(nc, g)

        experts_and_middle(nc, g, dram)
        clear_released_semaphores(nc)
        many_head_attention(nc, g, dram)
        f = Bufs(nc, ctx, "f")
        g.w13_h = f.sb("w13_h", [P, 2, KD, FF], F32R)
        g.w13_l = f.sb("w13_l", [P, 2, KD, FF], F32R)
        g.w2f = f.sb("w2f", [P, NFF, D])
        prepare_ffn(nc, g, dram)
        feed_forward(nc, g, "f1")
        gated_cumsum(nc, g, dram)
        feed_forward(nc, g, "f2")

        with nc.Block() as block:
            @block.sync
            def _(sp):
                sp.wait_ge(g.loaded_const, 16 * g.N_CONST)
                sp.dma_start(out, X[:].rearrange("p (t d) -> p t d", d=D)).then_inc(stored, 16)
                sp.wait_ge(stored, 16)


def _rope_tables(np):
    inv = np.float32(1.0) / np.float32(10000.0) ** (np.arange(0, DR, 2, dtype=np.float32) / np.float32(DR))
    freqs = np.outer(np.arange(T, dtype=np.float32), inv.astype(np.float32)).astype(np.float32)
    cos, sin = np.cos(freqs), np.sin(freqs)
    lay = lambda a: np.ascontiguousarray(a.reshape(NT, P, DR).transpose(1, 0, 2).astype(np.float32))
    return lay(np.concatenate([cos, cos], 1)), lay(np.concatenate([-sin, sin], 1))


def kernel(**inputs):
    import ml_dtypes
    import numpy as np
    import concourse.bacc as bacc
    from concourse.bass_utils import run_bass_kernel_spmd

    w = {k: np.asarray(v) for k, v in inputs.items()}
    rows = lambda a: np.ascontiguousarray(a.reshape(KD, P, -1).transpose(1, 0, 2))
    cat = np.concatenate
    arrays = {}
    arrays["x"] = np.ascontiguousarray(w["L0_attn_a_hidden_states"][0].reshape(NT, P, D).transpose(1, 0, 2))

    wq_b = w["L0_attn_a_Wq_b"].reshape(QL, H, DN + DR)
    wkv_b = w["L0_attn_a_Wkv_b"].reshape(KL, H, 2 * DN)
    wo = w["L0_attn_a_Wo"].reshape(H, DN, D)
    arrays["wa"] = rows(cat([w["L0_attn_a_Wq_a"], w["L0_attn_a_Wkv_a"], w["L0_attn_a_Wk_rope"]], 1))
    arrays["wr"] = np.ascontiguousarray(wq_b[:, :, DN:]).reshape(QL, H * DR)
    heads = cat([wq_b[:, :, :DN].transpose(1, 2, 0), wkv_b[:, :, :DN].transpose(1, 2, 0),
                 wkv_b[:, :, DN:].transpose(1, 2, 0), wo], 2)
    arrays["wh"] = np.ascontiguousarray(heads.reshape(NP, 2, P, WH_N).transpose(0, 2, 1, 3))
    arrays["qnw"] = w["L0_attn_a_q_norm_w"].reshape(QL, 1)
    arrays["kvw"] = cat([w["L0_attn_a_kv_norm_w"]] * 2).reshape(P, 1)

    w1 = [w["L0_ffn_sw1"].T, w["L0_ffn_sw2"].T, w["L0_ffn_gate_w"].T] + list(w["L0_ffn_w1"])
    arrays["w1"] = rows(cat(w1, 1))
    arrays["w2"] = cat([w["L0_ffn_sw3"].T, w["L0_ffn_w2"].reshape(NE * FI, D)], 0)

    arrays["wb"] = np.stack([rows(w["L0_attn_b_W_q"].T), rows(w["L0_attn_b_W_k"].T), rows(w["L0_attn_b_W_v"].T),
                             rows(w["L0_attn_b_W_o"])], 1)

    arrays["wqkv"] = rows(w["L1_attn_a_w_qkv"])
    arrays["wout"] = rows(w["L1_attn_a_w_out"])

    arrays["w13"] = np.stack([rows(w["L1_ffn_W1"].T), rows(w["L1_ffn_W3"].T)], 1)
    arrays["w2f"] = w["L1_ffn_W2"].T.reshape(NFF, P, D).transpose(1, 0, 2)
    had = np.ones((1, 1), np.float32)
    while had.shape[0] < P:
        had = np.block([[had, had], [had, -had]])
    arrays["had"] = had

    chunks = lambda a: a.reshape(KD, P, -1).transpose(1, 0, 2)
    arrays["wuvg"] = rows(cat([w["L1_attn_b_Wu"].T, w["L1_attn_b_Wv"].T, w["L1_attn_b_Wg1"].T], 1))
    arrays["wg2"] = w["L1_attn_b_Wg2"].T
    arrays["wu"] = rows(w["L1_attn_b_Wu"].T)
    arrays["bias3"] = np.stack([chunks(w[f"L1_attn_b_{n}"])[:, :, 0] for n in ("bu", "bv", "bg2")], 1)
    arrays["bg1"] = w["L1_attn_b_bg1"].reshape(-1, 1)
    arrays["taps"] = cat([chunks(w["L1_attn_b_conv_w"].reshape(D, 3)), chunks(w["L1_attn_b_conv_b"])], 2)

    cos, sin = _rope_tables(np)
    scale = np.float32((DN + DR) ** -0.5)
    arrays["cos_k"], arrays["sin_k"] = cos, sin
    arrays["cos_q"], arrays["sin_q"] = cos * scale, sin * scale
    arrays["ident"] = np.eye(P, dtype=np.float32)
    arrays["ident_b"] = np.eye(P, dtype=ml_dtypes.bfloat16)
    arrays["causal"] = np.where(np.tri(P, dtype=bool), 0.0, -3e38).astype(ml_dtypes.bfloat16)

    nc = bacc.Bacc("TRN2", target_bir_lowering=False, num_devices=1)
    dram = {}
    for name, a in arrays.items():
        a = arrays[name] = np.ascontiguousarray(a)
        dram[name] = nc.dram_tensor(name, a.shape, mybir.dt.from_np(a.dtype), kind="ExternalInput").ap()
    out = nc.dram_tensor("out", (P, NT, D), F32, kind="ExternalOutput").ap()
    build(nc, dram, out)
    r = run_bass_kernel_spmd(nc, [arrays], core_ids=[0])
    got = r.results[0]["out"]
    return np.ascontiguousarray(np.asarray(got).transpose(1, 0, 2)).reshape(1, T, D)
```

```python
from contextlib import ExitStack

import concourse.bass as bass
from concourse import mybir

ALU = mybir.AluOpType
ACT = mybir.ActivationFunctionType
AX = mybir.AxisListType.X
F32 = mybir.dt.float32
F32R = mybir.dt.float32r
BF16 = mybir.dt.bfloat16

P = 128
T, D = 1024, 256
NT = T // P
KD = D // P
LN_EPS = 1e-5

H = 16
NP = H // 2
QL, KL, DR, DN = 192, 64, 64, 128
QR1 = QL - P
WA_N = QL + KL + DR
RMS_EPS = 1e-6
WH_N = QL + KL + KL + D

NE, FI = 8, 176
BLK = 2 * FI
W1_N = (NE + 1) * BLK + NE
FH = (NE + 1) * FI
NF = (FH + P - 1) // P
FTAIL = FH - (NF - 1) * P

HD = D // H
FF = 1024
NFF = FF // P


def ds(start, size):
    return bass.ds(start, size)


class Bufs:

    def __init__(self, nc, ctx, tag):
        self.nc, self.ctx, self.tag = nc, ctx, tag

    def sb(self, name, shape, dt=F32):
        return self.ctx.enter_context(self.nc.sbuf_tensor(f"{self.tag}_{name}", shape, dt))

    def ps(self, name, shape, dt=F32):
        return self.ctx.enter_context(self.nc.psum_tensor(f"{self.tag}_{name}", shape, dt))

    def sem(self, name):
        return self.ctx.enter_context(self.nc.semaphore(f"{self.tag}_{name}"))


def split3(pe, out, lhs, rhs, start, stop):
    (lh, ll), (rh, rl) = lhs, rhs
    pe.matmul(out, lh, rh, start=start, stop=False)
    pe.matmul(out, lh, rl, start=False, stop=False)
    return pe.matmul(out, ll, rh, start=False, stop=stop)


def staged(stages, eng, step):
    for i in range(stages):
        step(i, *[s <= i for s in range(stages)], i)
    with eng.Fori(stages, NT) as i:
        step(i, *[True] * stages, stages)
    for i in range(NT, NT + stages - 1):
        step(i, *[s > i - NT for s in range(stages)], i)


class LayerNorm:

    def __init__(self, b, g):
        self.g = g
        self.stats = b.sb("ln_stats", [P, 6])
        self.mean_var = b.sb("ln_mean_var", [P, 2])
        self.var_eps = b.sb("ln_var_eps", [P, 1])
        self.rstd = b.sb("ln_rstd", [P, 1])
        self.xn = b.sb("ln_xn", [P, D])
        self.waiter = b.sb("ln_waiter", [1, 1])
        self.stats_done = b.sem("ln_stats_done")
        self.aggr_done = b.sem("ln_aggr_done")
        self.var_done = b.sem("ln_var_done")
        self.rstd_done = b.sem("ln_rstd_done")
        self.xn_done = b.sem("ln_xn_done")
        self.xn_read = b.sem("ln_xn_read")

    def vector_stats(self, v, t, n):
        v.bn_stats(self.stats[:], self.g.X[:, ds(t * D, D)]).then_inc(self.stats_done, 1)
        v.wait_ge(self.stats_done, n + 1)
        v.memset(self.waiter[:], 0.0)
        v.bn_aggr(self.mean_var[:], self.stats[:]).then_inc(self.aggr_done, 1)
        v.wait_ge(self.aggr_done, n + 1)
        v.tensor_scalar(self.var_eps[:], self.mean_var[:, 1:2], LN_EPS, None, ALU.add).then_inc(self.var_done, 1)

    def gpsimd_power(self, pool, n):
        pool.wait_ge(self.var_done, n + 1)
        pool.tensor_tensor(self.rstd[:], self.var_eps[:], self.g.neg_half[:, 0:1], ALU.pow).then_inc(self.rstd_done, 1)

    def vector_scale(self, v, t, n, first):
        v.wait_ge(self.rstd_done, n + 1)
        if not first:
            v.wait_ge(self.xn_read, n)
        v.tensor_scalar(self.xn[:], self.g.X[:, ds(t * D, D)], self.mean_var[:, 0:1], self.rstd[:, 0:1],
                        ALU.subtract, ALU.mult).then_inc(self.xn_done, 1)

    def tensor_transpose(self, pe, out, n):
        pe.wait_ge(self.xn_done, n + 1)
        for c in range(KD):
            mm = pe.transpose(out[:, c * P:(c + 1) * P], self.xn[:, c * P:(c + 1) * P], self.g.ident[:])
        mm.then_inc(self.xn_read, 1)


def latent_projections(nc, g, dram):
    with ExitStack() as ctx:
        b = Bufs(nc, ctx, "a1")
        ln = LayerNorm(b, g)
        wa_h = b.sb("wa_h", [P, KD, WA_N], F32R)
        wa_l = b.sb("wa_l", [P, KD, WA_N], F32R)
        xt_h = b.sb("xt_h", [P, KD * P], F32R)
        xt_l = b.sb("xt_l", [P, KD * P], F32R)
        square = b.sb("square", [P, QL])
        sumsq = b.sb("sumsq", [P, 2])
        meansq = b.sb("meansq", [P, 2])
        rrms = b.sb("rrms", [P, 2])
        qa = b.sb("qa", [P, QL])
        kck = b.sb("kck", [P, 3, DR])
        krc = b.sb("krc", [P, DR])
        krs = b.sb("krs", [P, DR])
        qat0 = b.sb("qat0", [P, P])
        qat1 = b.sb("qat1", [QR1, P])
        rot = g.u_space[:, 2048:3072].rearrange("p (h c) -> p h c", c=DR)
        rot_s = g.u_space[:, 3072:4096].rearrange("p (h c) -> p h c", c=DR)
        qr = b.sb("qr", [P, H * DR])
        rot_c = qr[:].rearrange("p (h c) -> p h c", c=DR)
        ps_x = b.ps("ps_x", [P, 512])
        ps_a = b.ps("ps_a", [P, 512])
        ps_t = b.ps("ps_t", [P, 512])
        ps_r = b.ps("ps_r", [P, 2, 512])
        ps_q = b.ps("ps_q", [P, 2, 512])
        ps_w = b.ps("ps_w", [P, 512])
        wh = b.sb("wh", [P, 2, WH_N])
        wh_loaded = b.sem("wh_loaded")
        w_done = b.sem("w_done")
        w_evac = b.sem("w_evac")
        wa_split = b.sem("wa_split")
        wr_scaled = b.sem("wr_scaled")
        xt_hi = b.sem("xt_hi")
        xt_lo = b.sem("xt_lo")
        proj_done = b.sem("proj_done")
        sumsq_done = b.sem("sumsq_done")
        meansq_done = b.sem("meansq_done")
        rrms_done = b.sem("rrms_done")
        kr_parts = b.sem("kr_parts")
        kr_done = b.sem("kr_done")
        latents_done = b.sem("latents_done")
        key_copied = b.sem("key_copied")
        lat_t_done = b.sem("lat_t_done")
        lat_evac = b.sem("lat_evac")
        key_lo = b.sem("key_lo")
        qat_kept = b.sem("qat_kept")
        rope_mm = b.sem("rope_mm")
        rot_copied = b.sem("rot_copied")
        rot_s_done = b.sem("rot_s_done")
        rot_c_done = b.sem("rot_c_done")
        qr_done = b.sem("qr_done")
        qr_t_done = b.sem("qr_t_done")
        qr_evac = b.sem("qr_evac")
        block = ctx.enter_context(nc.Block())

        @block.sync
        def _(sp):
            def load(p, first):
                if not first:
                    sp.wait_ge(w_done, p)
                sp.dma_start(wh[:], dram["wh"][ds(p, 1)].squeeze(0)).then_inc(wh_loaded, 16)
            load(0, True)
            with sp.Fori(1, NP) as p:
                load(p, False)


        @block.tensor
        def _(pe):
            def step(i, one, two, three, four, least):
                if two:
                    t = i - 1
                    pe.wait_ge(xt_hi, t + 1)
                    pe.wait_ge(xt_lo, t + 1)
                    if least == 1:
                        pe.wait_ge(wa_split, 2)
                    if least >= 2:
                        pe.wait_ge(latents_done, 2 * t)
                        pe.wait_ge(kr_parts, 2 * t)
                    for c in range(KD):
                        cs = slice(c * P, (c + 1) * P)
                        mm = split3(pe, ps_a[:, 0:WA_N], (xt_h[:, cs], xt_l[:, cs]), (wa_h[:, c, :], wa_l[:, c, :]),
                                    c == 0, c == KD - 1)
                    mm.then_inc(proj_done, 1)
                if three:
                    t = i - 2
                    pe.wait_ge(latents_done, 2 * t + 2)
                    pe.wait_ge(key_copied, t + 1)
                    if least >= 3:
                        pe.wait_ge(lat_evac, 3 * t)
                        pe.wait_ge(key_lo, t)
                    pe.transpose(ps_t[:, 0:P], qa[:, 0:P], g.ident[:])
                    pe.transpose(ps_t[0:QR1, P:2 * P], qa[:, P:QL], g.ident[:])
                    pe.transpose(ps_t[:, 2 * P:3 * P], kck[:, 0:2, :], g.ident[:])
                    pe.transpose(ps_t[:, 3 * P:4 * P], kck[:, 1:3, :], g.ident[:]).then_inc(lat_t_done, 1)
                if two:
                    t = i - 1
                    pe.wait_ge(wh_loaded, 16 * t + 16)
                    if least >= 2:
                        pe.wait_ge(w_evac, 3 * t)
                    for head in range(2):
                        c = (1 - head) * KL
                        pe.matmul(ps_w[:, c:c + KL], wh[:, head, 0:P], wh[:, head, QL:QL + KL], start=True, stop=True)
                        pe.matmul(ps_w[0:QR1, P + c:P + c + KL], wh[:, head, P:QL], wh[:, head, QL:QL + KL],
                                  start=True, stop=True)
                    for head in range(2):
                        mm = pe.matmul(ps_w[head * KL:(head + 1) * KL, 2 * P:512], wh[:, head, QL + KL:QL + 2 * KL],
                                       wh[:, head, QL + 2 * KL:WH_N], start=True, stop=True)
                    mm.then_inc(w_done, 1)
                if one:
                    if least >= 1:
                        pe.wait_ge(xt_hi, i)
                        pe.wait_ge(xt_lo, i)
                    ln.tensor_transpose(pe, ps_x, i)
                if three:
                    t = i - 2
                    pe.wait_ge(lat_evac, 3 * t + 2)
                    if least >= 3:
                        pe.wait_ge(rot_copied, t)
                        pe.wait_ge(rot_c_done, t)
                    if least == 2:
                        pe.wait_ge(wr_scaled, 2)
                    for n in range(2):
                        pe.matmul(ps_r[:, n, :], qat0[:], g.wr0[:, n * 512:(n + 1) * 512], start=True, stop=False)
                        mm = pe.matmul(ps_r[:, n, :], qat1[:], g.wr1[:, n * 512:(n + 1) * 512], start=False, stop=True)
                    mm.then_inc(rope_mm, 1)
                if four:
                    t = i - 3
                    pe.wait_ge(qr_done, t + 1)
                    if least >= 4:
                        pe.wait_ge(qr_evac, 2 * t)
                    for c in range(NP):
                        mm = pe.transpose(ps_q[:, c // 4, (c % 4) * P:(c % 4 + 1) * P], qr[:, c * P:(c + 1) * P],
                                          g.ident[:])
                    mm.then_inc(qr_t_done, 1)

            pe.wait_ge(g.loaded_ident, 16)
            staged(4, pe, step)

        @block.scalar
        def _(act):
            def step(i, one, two, three, four, least):
                if two:
                    t = i - 1
                    act.wait_ge(proj_done, t + 1)
                    if least >= 2:
                        act.wait_ge(meansq_done, 2 * t)
                    act.activation(square[:], ps_a[:, 0:QL], ACT.Square,
                                   accum_out=sumsq[:, 0:1]).then_inc(sumsq_done, 1)
                    act.wait_ge(sumsq_done, 2 * t + 1)
                    act.activation(square[:, 0:KL], ps_a[:, QL:QL + KL], ACT.Square,
                                   accum_out=sumsq[:, 1:2]).then_inc(sumsq_done, 1)
                if three:
                    t = i - 2
                    act.wait_ge(lat_t_done, t + 1)
                    if least >= 3:
                        act.wait_ge(rope_mm, t)
                        act.wait_ge(qat_kept, 2 * t)
                    act.activation(qat0[:], ps_t[:, 0:P], ACT.Copy).then_inc(lat_evac, 1)
                    act.activation(qat1[:], ps_t[0:QR1, P:2 * P], ACT.Copy).then_inc(lat_evac, 1)
                    act.activation(g.kt_h[:, :, ds(t * P, P)], ps_t[:, 2 * P:4 * P].rearrange("p (a c) -> p a c", a=2),
                                   ACT.Copy).then_inc(lat_evac, 1)
                if two:
                    t = i - 1
                    if least == 1:
                        act.wait_ge(g.loaded_wr, 16 * 5)
                        act.activation(g.wr0, g.wr0, ACT.Copy, scale=g.qnw0[:, 0:1]).then_inc(wr_scaled, 1)
                        act.activation(g.wr1, g.wr1, ACT.Copy, scale=g.qnw1[:, 0:1]).then_inc(wr_scaled, 1)
                    act.wait_ge(w_done, t + 1)
                    act.activation(g.wq[:, ds(t, 1), 0:P].squeeze(1), ps_w[:, 0:P], ACT.Copy,
                                   scale=g.qnw0[:, 0:1]).then_inc(w_evac, 1)
                    act.activation(g.wq[0:QR1, ds(t, 1), P:2 * P].squeeze(1), ps_w[0:QR1, P:2 * P], ACT.Copy,
                                   scale=g.qnw1[:, 0:1]).then_inc(w_evac, 1)
                    act.activation(g.wvo[:, ds(t, 1), :].squeeze(1), ps_w[:, 2 * P:512], ACT.Copy,
                                   scale=g.kvw[:, 0:1]).then_inc(w_evac, 1)
                if one:
                    act.wait_ge(ln.xn_read, i + 1)
                    if least >= 1:
                        act.wait_ge(proj_done, i)
                    act.activation(xt_h[:], ps_x[:, 0:KD * P], ACT.Copy).then_inc(xt_hi, 1)
                if two:
                    t = i - 1
                    act.wait_ge(kr_done, t + 1)
                    act.activation(kck[:, 2, :], kck[:, 0, :], ACT.Copy).then_inc(key_copied, 1)
                if three:
                    t = i - 2
                    act.wait_ge(rope_mm, t + 1)
                    if least >= 3:
                        act.wait_ge(rot_s_done, t)
                    act.activation(rot, ps_r[:].rearrange("p a (h c) -> p (a h) c", c=DR),
                                   ACT.Copy).then_inc(rot_copied, 1)
                if four:
                    t = i - 3
                    act.wait_ge(qr_t_done, t + 1)
                    act.activation(g.qrt[:, 0:4, ds(t * P, P)], ps_q[:, 0, :].rearrange("p (a c) -> p a c", a=4),
                                   ACT.Copy).then_inc(qr_evac, 1)
            act.wait_ge(g.loaded_wa, 16)
            act.activation(wa_h[:], g.wa[:], ACT.Copy).then_inc(wa_split, 1)
            staged(4, act, step)

        @block.vector
        def _(v):
            def step(i, one, two, three, four, least):
                if one:
                    ln.vector_stats(v, i, i)
                if four:
                    t = i - 3
                    v.wait_ge(rot_c_done, t + 1)
                    v.wait_ge(rot_s_done, t + 1)
                    v.tensor_tensor(qr[:].rearrange("p (h c) -> p h c", c=DR), rot_c, rot_s,
                                    ALU.add).then_inc(qr_done, 1)
                if two and least == 1:
                    v.wait_ge(wa_split, 1)
                    v.tensor_tensor(wa_l[:], g.wa[:], wa_h[:].bitcast(F32), ALU.subtract).then_inc(wa_split, 1)
                if two:
                    t = i - 1
                    v.wait_ge(sumsq_done, 2 * t + 2)
                    v.tensor_scalar(meansq[:, 0:1], sumsq[:, 0:1], 1.0 / QL, RMS_EPS, ALU.mult,
                                    ALU.add).then_inc(meansq_done, 1)
                    v.tensor_scalar(meansq[:, 1:2], sumsq[:, 1:2], 1.0 / KL, RMS_EPS, ALU.mult,
                                    ALU.add).then_inc(meansq_done, 1)
                if one:
                    ln.vector_scale(v, i, i, least == 0)
                if two:
                    t = i - 1
                    if least == 1:
                        v.wait_ge(g.loaded_const, 16 * g.N_CONST)
                    key = ps_a[:, QL + KL:WA_N]
                    v.tensor_tensor(krc[:], key, g.cos_k[:, ds(t, 1), :].squeeze(1), ALU.mult).then_inc(kr_parts, 1)
                    swapped = key.rearrange("p (a c) -> p a c", a=2)[:, ::-1, :]
                    v.tensor_tensor(krs[:].rearrange("p (a c) -> p a c", a=2), swapped,
                                    g.sin_k[:, ds(t, 1), :].rearrange("p o (a c) -> p (o a) c", a=2),
                                    ALU.mult).then_inc(kr_parts, 1)
                    if least >= 2:
                        v.wait_ge(lat_t_done, t)
                        v.wait_ge(key_copied, t)
                        v.wait_ge(g.vext_done, t)
                    v.wait_ge(kr_parts, 2 * t + 2)
                    v.tensor_tensor(kck[:, 0, :], krc[:], krs[:], ALU.add).then_inc(kr_done, 1)
                    v.wait_ge(rrms_done, t + 1)
                    v.tensor_scalar(qa[:], ps_a[:, 0:QL], rrms[:, 0:1], None, ALU.mult).then_inc(latents_done, 1)
                    v.tensor_scalar(kck[:, 1, :], ps_a[:, QL:QL + KL], rrms[:, 1:2], None,
                                    ALU.mult).then_inc(latents_done, 1)
                if three:
                    t = i - 2
                    v.wait_ge(lat_evac, 3 * t + 3)
                    v.tensor_tensor(g.kt_l[:, :, ds(t * P, P)], ps_t[:, 2 * P:4 * P].rearrange("p (a c) -> p a c", a=2),
                                    g.kt_h[:, :, ds(t * P, P)].bitcast(F32), ALU.subtract).then_inc(key_lo, 1)
                if one:
                    v.wait_ge(ln.xn_read, i + 1)
                    v.wait_ge(xt_hi, i + 1)
                    if least >= 1:
                        v.wait_ge(proj_done, i)
                    v.tensor_tensor(xt_l[:], ps_x[:, 0:KD * P], xt_h[:].bitcast(F32), ALU.subtract).then_inc(xt_lo, 1)
                if four:
                    t = i - 3
                    v.wait_ge(qr_t_done, t + 1)
                    v.tensor_copy(g.qrt[:, 4:8, ds(t * P, P)],
                                  ps_q[:, 1, :].rearrange("p (a c) -> p a c", a=4)).then_inc(qr_evac, 1)
                if three:
                    t = i - 2
                    v.wait_ge(rope_mm, t + 1)
                    v.wait_ge(rot_copied, t + 1)
                    if least >= 3:
                        v.wait_ge(qr_t_done, t)
                    v.tensor_tensor(rot_c, ps_r[:].rearrange("p a (h c) -> p (a h) c", c=DR),
                                    g.cos_q[:, ds(t, 1), :].broadcast_to([P, H, DR]), ALU.mult).then_inc(rot_c_done, 1)
            v.wait_ge(g.loaded_x, 16)
            staged(4, v, step)

        @block.gpsimd
        def _(pool):
            pool.wait_ge(g.neg_half_set, 1)

            def step(i, one, two, three, four, least):
                if one:
                    ln.gpsimd_power(pool, i)
                if two:
                    t = i - 1
                    pool.wait_ge(meansq_done, 2 * t + 2)
                    if least >= 2:
                        pool.wait_ge(latents_done, 2 * t)
                    pool.tensor_tensor(rrms[:], meansq[:], g.neg_half[:, 0:2], ALU.pow).then_inc(rrms_done, 1)
                if three:
                    t = i - 2
                    pool.wait_ge(lat_evac, 3 * t + 2)
                    pool.tensor_copy(g.qat0[:, ds(t * P, P)], qat0[:]).then_inc(qat_kept, 1)
                    pool.tensor_copy(g.qat1[:, ds(t * P, P)], qat1[:]).then_inc(qat_kept, 1)
                if two:
                    t = i - 1
                    pool.wait_ge(latents_done, 2 * t + 2)
                    pool.tensor_copy(g.vext[:, ds(t, 1), 0:KL].squeeze(1), kck[:, 1, :]).then_inc(g.vext_done, 1)
                if three:
                    t = i - 2
                    pool.wait_ge(rot_copied, t + 1)
                    if least >= 3:
                        pool.wait_ge(qr_done, t)
                    pool.tensor_tensor(rot_s.rearrange("p h (a c) -> p h a c", a=2),
                                       rot.rearrange("p h (a c) -> p h a c", a=2)[:, :, ::-1, :],
                                       g.sin_q[:, ds(t, 1), :].rearrange("p o (a c) -> p o a c", a=2).broadcast_to([P, H, 2, DR // 2]),
                                       ALU.mult).then_inc(rot_s_done, 1)
            staged(4, pool, step)
            pool.wait_ge(g.loaded_wr, 16 * 5)
            pool.tensor_scalar(g.kvw_s[:], g.kvw[:], float((DN + DR) ** -0.5), None, ALU.mult).then_inc(g.kvw_scaled, 1)


class CausalHeads:

    UNITS = [(head, block) for head in range(2) for block in range(NT // 4)]
    NU = len(UNITS)
    S_JOBS = [[(q, k, min(k + 4, q + 1)) for q in range(4 * blk, 4 * blk + 4) for k in range(0, q + 1, 4)]
              for _, blk in UNITS]
    T_JOBS = [[(k, max(k, 4 * blk)) for k in range(4 * blk + 4)] for _, blk in UNITS]
    SLOTS_S, SLOTS_T = 2, 3
    AHEAD = 0.6
    BEHIND = 0.2

    def __init__(self, b, g, width):
        self.g, self.width = g, width
        self.s_off, self.t_off = [0], [0]
        for s_jobs, t_jobs in zip(self.S_JOBS, self.T_JOBS):
            self.s_off.append(self.s_off[-1] + len(s_jobs))
            self.t_off.append(self.t_off[-1] + len(t_jobs))
        assert [blk for _, blk in self.UNITS] == [0, 1, 0, 1]
        self.NS, self.NTR = self.s_off[-1], self.t_off[-1]
        assert self.NS % self.SLOTS_S == 0 and self.NTR % self.SLOTS_T == 0
        self.p = b.sb("p", [P, self.t_off[2], 4 * P])
        self.p_row = [self.t_off[blk] for _, blk in self.UNITS]
        self.part = b.sb("part", [P, 4, 2])
        self.negmax = b.sb("negmax", [P, 2, 4])
        self.diag = b.sb("diag", [P, 2, 4, P], F32R)
        self.ones = b.sb("ones", [P, P], F32R)
        self.ps_s = b.ps("ps_s", [P, self.SLOTS_S, 512])
        self.ps_t = b.ps("ps_t", [P, self.SLOTS_T, 512])
        self.ps_u = b.ps("ps_u", [P, 2, 512])
        self.ones_done = b.sem("ones_done")
        self.scores_done = b.sem("scores_done")
        self.max_done = b.sem("max_done")
        self.joined = b.sem("joined")
        self.diag_done = b.sem("diag_done")
        self.trans_done = b.sem("trans_done")
        self.exp_done = b.sem("exp_done")
        self.value_done = b.sem("value_done")
        self.u_read = b.sem("u_read")

    def make_ones(self, v):
        v.tensor_scalar(self.ones[:], self.g.ident[:], 0.0, 1.0, ALU.mult, ALU.add).then_inc(self.ones_done, 1)

    def scores(self, pe, n, s, u, i, product, first):
        head = self.UNITS[u][0]
        q, k0, k1 = self.S_JOBS[u][i]
        job = self.s_off[u] + i
        if not (first and job < self.SLOTS_S):
            pe.wait_ge(self.max_done, self.NS * n + job - self.SLOTS_S + 1)
        out = self.ps_s[:, job % self.SLOTS_S, 0:(k1 - k0) * P]
        masked = k1 == q + 1
        mm = product(pe, out, s, head, q, k0, k1, not masked)
        if masked:
            mm = pe.matmul(out[:, (q - k0) * P:(q - k0 + 1) * P], self.g.ident_b[:], self.g.causal[:],
                           start=False, stop=True)
        mm.then_inc(self.scores_done, 1)

    def transposed(self, pe, n, s, u, i, product_t, first):
        head, blk = self.UNITS[u]
        k, q0 = self.T_JOBS[u][i]
        job = self.t_off[u] + i
        if i == 0:
            pe.wait_ge(self.diag_done, self.NU * n + u + 1)
        if not (first and job < self.SLOTS_T):
            pe.wait_ge(self.exp_done, self.NTR * n + job - self.SLOTS_T + 1)
        out = self.ps_t[:, job % self.SLOTS_T, (q0 - 4 * blk) * P:4 * P]
        product_t(pe, out, s, head, k, q0, 4 * blk + 4)
        masked = k >= 4 * blk
        mm = pe.matmul(out, self.ones[:], self.diag[:, u % 2, q0 - 4 * blk:4, :], start=False, stop=not masked)
        if masked:
            mm = pe.matmul(out[:, 0:P], self.g.causal[:], self.g.ident_b[:], start=False, stop=True)
        mm.then_inc(self.trans_done, 1)

    def values(self, pe, n, s, u, j, value, first):
        head, blk = self.UNITS[u]
        q = 4 * blk + j
        if j == 0 and not (first and u < 2):
            pe.wait_ge(self.u_read, self.NU * n + u - 1)
        pe.wait_ge(self.exp_done, self.NTR * n + self.t_off[u] + q + 1)
        for k in range(q + 1):
            mm = pe.matmul(self.ps_u[:, u % 2, j * self.width:(j + 1) * self.width],
                           self.p[:, self.p_row[u] + k, j * P:(j + 1) * P], value(s, head, k), start=(k == 0), stop=(k == q))
        if j == 3:
            mm.then_inc(self.value_done, 1)

    def tensor_step(self, pe, n, s, u, product, product_t, value, has_prev, has_next, first, extra=None):
        jobs = [((i + 0.3) / len(self.T_JOBS[u]), 1, i) for i in range(len(self.T_JOBS[u]))]
        nxt = (n, s, u + 1) if u + 1 < self.NU else (n + 1, 1 - s, 0)
        prev = (n, s, u - 1) if u > 0 else (n - 1, 1 - s, self.NU - 1)
        if nxt[2] or has_next:
            a = len(self.S_JOBS[nxt[2]])
            jobs += [((i + 0.2) / a * self.AHEAD, 0, i) for i in range(a)]
        if u > 0 or has_prev:
            jobs += [(self.BEHIND + (i + 0.5) / 4 * (1 - self.BEHIND), 2, i) for i in range(4)]
        if extra is not None:
            jobs.append((0.45, 3, 0))
        for _, kind, i in sorted(jobs):
            if kind == 0:
                self.scores(pe, *nxt, i, product, first and nxt[2] != 0)
            elif kind == 1:
                self.transposed(pe, n, s, u, i, product_t, first)
            elif kind == 2:
                self.values(pe, *prev, i, value, first)
            else:
                extra()

    def exponential(self, act, n, u, i, first):
        blk = self.UNITS[u][1]
        k, q0 = self.T_JOBS[u][i]
        job = self.t_off[u] + i
        if i == 0 and not (first and u < 2):
            act.wait_ge(self.value_done, self.NU * n + u - 1)
        act.wait_ge(self.trans_done, self.NTR * n + job + 1)
        cols = slice((q0 - 4 * blk) * P, 4 * P)
        act.activation(self.p[:, self.p_row[u] + k, cols], self.ps_t[:, job % self.SLOTS_T, cols],
                       ACT.Exp).then_inc(self.exp_done, 1)

    def maxima(self, v, n, u, first):
        head, blk = self.UNITS[u]
        halves = blk > 0
        if not (first and u < 2):
            v.wait_ge(self.diag_done, self.NU * n + u - 1)
        if halves and not (first and head == 0):
            v.wait_ge(self.joined, 2 * n + head)
        for i, (q, k0, k1) in enumerate(self.S_JOBS[u]):
            job = self.s_off[u] + i
            j = q - 4 * blk
            out = self.part[:, j, k0 // 4:k0 // 4 + 1] if halves else self.negmax[:, u % 2, j:j + 1]
            v.wait_ge(self.scores_done, self.NS * n + job + 1)
            v.tensor_reduce(out, self.ps_s[:, job % self.SLOTS_S, 0:(k1 - k0) * P], AX, ALU.max,
                            negate=True).then_inc(self.max_done, 1)
        v.wait_ge(self.max_done, self.NS * n + self.s_off[u + 1])
        if halves:
            v.tensor_reduce(self.negmax[:, u % 2, :], self.part[:], AX, ALU.min).then_inc(self.joined, 1)
            v.wait_ge(self.joined, 2 * n + head + 1)
        if not (first and u < 2):
            behind = self.t_off[u - 1] if u >= 2 else self.t_off[self.NU + u - 1] - self.NTR
            v.wait_ge(self.trans_done, self.NTR * n + behind)
        v.tensor_tensor(self.diag[:, u % 2], self.g.ident[:].unsqueeze(1).broadcast_to([P, 4, P]),
                        self.negmax[:, u % 2, :].unsqueeze(2).broadcast_to([P, 4, P]),
                        ALU.mult).then_inc(self.diag_done, 1)

    def result(self, v, n, u, out):
        head, blk = self.UNITS[u]
        v.wait_ge(self.value_done, self.NU * n + u + 1)
        v.tensor_copy(out(n, head, 4 * blk), self.ps_u[:, u % 2, 0:4 * self.width].rearrange("p (q c) -> p q c", q=4)
                      ).then_inc(self.u_read, 1)

    def vector_step(self, v, n, u, out, has_prev, has_next, first):
        if u >= 2:
            self.result(v, n, u - 2, out)
        elif has_prev:
            self.result(v, n - 1, self.NU + u - 2, out)
        if u + 1 < self.NU:
            self.maxima(v, n, u + 1, first)
        elif has_next:
            self.maxima(v, n + 1, 0, False)

    def vector_end(self, v, n, out):
        for u in (self.NU - 2, self.NU - 1):
            self.result(v, n, u, out)


class NarrowHeads(CausalHeads):

    WIDE = 64

    def __init__(self, b, g, width):
        super().__init__(b, g, width)
        self.ot = b.sb("ot", [P, 2, 4 * P])
        self.ps_o = b.ps("ps_o", [P, 4, P])
        self.back_done = b.sem("back_done")
        self.back_read = b.sem("back_read")

    def values(self, pe, n, s, u, j, value, first):
        head, blk = self.UNITS[u]
        if j == 0 and not (first and u < 2):
            pe.wait_ge(self.u_read, self.NU * n + u - 1)
        for k in range(j * (blk + 1), (j + 1) * (blk + 1)):
            q0 = self.T_JOBS[u][k][1] - 4 * blk
            pe.wait_ge(self.exp_done, self.NTR * n + self.t_off[u] + k + 1)
            mm = pe.matmul(self.ps_u[head * self.WIDE:(head + 1) * self.WIDE, u % 2, q0 * P:4 * P], value(s, head, k),
                           self.p[:, self.p_row[u] + k, q0 * P:4 * P], start=(k == 0), stop=(k == 4 * blk + 3))
        if j == 3:
            mm.then_inc(self.value_done, 1)

    def transpose_back(self, pe, n, blk, first):
        pe.wait_ge(self.u_read, self.NU * n + 2 + blk + 1)
        if not (first and blk == 0):
            pe.wait_ge(self.back_read, 2 * n + blk)
        for q in range(4):
            mm = pe.transpose(self.ps_o[:, q, :], self.ot[:, blk, q * P:(q + 1) * P], self.g.ident[:])
        mm.then_inc(self.back_done, 1)

    def keep(self, act, n, u, first):
        head, blk = self.UNITS[u]
        rows = slice(head * self.WIDE, (head + 1) * self.WIDE)
        act.wait_ge(self.value_done, self.NU * n + u + 1)
        if not first:
            act.wait_ge(self.back_done, 2 * n - 1 + blk)
        act.activation(self.ot[rows, blk, :], self.ps_u[rows, u % 2, :], ACT.Copy).then_inc(self.u_read, 1)

    def result(self, v, n, blk, out):
        v.wait_ge(self.back_done, 2 * n + blk + 1)
        v.tensor_copy(out(n, 4 * blk), self.ps_o[:].rearrange("p q (h c) -> p q h c", h=2)[:, :, :, 0:self.width]
                      ).then_inc(self.back_read, 1)

    def vector_step(self, v, n, u, out, has_prev, has_next, first):
        if u + 1 < self.NU:
            self.maxima(v, n, u + 1, first)
        elif has_next:
            self.maxima(v, n + 1, 0, False)
        if u < 2 and has_prev:
            self.result(v, n - 1, u, out)


def double_pairs(eng, body):
    for s in range(2):
        body(s, s, s == 0, False)
    with eng.Fori(1, NP // 2 - 1) as j:
        for s in range(2):
            body(2 * j + s, s, False, False)
    for s in range(2):
        body(NP - 2 + s, s, False, s == 1)


def latent_heads(nc, g, dram):
    with ExitStack() as ctx:
        b = Bufs(nc, ctx, "a2")
        att = CausalHeads(b, g, KL + 1)
        wq0 = b.sb("wq0", [P, P])
        wq1 = b.sb("wq1", [QR1, P])
        q_h = b.sb("q_h", [P, 2, 2, T], F32R)
        q_l = b.sb("q_l", [P, 2, 2, T], F32R)
        waiter = b.sb("waiter", [1, 1])
        ps_q = b.ps("ps_q", [P, 512])
        wq_loaded = b.sem("wq_loaded")
        qabs_done = b.sem("qabs_done")
        q_hi = b.sem("q_hi")
        q_lo = b.sem("q_lo")
        rope_hi = b.sem("rope_hi")
        rope_lo = b.sem("rope_lo")
        block = ctx.enter_context(nc.Block())

        @block.sync
        def _(sp):
            def load(p, first):
                if not first:
                    sp.wait_ge(qabs_done, 2 * p)
                sp.dma_start(wq0[:], g.wq[:, ds(p, 1), 0:P].squeeze(1)).then_inc(wq_loaded, 16)
                sp.dma_start(wq1[:], g.wq[0:QR1, ds(p, 1), P:2 * P].squeeze(1)).then_inc(wq_loaded, 16)
            load(0, True)
            load(1, False)
            sp.dma_start(g.w1_raw[:], dram["w1"]).then_inc(g.loaded_w1, 16)
            with sp.Fori(2, NP) as p:
                load(p, False)

        @block.tensor
        def _(pe):
            def product(pe, out, s, head, q, k0, k1, stop):
                return pe.matmul(out, q_h[:, s, head, q * P:(q + 1) * P], g.kt_h[:, head, k0 * P:k1 * P],
                                 start=True, stop=stop)

            def product_t(pe, out, s, head, k, q0, q1):
                keys, cols = slice(k * P, (k + 1) * P), slice(q0 * P, q1 * P)
                split3(pe, out, (g.kt_h[:, head, keys], g.kt_l[:, head, keys]),
                       (q_h[:, s, head, cols], q_l[:, s, head, cols]), True, False)

            def queries(p, half, first):
                if half == 0:
                    pe.wait_ge(wq_loaded, 32 * p + 32)
                if not (first and half == 0):
                    pe.wait_ge(q_lo, 4 * p + 2 * half)
                cols = slice(half * 512, (half + 1) * 512)
                pe.matmul(ps_q[:], wq0[:], g.qat0[:, cols], start=True, stop=False)
                pe.matmul(ps_q[:], wq1[:], g.qat1[:, cols], start=False, stop=True).then_inc(qabs_done, 1)

            def queries_ready(p):
                pe.wait_ge(q_hi, 4 * p + 4)
                pe.wait_ge(q_lo, 4 * p + 4)
                pe.wait_ge(rope_hi, 2 * p + 2)
                pe.wait_ge(rope_lo, 2 * p + 2)

            def pair(n, s, first, last):
                for u in range(att.NU):
                    if u == att.NU - 1 and not last:
                        queries_ready(n + 1)
                    extra = (lambda: queries(n + 1, u // 2, False)) if u % 2 == 0 and not last else None
                    att.tensor_step(pe, n, s, u, product, product_t, lambda s, head, k: g.vext[:, k, :],
                                    not first, not last, first, extra)

            for half in range(2):
                queries(0, half, True)
            pe.wait_ge(g.loaded_const, 16 * g.N_CONST)
            pe.wait_ge(att.ones_done, 1)
            queries_ready(0)
            for i in range(len(att.S_JOBS[0])):
                att.scores(pe, 0, 0, 0, i, product, True)
            double_pairs(pe, pair)
            for j in range(4):
                att.values(pe, NP - 1, 1, att.NU - 1, j, lambda s, head, k: g.vext[:, k, :], False)

        @block.scalar
        def _(act):
            def high(p, s, half, first):
                if half == 0 and not first:
                    act.wait_ge(att.trans_done, att.NTR * (p - 1))
                cols = slice(half * 512, (half + 1) * 512)
                act.wait_ge(qabs_done, 2 * p + half + 1)
                act.activation(q_h[KL:P, s, 0, cols], ps_q[KL:P, :], ACT.Copy,
                               scale=g.kvw_s[KL:P, 0:1]).then_inc(q_hi, 1)
                act.activation(q_h[0:KL, s, 1, cols], ps_q[0:KL, :], ACT.Copy,
                               scale=g.kvw_s[0:KL, 0:1]).then_inc(q_hi, 1)

            def pair(n, s, first, last):
                for u in range(att.NU):
                    jobs = len(att.T_JOBS[u])
                    for i in range(jobs):
                        if i == jobs - 2 and u % 2 == 0 and not last:
                            high(n + 1, 1 - s, u // 2, first)
                        att.exponential(act, n, u, i, first)
            act.wait_ge(g.kvw_scaled, 1)
            for half in range(2):
                high(0, 0, half, True)
            double_pairs(act, pair)

        @block.vector
        def _(v):
            def low(p, s, half):
                cols = slice(half * 512, (half + 1) * 512)
                v.wait_ge(q_hi, 4 * p + 2 * half + 2)
                v.scalar_tensor_tensor(q_l[KL:P, s, 0, cols], ps_q[KL:P, :], g.kvw_s[KL:P, 0:1],
                                       q_h[KL:P, s, 0, cols].bitcast(F32), ALU.mult, ALU.subtract).then_inc(q_lo, 1)
                v.scalar_tensor_tensor(q_l[0:KL, s, 1, cols], ps_q[0:KL, :], g.kvw_s[0:KL, 0:1],
                                       q_h[0:KL, s, 1, cols].bitcast(F32), ALU.mult, ALU.subtract).then_inc(q_lo, 1)

            def out(n, head, q0):
                return g.u[:, q0:q0 + 4, ds(2 * n + head, 1), :].squeeze(2)

            def pair(n, s, first, last):
                for u in range(att.NU):
                    att.vector_step(v, n, u, out, not first, not last, first)
                    if u % 2 == 0 and not last:
                        low(n + 1, 1 - s, u // 2)
            att.make_ones(v)
            for half in range(2):
                low(0, 0, half)
            att.maxima(v, 0, 0, True)
            double_pairs(v, pair)
            att.vector_end(v, NP - 1, out)

        @block.gpsimd
        def _(pool):
            def rope_rows(p, s, first):
                if not first:
                    pool.wait_ge(att.trans_done, att.NTR * (p - 1))
                    pool.tensor_tensor(waiter[:], g.neg_half[0:1, 0:1], g.neg_half[0:1, 0:1], ALU.add)
                for head, rows in ((0, slice(0, DR)), (1, slice(DR, P))):
                    pool.tensor_copy(q_h[rows, s, head, :], g.qrt[rows, ds(p, 1), :].squeeze(1)).then_inc(rope_hi, 1)
                pool.wait_ge(rope_hi, 2 * p + 2)
                pool.tensor_tensor(waiter[:], g.neg_half[0:1, 0:1], g.neg_half[0:1, 0:1], ALU.add)
                for head, rows in ((0, slice(0, DR)), (1, slice(DR, P))):
                    pool.tensor_tensor(q_l[rows, s, head, :], g.qrt[rows, ds(p, 1), :].squeeze(1),
                                       q_h[rows, s, head, :].bitcast(F32), ALU.subtract).then_inc(rope_lo, 1)
            for s in range(2):
                rope_rows(s, s, True)
            with pool.Fori(1, NP // 2) as j:
                for s in range(2):
                    rope_rows(2 * j + s, s, False)


def latent_output(nc, g):
    with ExitStack() as ctx:
        b = Bufs(nc, ctx, "a3")
        rden = b.sb("rden", [P, H])
        un = b.sb("un", [P, H * KL])
        ut = b.sb("ut", [P, NP, P])
        ps_t = b.ps("ps_t", [P, 2, 512])
        ps_y = b.ps("ps_y", [P, 512])
        rden_done = b.sem("rden_done")
        un_done = b.sem("un_done")
        un_t_done = b.sem("un_t_done")
        ut_by_scalar = b.sem("ut_by_scalar")
        ut_by_vector = b.sem("ut_by_vector")
        y_done = b.sem("y_done")
        y_added = b.sem("y_added")
        block = ctx.enter_context(nc.Block())

        @block.tensor
        def _(pe):
            def step(i, one, two, least):
                if one:
                    pe.wait_ge(un_done, i + 1)
                    if least >= 1:
                        pe.wait_ge(ut_by_scalar, i)
                        pe.wait_ge(ut_by_vector, i)
                    for c in range(NP):
                        mm = pe.transpose(ps_t[:, c // 4, (c % 4) * P:(c % 4 + 1) * P], un[:, c * P:(c + 1) * P],
                                          g.ident[:])
                    mm.then_inc(un_t_done, 1)
                    pe.wait_ge(ut_by_scalar, i + 1)
                    pe.wait_ge(ut_by_vector, i + 1)
                    if least >= 1:
                        pe.wait_ge(y_added, i)
                    for c in range(NP):
                        mm = pe.matmul(ps_y[:, 0:D], ut[:, c, :], g.wvo[:, c, :], start=(c == 0), stop=(c == NP - 1))
                    mm.then_inc(y_done, 1)
            staged(2, pe, step)

        @block.scalar
        def _(act):
            def step(i, one, two, least):
                if one:
                    act.wait_ge(un_t_done, i + 1)
                    if least >= 1:
                        act.wait_ge(y_done, i)
                    act.activation(ut[:, 0:4, :], ps_t[:, 0, :].rearrange("p (k c) -> p k c", c=P),
                                   ACT.Copy).then_inc(ut_by_scalar, 1)
            staged(2, act, step)

        @block.vector
        def _(v):
            def step(i, one, two, least):
                if one:
                    v.reciprocal(rden[:], g.u[:, ds(i, 1), :, KL].squeeze(1)).then_inc(rden_done, 1)
                    v.wait_ge(rden_done, i + 1)
                    if least >= 1:
                        v.wait_ge(un_t_done, i)
                    v.tensor_tensor(un[:].rearrange("p (h c) -> p h c", c=KL), g.u[:, ds(i, 1), :, 0:KL].squeeze(1),
                                    rden[:].unsqueeze(2).broadcast_to([P, H, KL]), ALU.mult).then_inc(un_done, 1)
                if two:
                    t = i - 1
                    v.wait_ge(y_done, t + 1)
                    v.tensor_tensor(g.X[:, ds(t * D, D)], g.X[:, ds(t * D, D)], ps_y[:, 0:D],
                                    ALU.add).then_inc(y_added, 1)
                if one:
                    v.wait_ge(un_t_done, i + 1)
                    v.tensor_copy(ut[:, 4:8, :], ps_t[:, 1, :].rearrange("p (k c) -> p k c", c=P))\
                        .then_inc(ut_by_vector, 1)
            staged(2, v, step)


def split_expert_weights(nc, g, dram):
    with ExitStack() as ctx:
        b = Bufs(nc, ctx, "ws")
        w1_hi = b.sem("w1_hi")
        w1_lo = b.sem("w1_lo")
        block = ctx.enter_context(nc.Block())
        N = 4
        CH = W1_N // N

        @block.sync
        def _(sp):
            sp.dma_start(g.w2[:, 0:NF - 1, :], dram["w2"][0:(NF - 1) * P, :]
                         .rearrange("(k p) d -> p k d", p=P)).then_inc(g.loaded_w2, 16)
            sp.dma_start(g.w2[0:FTAIL, NF - 1, :], dram["w2"][(NF - 1) * P:FH, :]).then_inc(g.loaded_w2, 16)

        @block.scalar
        def _(act):
            act.wait_ge(g.loaded_w1, 16)
            for n in range(N):
                act.activation(g.w1_h[:, :, n * CH:(n + 1) * CH], g.w1_raw[:, :, n * CH:(n + 1) * CH],
                               ACT.Copy).then_inc(w1_hi, 1)

        @block.vector
        def _(v):
            for n in range(N):
                cols = slice(n * CH, (n + 1) * CH)
                v.wait_ge(w1_hi, n + 1)
                v.tensor_tensor(g.w1_l[:, :, cols], g.w1_raw[:, :, cols], g.w1_h[:, :, cols].bitcast(F32),
                                ALU.subtract).then_inc(w1_lo, 1)


def experts(nc, g, tag):
    NBLK = NE + 1
    with ExitStack() as ctx:
        b = Bufs(nc, ctx, tag)
        ln = LayerNorm(b, g)
        xt_h = b.sb("xt_h", [P, KD * P], F32R)
        xt_l = b.sb("xt_l", [P, KD * P], F32R)
        silu = b.sb("silu", [P, 2, FI])
        hid = b.sb("hid", [P, FH])
        hid_t = b.sb("hid_t", [P, NF, P])
        logits = b.sb("logits", [P, NE])
        top = b.sb("top", [P, 8])
        top_at = b.sb("top_at", [P, 8], mybir.dt.uint32)
        top_atf = b.sb("top_atf", [P, 2])
        neg_top = b.sb("neg_top", [P, 1])
        expert_no = b.sb("expert_no", [P, NE])
        expo = b.sb("expo", [P, NE])
        expo_sum = b.sb("expo_sum", [P, 1])
        first_w = b.sb("first_w", [P, NE])
        second_w = b.sb("second_w", [P, NE])
        both_w = b.sb("both_w", [P, NE])
        pair_sum = b.sb("pair_sum", [P, 1])
        den = b.sb("den", [P, 1])
        rden = b.sb("rden", [P, 1])
        comb = b.sb("comb", [P, NE])
        ps_b = b.ps("ps_b", [P, 4, 512])
        ps_x = b.ps("ps_x", [P, 512])
        ps_h = b.ps("ps_h", [P, 2, 512])
        ps_y = b.ps("ps_y", [P, 512])
        numbered = b.sem("numbered")
        xt_hi = b.sem("xt_hi")
        xt_lo = b.sem("xt_lo")
        block_done = b.sem("block_done")
        silu_done = b.sem("silu_done")
        hid_done = b.sem("hid_done")
        hid_t_done = b.sem("hid_t_done")
        even_copied = b.sem("even_copied")
        odd_copied = b.sem("odd_copied")
        y_done = b.sem("y_done")
        y_added = b.sem("y_added")
        logits_done = b.sem("logits_done")
        router = b.sem("router")
        expo_done = b.sem("expo_done")
        den_done = b.sem("den_done")
        comb_done = b.sem("comb_done")
        ROUTER = 8
        block = ctx.enter_context(nc.Block())
        col = lambda k: 0 if k == 0 else BLK + NE + (k - 1) * BLK
        wid = lambda k: BLK + NE if k == 0 else BLK
        groups = [(0, 4), (4, 8), (8, 12), (12, NF)]

        def slot_before(k, slots):
            if k >= slots:
                return k - slots
            return max(j for j in range(NBLK) if j % slots == k % slots) - NBLK

        def tiles(eng, step):
            step(0, True, False)
            with eng.Fori(1, NT - 1) as t:
                step(t, False, False)
            step(NT - 1, False, True)

        @block.tensor
        def _(pe):
            def transposed_input(t, first):
                if not first:
                    pe.wait_ge(xt_hi, t)
                    pe.wait_ge(xt_lo, t)
                ln.tensor_transpose(pe, ps_x, t)

            def transposes(t, n, first):
                k0, k1 = groups[n]
                need = min(NBLK, -(-k1 * P // FI))
                if n < 3:
                    pe.wait_ge(hid_done, NBLK * t + need)
                if n == 2:
                    pe.wait_ge(even_copied, 2 * t + 1)
                    pe.wait_ge(odd_copied, 2 * t + 1)
                elif n < 2 and not first:
                    pe.wait_ge((even_copied, odd_copied)[n % 2], 2 * t)
                for k in range(k0, k1):
                    m = min(P, FH - k * P)
                    mm = pe.transpose(ps_h[0:m, n % 2, (k - k0) * P:(k - k0 + 1) * P], hid[:, k * P:k * P + m], g.ident[:])
                mm.then_inc(hid_t_done, 1)

            def outputs(t, k0, k1):
                for k in range(k0, k1):
                    m = min(P, FH - k * P)
                    mm = pe.matmul(ps_y[:, 0:D], hid_t[0:m, k, :], g.w2[0:m, k, :], start=(k == 0), stop=(k == NF - 1))
                return mm

            def step(t, first, last):
                pe.wait_ge(xt_hi, t + 1)
                pe.wait_ge(xt_lo, t + 1)
                for k in range(NBLK):
                    if not (first and k < 4):
                        pe.wait_ge(hid_done, NBLK * t + slot_before(k, 4) + 1)
                    for c in range(KD):
                        cs, ws = slice(c * P, (c + 1) * P), slice(col(k), col(k) + wid(k))
                        mm = split3(pe, ps_b[:, k % 4, 0:wid(k)], (xt_h[:, cs], xt_l[:, cs]),
                                    (g.w1_h[:, c, ws], g.w1_l[:, c, ws]), c == 0, c == KD - 1)
                    mm.then_inc(block_done, 1)
                    if k == 4:
                        transposes(t, 0, first)
                    if k == 7:
                        transposes(t, 1, first)
                if not last:
                    transposed_input(t + 1, False)
                if first:
                    pe.wait_ge(g.loaded_w2, 32)
                if not first:
                    pe.wait_ge(y_added, t)
                pe.wait_ge(even_copied, 2 * t + 1)
                outputs(t, 0, 4)
                transposes(t, 2, first)
                transposes(t, 3, first)
                pe.wait_ge(odd_copied, 2 * t + 1)
                outputs(t, 4, 8)
                pe.wait_ge(even_copied, 2 * t + 2)
                pe.wait_ge(odd_copied, 2 * t + 2)
                outputs(t, 8, NF).then_inc(y_done, 1)
            transposed_input(0, True)
            tiles(pe, step)

        @block.scalar
        def _(act):
            def transposed_high(t, first):
                act.wait_ge(ln.xn_read, t + 1)
                if not first:
                    act.wait_ge(block_done, NBLK * t)
                act.activation(xt_h[:], ps_x[:, 0:KD * P], ACT.Copy).then_inc(xt_hi, 1)

            def copy_group(t, n, first):
                k0, k1 = groups[n]
                act.wait_ge(hid_t_done, 4 * t + n + 1)
                if not first:
                    act.wait_ge(y_done, t)
                act.activation(hid_t[:, k0:k1, :], ps_h[:, 0, :].rearrange("p (k c) -> p k c", c=P),
                               ACT.Copy).then_inc(even_copied, 1)

            def step(t, first, last):
                for k in range(NBLK):
                    act.wait_ge(block_done, NBLK * t + k + 1)
                    if not (first and k < 2):
                        act.wait_ge(hid_done, NBLK * t + slot_before(k, 2) + 1)
                    act.activation(silu[:, k % 2, :], ps_b[:, k % 4, 0:FI], ACT.Silu).then_inc(silu_done, 1)
                    if k == 0:
                        act.wait_ge(router, ROUTER * t + 3)
                        if not first:
                            act.wait_ge(comb_done, t)
                        act.activation(expo[:], logits[:], ACT.Exp, bias=neg_top[:, 0:1],
                                       accum_out=expo_sum[:]).then_inc(expo_done, 1)
                    if k == 4:
                        copy_group(t, 0, first)
                if not last:
                    transposed_high(t + 1, False)
                copy_group(t, 2, first)
            transposed_high(0, True)
            tiles(act, step)

        @block.vector
        def _(v):
            def transposed_low(t, first):
                v.wait_ge(xt_hi, t + 1)
                v.tensor_tensor(xt_l[:], ps_x[:, 0:KD * P], xt_h[:].bitcast(F32), ALU.subtract).then_inc(xt_lo, 1)

            def gated(t, k, first):
                v.wait_ge(silu_done, NBLK * t + k + 1)
                if k == 0 and not first:
                    v.wait_ge(hid_t_done, 4 * t)
                out, up = hid[:, k * FI:(k + 1) * FI], ps_b[:, k % 4, FI:BLK]
                if k == 0:
                    v.tensor_tensor(out, up, silu[:, 0, :], ALU.mult).then_inc(hid_done, 1)
                else:
                    if k == 1:
                        v.wait_ge(comb_done, t + 1)
                    v.scalar_tensor_tensor(out, up, comb[:, k - 1:k], silu[:, k % 2, :], ALU.mult,
                                           ALU.mult).then_inc(hid_done, 1)

            def copy_group(t, n, first):
                k0, k1 = groups[n]
                m = min(P, FH - k0 * P)
                v.wait_ge(hid_t_done, 4 * t + n + 1)
                if not first:
                    v.wait_ge(y_done, t)
                v.tensor_copy(hid_t[0:m, k0:k1, :], ps_h[0:m, 1, 0:(k1 - k0) * P].rearrange("p (k c) -> p k c", c=P))\
                    .then_inc(odd_copied, 1)

            def route(t):
                def after(n):
                    v.wait_ge(router, ROUTER * t + n)
                v.wait_ge(logits_done, t + 1)
                v.memset(ln.waiter[:], 0.0)
                v.max(top[:], logits[:]).then_inc(router, 1)
                after(1)
                v.memset(ln.waiter[:], 0.0)
                v.max_index(top_at[:], top[:], logits[:]).then_inc(router, 1)
                v.tensor_scalar(neg_top[:], top[:, 0:1], -1.0, None, ALU.mult).then_inc(router, 1)
                after(2)
                v.tensor_copy(top_atf[:], top_at[:, 0:2]).then_inc(router, 1)
                after(4)
                v.wait_ge(expo_done, t + 1)
                v.scalar_tensor_tensor(first_w[:], expert_no[:], top_atf[:, 0:1], expo[:], ALU.is_equal,
                                       ALU.mult).then_inc(router, 1)
                v.scalar_tensor_tensor(second_w[:], expert_no[:], top_atf[:, 1:2], expo[:], ALU.is_equal,
                                       ALU.mult).then_inc(router, 1)
                after(6)
                v.tensor_tensor(both_w[:], first_w[:], second_w[:], ALU.add).then_inc(router, 1)
                after(7)
                v.tensor_reduce(pair_sum[:], both_w[:], AX, ALU.add).then_inc(router, 1)
                after(8)
                v.scalar_tensor_tensor(den[:], expo_sum[:], 1e-20, pair_sum[:], ALU.mult, ALU.add).then_inc(den_done, 1)
                v.wait_ge(den_done, 2 * t + 1)
                v.reciprocal(rden[:], den[:]).then_inc(den_done, 1)
                v.wait_ge(den_done, 2 * t + 2)
                v.tensor_scalar(comb[:], both_w[:], rden[:, 0:1], None, ALU.mult).then_inc(comb_done, 1)

            def step(t, first, last):
                v.wait_ge(block_done, NBLK * t + 1)
                v.wait_ge(silu_done, NBLK * t + 1)
                v.tensor_copy(logits[:], ps_b[:, 0, BLK:BLK + NE]).then_inc(logits_done, 1)
                gated(t, 0, first)
                route(t)
                for k in range(1, NBLK):
                    gated(t, k, first)
                    if not last and k == 2:
                        ln.vector_stats(v, t + 1, t + 1)
                    if not last and k == 4:
                        ln.vector_scale(v, t + 1, t + 1, False)
                    if k == 7:
                        copy_group(t, 1, first)
                if not last:
                    transposed_low(t + 1, False)
                copy_group(t, 3, first)
                v.wait_ge(y_done, t + 1)
                v.tensor_tensor(g.X[:, ds(t * D, D)], g.X[:, ds(t * D, D)], ps_y[:, 0:D], ALU.add).then_inc(y_added, 1)
            v.wait_ge(numbered, 1)
            ln.vector_stats(v, 0, 0)
            ln.vector_scale(v, 0, 0, True)
            transposed_low(0, True)
            tiles(v, step)

        @block.gpsimd
        def _(pool):
            pool.iota(expert_no[:], pattern=[[1, NE]], base=0, channel_multiplier=0,
                      allow_small_or_imprecise_dtypes=True).then_inc(numbered, 1)
            ln.gpsimd_power(pool, 0)
            with pool.Fori(1, NT) as t:
                ln.gpsimd_power(pool, t)


def plain_attention(nc, g, dram):
    with ExitStack() as ctx:
        b = Bufs(nc, ctx, "b")
        xt_h = b.sb("xt_h", [P, KD, T], F32R)
        xt_l = b.sb("xt_l", [P, KD, T], F32R)
        wqk_h = b.sb("wqk_h", [P, KD, D], F32R)
        wqk_l = b.sb("wqk_l", [P, KD, D], F32R)
        wvo_h = b.sb("wvo_h", [P, KD, D], F32R)
        wvo_l = b.sb("wvo_l", [P, KD, D], F32R)
        vo = b.sb("vo", [P, NT, D])
        keys_and_values(nc, g, dram, xt_h, xt_l, wqk_h, wqk_l, wvo_h, wvo_l, vo)
        plain_queries(nc, g, xt_h, xt_l, wqk_h, wqk_l, vo)


def keys_and_values(nc, g, dram, xt_h, xt_l, wqk_h, wqk_l, wvo_h, wvo_l, vo):
    with ExitStack() as ctx:
        b = Bufs(nc, ctx, "bk")
        ln = LayerNorm(b, g)
        w = b.sb("w", [P, 4, KD, D])
        xs_h = b.sb("xs_h", [P, KD, P], F32R)
        xs_l = b.sb("xs_l", [P, KD, P], F32R)
        ps_w = b.ps("ps_w", [P, 2, 512])
        ps_x = b.ps("ps_x", [P, 512])
        ps_v = b.ps("ps_v", [P, 512])
        w_loaded = b.sem("w_loaded")
        w_done = b.sem("w_done")
        w_hi = b.sem("w_hi")
        w_lo = b.sem("w_lo")
        xt_hi = b.sem("xt_hi")
        xt_lo = b.sem("xt_lo")
        xt_kept = b.sem("xt_kept")
        vo_done = b.sem("vo_done")
        vo_copied = b.sem("vo_copied")
        block = ctx.enter_context(nc.Block())

        @block.sync
        def _(sp):
            sp.dma_start(w[:], dram["wb"]).then_inc(w_loaded, 16)

        @block.tensor
        def _(pe):
            pe.wait_ge(w_loaded, 16)
            for n, (left, right) in enumerate(((0, 1), (2, 3))):
                for m in range(KD):
                    for c in range(KD):
                        mm = pe.matmul(ps_w[:, n, m * D:(m + 1) * D], w[:, left, c, m * P:(m + 1) * P],
                                       w[:, right, c, :], start=(c == 0), stop=(c == KD - 1))
                mm.then_inc(w_done, 1)

            def step(t, one, least):
                if least >= 1:
                    pe.wait_ge(xt_lo, t)
                ln.tensor_transpose(pe, ps_x, t)
                pe.wait_ge(xt_hi, t + 1)
                pe.wait_ge(xt_lo, t + 1)
                if least == 0:
                    pe.wait_ge(w_lo, 2)
                else:
                    pe.wait_ge(vo_copied, t)
                for c in range(KD):
                    mm = split3(pe, ps_v[:, 0:D], (xs_h[:, c, :], xs_l[:, c, :]), (wvo_h[:, c, :], wvo_l[:, c, :]),
                                c == 0, c == KD - 1)
                mm.then_inc(vo_done, 1)
            staged(1, pe, step)

        @block.scalar
        def _(act):
            for n, (hi, scale) in enumerate(((wqk_h, D ** -0.5), (wvo_h, 1.0))):
                act.wait_ge(w_done, n + 1)
                act.activation(hi[:], ps_w[:, n, :].rearrange("p (m c) -> p m c", m=KD), ACT.Copy,
                               scale=scale).then_inc(w_hi, 1)

            def step(t, one, least):
                act.wait_ge(ln.xn_read, t + 1)
                if least >= 1:
                    act.wait_ge(vo_done, t)
                    act.wait_ge(xt_kept, 2 * t)
                act.activation(xs_h[:], ps_x[:, 0:KD * P].rearrange("p (m c) -> p m c", m=KD),
                               ACT.Copy).then_inc(xt_hi, 1)
                act.wait_ge(vo_done, t + 1)
                act.activation(vo[:, ds(t, 1), :].squeeze(1), ps_v[:, 0:D], ACT.Copy).then_inc(vo_copied, 1)
            staged(1, act, step)

        @block.vector
        def _(v):
            ln.vector_stats(v, 0, 0)
            ln.vector_scale(v, 0, 0, True)
            for n, (hi, lo, scale) in enumerate(((wqk_h, wqk_l, D ** -0.5), (wvo_h, wvo_l, 1.0))):
                v.wait_ge(w_hi, n + 1)
                v.scalar_tensor_tensor(lo[:], ps_w[:, n, :].rearrange("p (m c) -> p m c", m=KD), scale,
                                       hi[:].bitcast(F32), ALU.mult, ALU.subtract).then_inc(w_lo, 1)

            def low(t):
                v.wait_ge(xt_hi, t + 1)
                v.tensor_tensor(xs_l[:], ps_x[:, 0:KD * P].rearrange("p (m c) -> p m c", m=KD),
                                xs_h[:].bitcast(F32), ALU.subtract).then_inc(xt_lo, 1)

            def step(t):
                ln.vector_stats(v, t + 1, t + 1)
                low(t)
                ln.vector_scale(v, t + 1, t + 1, False)
            step(0)
            with v.Fori(1, NT - 1) as t:
                step(t)
            low(NT - 1)

        @block.gpsimd
        def _(pool):
            def step(t, one, least):
                if least == 0:
                    ln.gpsimd_power(pool, 0)
                    ln.gpsimd_power(pool, 1)
                pool.wait_ge(xt_lo, t + 1)
                pool.tensor_copy(xt_h[:, :, ds(t * P, P)], xs_h[:]).then_inc(xt_kept, 1)
                pool.tensor_copy(xt_l[:, :, ds(t * P, P)], xs_l[:]).then_inc(xt_kept, 1)
            step(0, True, 0)
            with pool.Fori(1, NT - 1) as t:
                ln.gpsimd_power(pool, t + 1)
                step(t, True, 1)
            step(NT - 1, True, 1)


def plain_queries(nc, g, xt_h, xt_l, wqk_h, wqk_l, vo):
    with ExitStack() as ctx:
        b = Bufs(nc, ctx, "bq")
        qt_h = b.sb("qt_h", [P, KD, P], F32R)
        qt_l = b.sb("qt_l", [P, KD, P], F32R)
        negmax = b.sb("negmax", [P, 1])
        wsum = b.sb("wsum", [P, 1])
        rsum = b.sb("rsum", [P, 1])
        p = b.sb("p", [P, T])
        pt = b.sb("pt", [P, NT, P])
        ps_q = b.ps("ps_q", [P, 512])
        ps_s = b.ps("ps_s", [P, 2, 512])
        ps_t = b.ps("ps_t", [P, 2, 512])
        ps_y = b.ps("ps_y", [P, 512])
        q_done = b.sem("q_done")
        q_hi = b.sem("q_hi")
        q_lo = b.sem("q_lo")
        scores_done = b.sem("scores_done")
        max_done = b.sem("max_done")
        exp_done = b.sem("exp_done")
        rsum_done = b.sem("rsum_done")
        p_t_done = b.sem("p_t_done")
        pt_by_scalar = b.sem("pt_by_scalar")
        pt_by_vector = b.sem("pt_by_vector")
        y_done = b.sem("y_done")
        y_added = b.sem("y_added")
        block = ctx.enter_context(nc.Block())

        @block.tensor
        def _(pe):
            def step(i, one, two, least):
                if one:
                    if least >= 1:
                        pe.wait_ge(q_lo, i)
                    for m in range(KD):
                        for c in range(KD):
                            tokens = ds(i * P, P)
                            mm = split3(pe, ps_q[:, m * P:(m + 1) * P],
                                        (wqk_h[:, c, m * P:(m + 1) * P], wqk_l[:, c, m * P:(m + 1) * P]),
                                        (xt_h[:, c, tokens], xt_l[:, c, tokens]), c == 0, c == KD - 1)
                    mm.then_inc(q_done, 1)
                if two:
                    t = i - 1
                    pe.wait_ge(exp_done, t + 1)
                    if least >= 2:
                        pe.wait_ge(pt_by_scalar, t)
                        pe.wait_ge(pt_by_vector, t)
                    for k in range(NT):
                        mm = pe.transpose(ps_t[:, k // 4, (k % 4) * P:(k % 4 + 1) * P], p[:, k * P:(k + 1) * P],
                                          g.ident[:])
                    mm.then_inc(p_t_done, 1)
                if one:
                    pe.wait_ge(q_hi, i + 1)
                    pe.wait_ge(q_lo, i + 1)
                    for n in range(2):
                        cols = slice(n * 512, (n + 1) * 512)
                        for c in range(KD):
                            mm = split3(pe, ps_s[:, n, :], (qt_h[:, c, :], qt_l[:, c, :]),
                                        (xt_h[:, c, cols], xt_l[:, c, cols]), c == 0, c == KD - 1)
                    mm.then_inc(scores_done, 1)
                if two:
                    t = i - 1
                    pe.wait_ge(pt_by_scalar, t + 1)
                    pe.wait_ge(pt_by_vector, t + 1)
                    if least >= 2:
                        pe.wait_ge(y_added, t)
                    for k in range(NT):
                        mm = pe.matmul(ps_y[:, 0:D], pt[:, k, :], vo[:, k, :], start=(k == 0), stop=(k == NT - 1))
                    mm.then_inc(y_done, 1)
            staged(2, pe, step)

        @block.scalar
        def _(act):
            def step(i, one, two, least):
                if one:
                    act.wait_ge(q_done, i + 1)
                    if least >= 1:
                        act.wait_ge(scores_done, i)
                    act.activation(qt_h[:], ps_q[:, 0:KD * P].rearrange("p (m c) -> p m c", m=KD),
                                   ACT.Copy).then_inc(q_hi, 1)
                if two:
                    t = i - 1
                    act.wait_ge(p_t_done, t + 1)
                    if least >= 2:
                        act.wait_ge(y_done, t)
                    act.activation(pt[:, 0:4, :], ps_t[:, 0, :].rearrange("p (k c) -> p k c", c=P),
                                   ACT.Copy).then_inc(pt_by_scalar, 1)
                if one:
                    act.wait_ge(max_done, i + 1)
                    if least >= 1:
                        act.wait_ge(rsum_done, i)
                    act.activation(p[:], ps_s[:].rearrange("p a c -> p (a c)"), ACT.Exp, bias=negmax[:, 0:1],
                                   accum_out=wsum[:]).then_inc(exp_done, 1)
            staged(2, act, step)

        @block.vector
        def _(v):
            def step(i, one, two, least):
                if one:
                    v.wait_ge(q_hi, i + 1)
                    v.tensor_tensor(qt_l[:], ps_q[:, 0:KD * P].rearrange("p (m c) -> p m c", m=KD),
                                    qt_h[:].bitcast(F32), ALU.subtract).then_inc(q_lo, 1)
                if two:
                    t = i - 1
                    v.wait_ge(p_t_done, t + 1)
                    if least >= 2:
                        v.wait_ge(y_done, t)
                    v.tensor_copy(pt[:, 4:8, :], ps_t[:, 1, :].rearrange("p (k c) -> p k c", c=P))\
                        .then_inc(pt_by_vector, 1)
                if one:
                    v.wait_ge(scores_done, i + 1)
                    v.tensor_reduce(negmax[:], ps_s[:].rearrange("p a c -> p (a c)"), AX, ALU.max,
                                    negate=True).then_inc(max_done, 1)
                if two:
                    t = i - 1
                    v.wait_ge(y_done, t + 1)
                    v.scalar_tensor_tensor(g.X[:, ds(t * D, D)], ps_y[:, 0:D], rsum[:, 0:1], g.X[:, ds(t * D, D)],
                                           ALU.mult, ALU.add).then_inc(y_added, 1)
                if one:
                    v.wait_ge(exp_done, i + 1)
                    if least >= 1:
                        v.wait_ge(y_added, i)
                    v.reciprocal(rsum[:], wsum[:]).then_inc(rsum_done, 1)
            staged(2, v, step)


def experts_and_middle(nc, g, dram):
    with ExitStack() as ctx:
        b = Bufs(nc, ctx, "m")
        g.w1_h = b.sb("w1_h", [P, KD, W1_N], F32R)
        g.w1_l = b.sb("w1_l", [P, KD, W1_N], F32R)
        g.w2 = b.sb("w2", [P, NF, D])
        split_expert_weights(nc, g, dram)
        experts(nc, g, "m1")
        plain_attention(nc, g, dram)
        experts(nc, g, "m2")


def heads_projections(nc, g, dram):
    with ExitStack() as ctx:
        b = Bufs(nc, ctx, "c1")
        ln = LayerNorm(b, g)
        w = b.sb("w", [P, KD, 3 * D])
        w_h = b.sb("w_h", [P, KD, 3 * D], F32R)
        w_l = b.sb("w_l", [P, KD, 3 * D], F32R)
        xt_h = b.sb("xt_h", [P, KD * P], F32R)
        xt_l = b.sb("xt_l", [P, KD * P], F32R)
        st = b.sb("st", [P, 2, H, 4, HD], F32R)
        waiter = b.sb("waiter", [1, 1])
        ps_x = b.ps("ps_x", [P, 512])
        ps_qk = b.ps("ps_qk", [P, 512])
        ps_v = b.ps("ps_v", [P, 512])
        ps_t = b.ps("ps_t", [P, 4, 512])
        w_loaded = b.sem("w_loaded")
        w_hi = b.sem("w_hi")
        w_lo = b.sem("w_lo")
        xt_hi = b.sem("xt_hi")
        xt_lo = b.sem("xt_lo")
        qk_done = b.sem("qk_done")
        v_done = b.sem("v_done")
        st_hi = b.sem("st_hi")
        st_lo = b.sem("st_lo")
        v_kept = b.sem("v_kept")
        st_copied = b.sem("st_copied")
        st_t_done = b.sem("st_t_done")
        by_scalar = b.sem("by_scalar")
        by_vector = b.sem("by_vector")
        block = ctx.enter_context(nc.Block())
        qk = ps_qk[:].rearrange("p (a h c) -> p a h c", a=2, c=HD)
        HIGH = ((0, 0), (1, 0))
        HIGH2 = ((0, 1), (1, 2))
        LOW = ((0, 2), (1, 1))
        LOW2 = ((0, 3), (1, 3))
        SCALE = (HD ** -0.5, 1.0)

        @block.sync
        def _(sp):
            sp.dma_start(w[:], dram["wqkv"]).then_inc(w_loaded, 16)

        @block.tensor
        def _(pe):
            def step(i, one, two, least):
                if one:
                    if least >= 1:
                        pe.wait_ge(xt_lo, i)
                    ln.tensor_transpose(pe, ps_x, i)
                if two:
                    t = i - 1
                    pe.wait_ge(st_lo, 2 * t + 2)
                    pe.wait_ge(st_copied, 2 * t + 2)
                    if least >= 2:
                        pe.wait_ge(by_scalar, 2 * t)
                        pe.wait_ge(by_vector, 2 * t)
                    flat = st[:].rearrange("p a h s c -> p (a h s c)").bitcast(F32)
                    for c in range(2 * NP):
                        mm = pe.transpose(ps_t[:, c // 4, (c % 4) * P:(c % 4 + 1) * P], flat[:, c * P:(c + 1) * P],
                                          g.ident[:])
                    mm.then_inc(st_t_done, 1)
                if one:
                    pe.wait_ge(xt_hi, i + 1)
                    pe.wait_ge(xt_lo, i + 1)
                    if least == 0:
                        pe.wait_ge(w_lo, 1)
                    else:
                        pe.wait_ge(st_lo, 2 * i)
                        pe.wait_ge(v_kept, i)
                    for out, cols, sem in ((ps_qk[:], slice(0, 2 * D), qk_done), (ps_v[:, 0:D], slice(2 * D, 3 * D), v_done)):
                        for c in range(KD):
                            cs = slice(c * P, (c + 1) * P)
                            mm = split3(pe, out, (xt_h[:, cs], xt_l[:, cs]), (w_h[:, c, cols], w_l[:, c, cols]),
                                        c == 0, c == KD - 1)
                        mm.then_inc(sem, 1)
            staged(2, pe, step)

        @block.scalar
        def _(act):
            act.wait_ge(w_loaded, 16)
            act.activation(w_h[:], w[:], ACT.Copy).then_inc(w_hi, 1)

            def step(i, one, two, least):
                if one:
                    act.wait_ge(ln.xn_read, i + 1)
                    if least >= 1:
                        act.wait_ge(v_done, i)
                    act.activation(xt_h[:], ps_x[:, 0:KD * P], ACT.Copy).then_inc(xt_hi, 1)
                if two:
                    t = i - 1
                    act.wait_ge(st_t_done, t + 1)
                    for n in range(2):
                        act.activation(g.qks[:, 4 * n:4 * n + 4, ds(t * P, P)],
                                       ps_t[:, n, :].rearrange("p (k c) -> p k c", c=P), ACT.Copy).then_inc(by_scalar, 1)
                if one:
                    act.wait_ge(qk_done, i + 1)
                    if least >= 1:
                        act.wait_ge(st_t_done, i)
                    for n, (a, s) in enumerate(HIGH):
                        act.activation(st[:, a, :, s, :], qk[:, a], ACT.Copy, scale=SCALE[a]).then_inc(st_hi, 1)
                    act.wait_ge(v_done, i + 1)
                    act.activation(g.vh[:, :, ds(i, 1), :, 0:HD].squeeze(2), ps_v[:, 0:D].rearrange("p (n h c) -> p n h c", h=2, c=HD),
                                   ACT.Copy).then_inc(v_kept, 1)
            staged(2, act, step)

        @block.vector
        def _(v):
            ln.vector_stats(v, 0, 0)
            ln.vector_scale(v, 0, 0, True)
            v.wait_ge(w_hi, 1)
            v.tensor_tensor(w_l[:], w[:], w_h[:].bitcast(F32), ALU.subtract).then_inc(w_lo, 1)

            def low(i):
                v.wait_ge(xt_hi, i + 1)
                v.tensor_tensor(xt_l[:], ps_x[:, 0:KD * P], xt_h[:].bitcast(F32), ALU.subtract).then_inc(xt_lo, 1)

            def copies(t):
                v.wait_ge(st_t_done, t + 1)
                for n in range(2, 4):
                    v.tensor_copy(g.qks[:, 4 * n:4 * n + 4, ds(t * P, P)],
                                  ps_t[:, n, :].rearrange("p (k c) -> p k c", c=P)).then_inc(by_vector, 1)

            def stack_low(i):
                v.wait_ge(st_hi, 2 * i + 2)
                for (a, s), (_, s_hi) in zip(LOW, HIGH):
                    v.scalar_tensor_tensor(st[:, a, :, s, :], qk[:, a], SCALE[a], st[:, a, :, s_hi, :].bitcast(F32),
                                           ALU.mult, ALU.subtract).then_inc(st_lo, 1)

            def step(i, one, two, least):
                if one:
                    low(i)
                    if least < NT - 1:
                        ln.vector_stats(v, i + 1, i + 1)
                if two:
                    copies(i - 1)
                if one:
                    if least < NT - 1:
                        ln.vector_scale(v, i + 1, i + 1, False)
                    stack_low(i)
            step(0, True, False, 0)
            with v.Fori(1, NT - 1) as i:
                step(i, True, True, 1)
            step(NT - 1, True, True, NT - 1)
            step(NT, False, True, NT)

        @block.gpsimd
        def _(pool):
            pool.memset(g.vh[:, :, :, :, HD:HD + 1], 1.0).then_inc(g.ones_set, 1)
            pool.memset(g.vh[:, :, :, :, HD + 1:], 0.0).then_inc(g.ones_set, 1)
            pool.wait_ge(g.ones_set, 3)

            def step(i, norm_next):
                if norm_next:
                    ln.gpsimd_power(pool, i + 1)
                pool.wait_ge(st_lo, 2 * i + 2)
                pool.tensor_tensor(waiter[:], g.neg_half[0:1, 0:1], g.neg_half[0:1, 0:1], ALU.add)
                for high, high2, low, low2 in zip(HIGH, HIGH2, LOW, LOW2):
                    a = high[0]
                    pool.tensor_copy(st[:, a, :, high2[1], :], st[:, a, :, high[1], :])
                    pool.tensor_copy(st[:, a, :, low2[1], :], st[:, a, :, low[1], :]).then_inc(st_copied, 1)
            ln.gpsimd_power(pool, 0)
            step(0, True)
            with pool.Fori(1, NT - 1) as i:
                step(i, True)
            step(NT - 1, False)


def head_pairs(nc, g):
    with ExitStack() as ctx:
        b = Bufs(nc, ctx, "c2")
        att = NarrowHeads(b, g, HD + 1)
        q_s = b.sb("q_s", [P, 2, T], F32R)
        k_s = b.sb("k_s", [P, 2, T], F32R)
        v_s = b.sb("v_s", [P, 2, NT, 2, att.WIDE])
        slot_loaded = [b.sem(f"slot{s}_loaded") for s in range(2)]
        block = ctx.enter_context(nc.Block())

        @block.sync
        def _(sp):
            def load(j, s, first):
                pair = 2 * j + s
                if not first:
                    sp.wait_ge(att.value_done, att.NU * (pair - 1))
                sp.dma_start(q_s[:, s].bitcast(F32), g.qks[:, ds(pair, 1), :].squeeze(1).bitcast(F32)).then_inc(slot_loaded[s], 16)
                sp.dma_start(k_s[:, s].bitcast(F32), g.qks[:, ds(pair + NP, 1), :].squeeze(1).bitcast(F32)).then_inc(slot_loaded[s], 16)
                sp.dma_start(v_s[:, s], g.vh[:, ds(pair, 1)].squeeze(1)).then_inc(slot_loaded[s], 16)
            for s in range(2):
                load(0, s, True)
            with sp.Fori(1, NP // 2) as j:
                for s in range(2):
                    load(j, s, False)

        @block.tensor
        def _(pe):
            def product(pe, out, s, head, q, k0, k1, stop):
                rows = slice(head * 64, head * 64 + 64)
                return pe.matmul(out, q_s[rows, s, q * P:(q + 1) * P], k_s[rows, s, k0 * P:k1 * P],
                                 start=True, stop=stop)

            def product_t(pe, out, s, head, k, q0, q1):
                rows = slice(head * 64, head * 64 + 64)
                pe.matmul(out, k_s[rows, s, k * P:(k + 1) * P], q_s[rows, s, q0 * P:q1 * P], start=True, stop=False)

            def value(s, head, k):
                return v_s[:, s, k, head, :]

            def pair(n, s, first, last):
                one = isinstance(n, int) and n == 1
                for u in range(att.NU):
                    if u == att.NU - 1 and not last:
                        pe.wait_ge(slot_loaded[1 - s], 24 * (n + 1 - (1 - s)) + 48)
                    back = (lambda: att.transpose_back(pe, n - 1, u, one)) if u < 2 and not first else None
                    att.tensor_step(pe, n, s, u, product, product_t, value, not first, not last, first, back)
            pe.wait_ge(slot_loaded[0], 48)
            pe.wait_ge(att.ones_done, 1)
            for i in range(len(att.S_JOBS[0])):
                att.scores(pe, 0, 0, 0, i, product, True)
            double_pairs(pe, pair)
            for j in range(4):
                att.values(pe, NP - 1, 1, att.NU - 1, j, value, False)
            for blk in range(2):
                att.transpose_back(pe, NP - 1, blk, False)

        @block.scalar
        def _(act):
            def pair(n, s, first, last):
                one = isinstance(n, int) and n == 1
                for u in range(att.NU):
                    if u >= 2:
                        att.keep(act, n, u - 2, first)
                    elif not first:
                        att.keep(act, n - 1, u + 2, one)
                    for i in range(len(att.T_JOBS[u])):
                        att.exponential(act, n, u, i, first)
            double_pairs(act, pair)
            for u in (2, 3):
                att.keep(act, NP - 1, u, False)

        @block.vector
        def _(v):
            def out(n, q0):
                return g.o[:, q0:q0 + 4, ds(2 * n, 2), :]

            def pair(n, s, first, last):
                for u in range(att.NU):
                    att.vector_step(v, n, u, out, not first, not last, first)
            att.make_ones(v)
            att.maxima(v, 0, 0, True)
            double_pairs(v, pair)
            for blk in range(2):
                att.result(v, NP - 1, blk, out)


def heads_output(nc, g, dram):
    with ExitStack() as ctx:
        b = Bufs(nc, ctx, "c3")
        w = b.sb("w", [P, KD, D])
        rden = b.sb("rden", [P, H])
        on = b.sb("on", [P, D])
        ot = b.sb("ot", [P, KD, P])
        ps_t = b.ps("ps_t", [P, 512])
        ps_y = b.ps("ps_y", [P, 512])
        w_loaded = b.sem("w_loaded")
        rden_done = b.sem("rden_done")
        on_done = b.sem("on_done")
        on_t_done = b.sem("on_t_done")
        ot_copied = b.sem("ot_copied")
        y_done = b.sem("y_done")
        y_added = b.sem("y_added")
        block = ctx.enter_context(nc.Block())

        @block.sync
        def _(sp):
            sp.dma_start(w[:], dram["wout"]).then_inc(w_loaded, 16)

        @block.tensor
        def _(pe):
            pe.wait_ge(w_loaded, 16)

            def step(i, one, least):
                pe.wait_ge(on_done, i + 1)
                if least >= 1:
                    pe.wait_ge(ot_copied, i)
                for c in range(KD):
                    mm = pe.transpose(ps_t[:, c * P:(c + 1) * P], on[:, c * P:(c + 1) * P], g.ident[:])
                mm.then_inc(on_t_done, 1)
                pe.wait_ge(ot_copied, i + 1)
                if least >= 1:
                    pe.wait_ge(y_added, i)
                for c in range(KD):
                    mm = pe.matmul(ps_y[:, 0:D], ot[:, c, :], w[:, c, :], start=(c == 0), stop=(c == KD - 1))
                mm.then_inc(y_done, 1)
            staged(1, pe, step)

        @block.scalar
        def _(act):
            def step(i, one, least):
                act.wait_ge(on_t_done, i + 1)
                if least >= 1:
                    act.wait_ge(y_done, i)
                act.activation(ot[:], ps_t[:, 0:D].rearrange("p (k c) -> p k c", c=P), ACT.Copy).then_inc(ot_copied, 1)
            staged(1, act, step)

        @block.vector
        def _(v):
            def step(i, one, two, least):
                if one:
                    if least >= 1:
                        v.wait_ge(on_t_done, i)
                    v.reciprocal(rden[:], g.o[:, ds(i, 1), :, HD].squeeze(1)).then_inc(rden_done, 1)
                    v.wait_ge(rden_done, i + 1)
                    v.tensor_tensor(on[:].rearrange("p (h c) -> p h c", c=HD), g.o[:, ds(i, 1), :, 0:HD].squeeze(1),
                                    rden[:].unsqueeze(2).broadcast_to([P, H, HD]), ALU.mult).then_inc(on_done, 1)
                if two:
                    t = i - 1
                    v.wait_ge(y_done, t + 1)
                    v.tensor_tensor(g.X[:, ds(t * D, D)], g.X[:, ds(t * D, D)], ps_y[:, 0:D],
                                    ALU.add).then_inc(y_added, 1)
            staged(2, v, step)


def many_head_attention(nc, g, dram):
    with ExitStack() as ctx:
        b = Bufs(nc, ctx, "c")
        g.o = b.sb("o", [P, NT, H, HD + 1])
        with ExitStack() as hctx:
            h = Bufs(nc, hctx, "ch")
            g.qks = h.sb("qks", [P, 2 * NP, T], F32R)
            g.vh = h.sb("vh", [P, NP, NT, 2, NarrowHeads.WIDE])
            heads_projections(nc, g, dram)
            head_pairs(nc, g)
        heads_output(nc, g, dram)


HALF = T // 2
HT = NT // 2


def prepare_ffn(nc, g, dram):
    with ExitStack() as ctx:
        b = Bufs(nc, ctx, "fp")
        raw = b.sb("raw", [P, 2, KD, FF])
        w2 = b.sb("w2", [P, NFF, D])
        had = b.sb("had", [P, P])
        fly = b.sb("fly", [P, 2, NFF, D])
        ps = b.ps("ps", [P, NFF, D])
        raw_loaded = b.sem("raw_loaded")
        w2_loaded = b.sem("w2_loaded")
        had_done = b.sem("had_done")
        fly_start = b.sem("fly_start")
        fly_done = b.sem("fly_done")
        w_hi = b.sem("w_hi")
        w_lo = b.sem("w_lo")
        block = ctx.enter_context(nc.Block())

        @block.sync
        def _(sp):
            sp.dma_start(had[:], dram["had"]).then_inc(w2_loaded, 16)
            sp.dma_start(w2[:], dram["w2f"]).then_inc(w2_loaded, 16)
            sp.dma_start(raw[:], dram["w13"]).then_inc(raw_loaded, 16)

        @block.tensor
        def _(pe):
            pe.wait_ge(w2_loaded, 32)
            for k in range(0, NFF, 2):
                for j in range(k, k + 2):
                    mm = pe.matmul(ps[:, j, :], had[:], w2[:, j, :], start=True, stop=True)
                mm.then_inc(had_done, 1)

        @block.scalar
        def _(act):
            for k in range(0, NFF, 2):
                act.wait_ge(had_done, k // 2 + 1)
                act.activation(fly[:, 0, k:k + 2, :], ps[:, k:k + 2, :], ACT.Copy, scale=FF ** -0.5).then_inc(fly_start, 1)
            act.wait_ge(raw_loaded, 16)
            for n in range(2):
                act.activation(g.w13_h[:, n], raw[:, n], ACT.Copy).then_inc(w_hi, 1)

        @block.vector
        def _(v):
            v.wait_ge(fly_start, NFF // 2)
            done = 0
            for stage in range(3):
                src = fly[:, stage % 2].rearrange("p (a two j) d -> p a two j d", two=2, j=1 << stage)
                dst = (g.w2f[:] if stage == 2 else fly[:, 1 - stage % 2])\
                    .rearrange("p (a two j) d -> p a two j d", two=2, j=1 << stage)
                if stage:
                    v.wait_ge(fly_done, done)
                for a in range(src.shape[1]):
                    v.tensor_tensor(dst[:, a, 0], src[:, a, 0], src[:, a, 1], ALU.add).then_inc(fly_done, 1)
                    v.tensor_tensor(dst[:, a, 1], src[:, a, 0], src[:, a, 1], ALU.subtract).then_inc(fly_done, 1)
                    done += 2
            for n in range(2):
                v.wait_ge(w_hi, n + 1)
                v.tensor_tensor(g.w13_l[:, n], raw[:, n], g.w13_h[:, n].bitcast(F32), ALU.subtract).then_inc(w_lo, 1)


def feed_forward(nc, g, tag):
    with ExitStack() as ctx:
        b = Bufs(nc, ctx, tag)
        ln = LayerNorm(b, g)
        xt_h = b.sb("xt_h", [P, 2, KD, HALF], F32R)
        xt_l = b.sb("xt_l", [P, 2, KD, HALF], F32R)
        silu = b.sb("silu", [P, 2, HALF])
        hid = b.sb("hid", [P, NFF, HALF])
        ps_x = b.ps("ps_x", [P, 512])
        ps_g = b.ps("ps_g", [P, 2, 512])
        ps_u = b.ps("ps_u", [P, 2, 512])
        ps_y = b.ps("ps_y", [P, 2, 512])
        xt_hi = b.sem("xt_hi")
        xt_lo = b.sem("xt_lo")
        gate_done = b.sem("gate_done")
        up_done = b.sem("up_done")
        silu_done = b.sem("silu_done")
        hid_done = b.sem("hid_done")
        y_done = b.sem("y_done")
        y_added = b.sem("y_added")
        block = ctx.enter_context(nc.Block())

        @block.tensor
        def _(pe):
            def input_tile(t):
                if t:
                    pe.wait_ge(xt_lo, t)
                ln.tensor_transpose(pe, ps_x, t)

            def features(s):
                half, f = divmod(s, NFF)
                fs = slice(f * P, (f + 1) * P)
                for n, (ps, sem) in enumerate(((ps_g, gate_done), (ps_u, up_done))):
                    if s >= 2:
                        pe.wait_ge(hid_done, s - 1)
                    for c in range(KD):
                        mm = split3(pe, ps[:, s % 2, :], (g.w13_h[:, n, c, fs], g.w13_l[:, n, c, fs]),
                                    (xt_h[:, half, c, :], xt_l[:, half, c, :]), c == 0, c == KD - 1)
                    mm.then_inc(sem, 1)

            def output(t):
                cols = slice(t % HT * P, (t % HT + 1) * P)
                if t >= 2:
                    pe.wait_ge(y_added, t - 1)
                for f in range(NFF):
                    if t % HT == 0:
                        pe.wait_ge(hid_done, t // HT * NFF + f + 1)
                    mm = pe.matmul(ps_y[:, t % 2, 0:D], hid[:, f, cols], g.w2f[:, f, :], start=(f == 0),
                                   stop=(f == NFF - 1))
                mm.then_inc(y_done, 1)

            for t in range(HT):
                input_tile(t)
            pe.wait_ge(xt_hi, HT)
            pe.wait_ge(xt_lo, HT)
            for f in range(NFF):
                features(f)
                if f % 2:
                    input_tile(HT + f // 2)
            for t in range(HT):
                output(t)
            pe.wait_ge(xt_hi, NT)
            pe.wait_ge(xt_lo, NT)
            for f in range(NFF):
                features(NFF + f)
            for t in range(HT, NT):
                output(t)

        @block.scalar
        def _(act):
            def high(t):
                act.wait_ge(ln.xn_read, t + 1)
                act.activation(xt_h[:, t // HT, :, t % HT * P:(t % HT + 1) * P],
                               ps_x[:, 0:D].rearrange("p (c q) -> p c q", c=KD), ACT.Copy).then_inc(xt_hi, 1)

            def gate(s):
                act.wait_ge(gate_done, s + 1)
                if s >= 2:
                    act.wait_ge(hid_done, s - 1)
                act.activation(silu[:, s % 2, :], ps_g[:, s % 2, :], ACT.Silu).then_inc(silu_done, 1)

            for t in range(HT):
                high(t)
            for f in range(NFF):
                gate(f)
                if f % 2:
                    high(HT + f // 2)
            for f in range(NFF):
                gate(NFF + f)

        @block.vector
        def _(v):
            def low(t):
                v.wait_ge(xt_hi, t + 1)
                half, cols = t // HT, slice(t % HT * P, (t % HT + 1) * P)
                v.tensor_tensor(xt_l[:, half, :, cols], ps_x[:, 0:D].rearrange("p (c q) -> p c q", c=KD),
                                xt_h[:, half, :, cols].bitcast(F32), ALU.subtract).then_inc(xt_lo, 1)

            def norm(t):
                ln.vector_stats(v, t, t)
                ln.vector_scale(v, t, t, t == 0)

            def hidden(s):
                half, f = divmod(s, NFF)
                v.wait_ge(silu_done, s + 1)
                v.wait_ge(up_done, s + 1)
                if half:
                    v.wait_ge(y_done, HT)
                v.tensor_tensor(hid[:, f, :], ps_u[:, s % 2, :], silu[:, s % 2, :], ALU.mult).then_inc(hid_done, 1)

            def add(t):
                v.wait_ge(y_done, t + 1)
                v.tensor_tensor(g.X[:, ds(t * D, D)], g.X[:, ds(t * D, D)], ps_y[:, t % 2, 0:D],
                                ALU.add).then_inc(y_added, 1)

            norm(0)
            for t in range(HT):
                norm(t + 1)
                low(t)
            for f in range(NFF):
                hidden(f)
                if f % 2:
                    t = HT + f // 2
                    low(t)
                    if t + 1 < NT:
                        norm(t + 1)
            for t in range(HT):
                add(t)
            for f in range(NFF):
                hidden(NFF + f)
            for t in range(HT, NT):
                add(t)

        @block.gpsimd
        def _(pool):
            for t in range(NT):
                ln.gpsimd_power(pool, t)


def gated_cumsum(nc, g, dram):
    M = KD
    GH = D // 4
    with ExitStack() as ctx:
        b = Bufs(nc, ctx, "d")
        ln = LayerNorm(b, g)
        w = b.sb("w", [P, KD, 2 * D + GH])
        w_h = b.sb("w_h", [P, KD, 2 * D + GH], F32R)
        w_l = b.sb("w_l", [P, KD, 2 * D + GH], F32R)
        wg2 = b.sb("wg2", [GH, D])
        wu = b.sb("wu", [P, M, D])
        bias = b.sb("bias", [P, 3, M])
        bg1 = b.sb("bg1", [GH, 1])
        taps = b.sb("taps", [P, KD, 4])
        xt = b.sb("xt", [P, KD, T + 2])
        xt_h = b.sb("xt_h", [P, KD, T], F32R)
        xt_l = b.sb("xt_l", [P, KD, T], F32R)
        hidden = b.sb("hidden", [GH, T])
        gates = b.sb("gates", [P, M, T])
        ones = b.sb("ones", [P, T])
        ug = b.sb("ug", [P, M, T])
        vg = b.sb("vg", [P, M, T])
        run = b.sb("run", [P, M, T])
        conv = b.sb("conv", [P, KD, T])
        ps_x = b.ps("ps_x", [P, 512])
        ps_h = b.ps("ps_h", [P, 2, 512])
        ps_uv = b.ps("ps_uv", [P, 2, 512])
        ps_y = b.ps("ps_y", [P, 2, 512])
        loaded = b.sem("loaded")
        small_loaded = b.sem("small_loaded")
        ones_set = b.sem("ones_set")
        w_hi = b.sem("w_hi")
        w_lo = b.sem("w_lo")
        xt_full = b.sem("xt_full")
        xt_hi = b.sem("xt_hi")
        xt_lo = b.sem("xt_lo")
        h_done = b.sem("h_done")
        relu_done = b.sem("relu_done")
        g_done = b.sem("g_done")
        gates_done = b.sem("gates_done")
        uv_done = b.sem("uv_done")
        uv_gated = b.sem("uv_gated")
        run_done = b.sem("run_done")
        out_done = b.sem("out_done")
        conv_done = b.sem("conv_done")
        y_done = b.sem("y_done")
        y_added = b.sem("y_added")
        block = ctx.enter_context(nc.Block())
        halves = [slice(n * HALF, (n + 1) * HALF) for n in range(2)]
        jobs = [(a, m, n) for m in range(M) for a in range(2) for n in range(2)]

        @block.sync
        def _(sp):
            sp.dma_start(w[:], dram["wuvg"]).then_inc(loaded, 16)
            sp.dma_start(wg2[:], dram["wg2"]).then_inc(small_loaded, 16)
            sp.dma_start(wu[:], dram["wu"]).then_inc(small_loaded, 16)
            sp.dma_start(bias[:], dram["bias3"]).then_inc(small_loaded, 16)
            sp.dma_start(bg1[:], dram["bg1"]).then_inc(small_loaded, 16)
            sp.dma_start(taps[:], dram["taps"]).then_inc(small_loaded, 16)

        @block.tensor
        def _(pe):
            def input_tile(t, least):
                if least:
                    pe.wait_ge(xt_full, t)
                    pe.wait_ge(xt_hi, t)
                ln.tensor_transpose(pe, ps_x, t)
            input_tile(0, 0)
            with pe.Fori(1, NT) as t:
                input_tile(t, 1)
            pe.wait_ge(xt_lo, NT)
            pe.wait_ge(w_lo, 1)

            def product(out, cols, n):
                for c in range(KD):
                    mm = split3(pe, out, (w_h[:, c, cols], w_l[:, c, cols]), (xt_h[:, c, halves[n]], xt_l[:, c, halves[n]]),
                                c == 0, c == KD - 1)
                return mm
            for n in range(2):
                product(ps_h[0:GH, n, :], slice(2 * D, 2 * D + GH), n).then_inc(h_done, 1)
            pe.wait_ge(small_loaded, 16 * 5)

            def gate(m):
                for n in range(2):
                    if m == 0:
                        pe.wait_ge(relu_done, n + 1)
                    else:
                        pe.wait_ge(gates_done, n + 1)
                    pe.matmul(ps_h[:, n, :], wg2[:, m * P:(m + 1) * P], hidden[:, halves[n]], start=True,
                              stop=True).then_inc(g_done, 1)

            def uv(j):
                a, m, n = jobs[j]
                if j >= 2:
                    pe.wait_ge(uv_gated, j - 1)
                product(ps_uv[:, j % 2, :], slice(a * D + m * P, a * D + (m + 1) * P), n).then_inc(uv_done, 1)
            pe.wait_ge(relu_done, 2)
            gate(0)
            for j in range(4):
                uv(j)
            gate(1)
            for j in range(4, 8):
                uv(j)
            pe.wait_ge(conv_done, 3 * KD)
            for t in range(NT):
                tokens = slice(t * P, (t + 1) * P)
                if t == 0:
                    pe.wait_ge(out_done, M)
                if t >= 2:
                    pe.wait_ge(y_added, t - 1)
                for m in range(M):
                    pe.matmul(ps_y[:, t % 2, 0:D], run[:, m, tokens], wu[:, m, :], start=(m == 0), stop=False)
                for c in range(KD):
                    mm = pe.matmul(ps_y[:, t % 2, c * P:(c + 1) * P], conv[:, c, tokens], g.ident[:], start=False,
                                   stop=(c == KD - 1))
                mm.then_inc(y_done, 1)

        @block.scalar
        def _(act):
            act.wait_ge(loaded, 16)
            act.activation(w_h[:], w[:], ACT.Copy).then_inc(w_hi, 1)

            def full(t):
                act.wait_ge(ln.xn_read, t + 1)
                act.activation(xt[:, :, ds(t * P + 1, P)], ps_x[:, 0:D].rearrange("p (c q) -> p c q", c=KD),
                               ACT.Copy).then_inc(xt_full, 1)
            full(0)
            with act.Fori(1, NT) as t:
                full(t)
            act.wait_ge(small_loaded, 16 * 5)
            for n in range(2):
                act.wait_ge(h_done, n + 1)
                act.activation(hidden[:, halves[n]], ps_h[0:GH, n, :], ACT.Relu, bias=bg1[:, 0:1]).then_inc(relu_done, 1)
            for m in range(M):
                for n in range(2):
                    act.wait_ge(g_done, 2 * m + n + 1)
                    act.activation(gates[:, m, halves[n]], ps_h[:, n, :], ACT.Sigmoid,
                                   bias=bias[:, 2, m:m + 1]).then_inc(gates_done, 1)

        @block.vector
        def _(v):
            ln.vector_stats(v, 0, 0)
            ln.vector_scale(v, 0, 0, True)
            v.wait_ge(w_hi, 1)
            v.tensor_tensor(w_l[:], w[:], w_h[:].bitcast(F32), ALU.subtract).then_inc(w_lo, 1)

            def high(t):
                v.wait_ge(xt_full, t + 1)
                v.tensor_copy(xt_h[:, :, ds(t * P, P)], ps_x[:, 0:D].rearrange("p (c q) -> p c q", c=KD)).then_inc(xt_hi, 1)

            def step(t):
                ln.vector_stats(v, t + 1, t + 1)
                high(t)
                ln.vector_scale(v, t + 1, t + 1, False)
            step(0)
            with v.Fori(1, NT - 1) as t:
                step(t)
            high(NT - 1)
            v.wait_ge(small_loaded, 16 * 5)

            def gated(j):
                a, m, n = jobs[j]
                v.wait_ge(uv_done, j + 1)
                v.wait_ge(gates_done, 2 * m + n + 1)
                v.scalar_tensor_tensor((ug, vg)[a][:, m, halves[n]], ps_uv[:, j % 2, :], bias[:, a, m:m + 1],
                                       gates[:, m, halves[n]], ALU.add, ALU.mult).then_inc(uv_gated, 1)

            def convolve(c):
                v.wait_ge(ones_set, 2)
                v.tensor_scalar(conv[:, c, :], xt[:, c, 1:T + 1], taps[:, c, 1:2], taps[:, c, 3:4], ALU.mult,
                                ALU.add).then_inc(conv_done, 1)
                for n, tap in enumerate((0, 2)):
                    v.wait_ge(conv_done, 3 * c + n + 1)
                    v.scalar_tensor_tensor(conv[:, c, :], xt[:, c, tap:tap + T], taps[:, c, tap:tap + 1], conv[:, c, :],
                                           ALU.mult, ALU.add).then_inc(conv_done, 1)
            convolve(0)
            for m in range(M):
                for j in range(4 * m, 4 * m + 4):
                    gated(j)
                if m == 0:
                    convolve(1)
                v.wait_ge(uv_gated, 4 * m + 2)
                v.tensor_tensor_scan(run[:, m, :], ones[:], ug[:, m, :], 0.0, ALU.mult, ALU.add).then_inc(run_done, 1)
                v.wait_ge(run_done, m + 1)
                v.wait_ge(uv_gated, 4 * m + 4)
                v.tensor_tensor(run[:, m, :], run[:, m, :], vg[:, m, :], ALU.mult).then_inc(out_done, 1)
            for t in range(NT):
                v.wait_ge(y_done, t + 1)
                v.tensor_tensor(g.X[:, ds(t * D, D)], g.X[:, ds(t * D, D)], ps_y[:, t % 2, 0:D],
                                ALU.add).then_inc(y_added, 1)

        @block.gpsimd
        def _(pool):
            pool.memset(ones[:], 1.0).then_inc(ones_set, 1)
            pool.memset(xt[:, :, 0:T + 2:T + 1], 0.0).then_inc(ones_set, 1)
            ln.gpsimd_power(pool, 0)

            def low(t):
                tokens = ds(t * P, P)
                pool.wait_ge(xt_hi, t + 1)
                pool.tensor_tensor(xt_l[:, :, tokens], xt[:, :, ds(t * P + 1, P)], xt_h[:, :, tokens].bitcast(F32),
                                   ALU.subtract).then_inc(xt_lo, 1)

            def step(t):
                ln.gpsimd_power(pool, t + 1)
                low(t)
            step(0)
            with pool.Fori(1, NT - 1) as t:
                step(t)
            low(NT - 1)


class Persistent:
    pass


def clear_released_semaphores(nc):
    done = sorted(nc.released_uncleared_semaphores)
    runs = []
    for n in done:
        if runs and runs[-1][1] == n:
            runs[-1][1] = n + 1
        else:
            runs.append([n, n + 1])
    with nc.Block() as block:
        @block.gpsimd
        def _(pool):
            for start, end in runs:
                pool.sem_clear(range(start, end))


def build(nc, dram, out):
    with ExitStack() as ctx:
        g = Persistent()
        b = Bufs(nc, ctx, "g")
        X = b.sb("X", [P, NT * D])
        g.X = X
        g.ident = b.sb("ident", [P, P])
        g.ident_b = b.sb("ident_b", [P, P], BF16)
        g.causal = b.sb("causal", [P, P], BF16)
        g.neg_half = b.sb("neg_half", [P, 8])
        g.qnw0 = b.sb("qnw0", [P, 1])
        g.qnw1 = b.sb("qnw1", [QR1, 1])
        g.kvw = b.sb("kvw", [P, 1])
        g.kvw_s = b.sb("kvw_s", [P, 1])
        g.w1_raw = b.sb("w1_raw", [P, KD, W1_N])
        g.loaded_x = b.sem("loaded_x")
        g.loaded_ident = b.sem("loaded_ident")
        g.loaded_const = b.sem("loaded_const")
        g.loaded_wa = b.sem("loaded_wa")
        g.loaded_wr = b.sem("loaded_wr")
        g.loaded_w1 = b.sem("loaded_w1")
        g.loaded_w2 = b.sem("loaded_w2")
        g.neg_half_set = b.sem("neg_half_set")
        g.vext_done = b.sem("vext_done")
        g.kvw_scaled = b.sem("kvw_scaled")
        g.ones_set = b.sem("ones_set")
        stored = b.sem("stored")
        g.N_CONST = 6

        with ExitStack() as actx:
            a = Bufs(nc, actx, "a")
            g.wvo = a.sb("wvo", [P, NP, D])
            g.u_space = a.sb("u", [P, NT * H * (KL + 1)])
            g.u = g.u_space[:].rearrange("p (t h c) -> p t h c", h=H, c=KL + 1)
            with ExitStack() as hctx:
                h = Bufs(nc, hctx, "h")
                g.kt_h = h.sb("kt_h", [P, 2, T], F32R)
                g.kt_l = h.sb("kt_l", [P, 2, T], F32R)
                g.vext = h.sb("vext", [P, NT, KL + 1])
                g.qrt = h.sb("qrt", [P, NP, T])
                g.qat0 = h.sb("qat0", [P, T])
                g.qat1 = h.sb("qat1", [QR1, T])
                g.wq = h.sb("wq", [P, NP, 2 * P])
                with ExitStack() as wctx:
                    w = Bufs(nc, wctx, "w")
                    g.cos_q = w.sb("cos_q", [P, NT, DR])
                    g.sin_q = w.sb("sin_q", [P, NT, DR])
                    g.cos_k = w.sb("cos_k", [P, NT, DR])
                    g.sin_k = w.sb("sin_k", [P, NT, DR])
                    g.wa = w.sb("wa", [P, KD, WA_N])
                    g.wr0 = g.u_space[:, 0:H * DR]
                    g.wr1 = g.u_space[0:QR1, H * DR:2 * H * DR]
                    with nc.Block() as block:
                        @block.sync
                        def _(sp):
                            sp.dma_start(X[:].rearrange("p (t d) -> p t d", d=D), dram["x"]).then_inc(g.loaded_x, 16)
                            sp.dma_start(g.wr0, dram["wr"][0:P, :]).then_inc(g.loaded_wr, 16)
                            sp.dma_start(g.wr1, dram["wr"][P:QL, :]).then_inc(g.loaded_wr, 16)
                            sp.dma_start(g.cos_q[:], dram["cos_q"]).then_inc(g.loaded_const, 16)
                            sp.dma_start(g.sin_q[:], dram["sin_q"]).then_inc(g.loaded_const, 16)

                        @block.scalar
                        def _(act):
                            act.dma_start(g.ident[:], dram["ident"]).then_inc(g.loaded_ident, 16)
                            act.dma_start(g.wa[:], dram["wa"]).then_inc(g.loaded_wa, 16)
                            act.dma_start(g.cos_k[:], dram["cos_k"]).then_inc(g.loaded_const, 16)
                            act.dma_start(g.sin_k[:], dram["sin_k"]).then_inc(g.loaded_const, 16)
                            act.dma_start(g.qnw0[:], dram["qnw"][0:P, :]).then_inc(g.loaded_wr, 16)
                            act.dma_start(g.qnw1[:], dram["qnw"][P:QL, :]).then_inc(g.loaded_wr, 16)
                            act.dma_start(g.kvw[:], dram["kvw"]).then_inc(g.loaded_wr, 16)
                            act.dma_start(g.causal[:], dram["causal"]).then_inc(g.loaded_const, 16)
                            act.dma_start(g.ident_b[:], dram["ident_b"]).then_inc(g.loaded_const, 16)

                        @block.gpsimd
                        def _(pool):
                            pool.memset(g.neg_half[:], -0.5).then_inc(g.neg_half_set, 1)
                            pool.memset(g.vext[:], 1.0).then_inc(g.ones_set, 1)
                            pool.wait_ge(g.ones_set, 1)
                    latent_projections(nc, g, dram)
                latent_heads(nc, g, dram)
            latent_output(nc, g)

        experts_and_middle(nc, g, dram)
        clear_released_semaphores(nc)
        many_head_attention(nc, g, dram)
        f = Bufs(nc, ctx, "f")
        g.w13_h = f.sb("w13_h", [P, 2, KD, FF], F32R)
        g.w13_l = f.sb("w13_l", [P, 2, KD, FF], F32R)
        g.w2f = f.sb("w2f", [P, NFF, D])
        prepare_ffn(nc, g, dram)
        feed_forward(nc, g, "f1")
        gated_cumsum(nc, g, dram)
        feed_forward(nc, g, "f2")

        with nc.Block() as block:
            @block.sync
            def _(sp):
                sp.wait_ge(g.loaded_const, 16 * g.N_CONST)
                sp.dma_start(out, X[:].rearrange("p (t d) -> p t d", d=D)).then_inc(stored, 16)
                sp.wait_ge(stored, 16)


def _rope_tables(np):
    inv = np.float32(1.0) / np.float32(10000.0) ** (np.arange(0, DR, 2, dtype=np.float32) / np.float32(DR))
    freqs = np.outer(np.arange(T, dtype=np.float32), inv.astype(np.float32)).astype(np.float32)
    cos, sin = np.cos(freqs), np.sin(freqs)
    lay = lambda a: np.ascontiguousarray(a.reshape(NT, P, DR).transpose(1, 0, 2).astype(np.float32))
    return lay(np.concatenate([cos, cos], 1)), lay(np.concatenate([-sin, sin], 1))


def kernel(**inputs):
    import ml_dtypes
    import numpy as np
    import concourse.bacc as bacc
    from concourse.bass_utils import run_bass_kernel_spmd

    w = {k: np.asarray(v) for k, v in inputs.items()}
    rows = lambda a: np.ascontiguousarray(a.reshape(KD, P, -1).transpose(1, 0, 2))
    cat = np.concatenate
    arrays = {}
    arrays["x"] = np.ascontiguousarray(w["L0_attn_a_hidden_states"][0].reshape(NT, P, D).transpose(1, 0, 2))

    wq_b = w["L0_attn_a_Wq_b"].reshape(QL, H, DN + DR)
    wkv_b = w["L0_attn_a_Wkv_b"].reshape(KL, H, 2 * DN)
    wo = w["L0_attn_a_Wo"].reshape(H, DN, D)
    arrays["wa"] = rows(cat([w["L0_attn_a_Wq_a"], w["L0_attn_a_Wkv_a"], w["L0_attn_a_Wk_rope"]], 1))
    arrays["wr"] = np.ascontiguousarray(wq_b[:, :, DN:]).reshape(QL, H * DR)
    heads = cat([wq_b[:, :, :DN].transpose(1, 2, 0), wkv_b[:, :, :DN].transpose(1, 2, 0),
                 wkv_b[:, :, DN:].transpose(1, 2, 0), wo], 2)
    arrays["wh"] = np.ascontiguousarray(heads.reshape(NP, 2, P, WH_N).transpose(0, 2, 1, 3))
    arrays["qnw"] = w["L0_attn_a_q_norm_w"].reshape(QL, 1)
    arrays["kvw"] = cat([w["L0_attn_a_kv_norm_w"]] * 2).reshape(P, 1)

    w1 = [w["L0_ffn_sw1"].T, w["L0_ffn_sw2"].T, w["L0_ffn_gate_w"].T] + list(w["L0_ffn_w1"])
    arrays["w1"] = rows(cat(w1, 1))
    arrays["w2"] = cat([w["L0_ffn_sw3"].T, w["L0_ffn_w2"].reshape(NE * FI, D)], 0)

    arrays["wb"] = np.stack([rows(w["L0_attn_b_W_q"].T), rows(w["L0_attn_b_W_k"].T), rows(w["L0_attn_b_W_v"].T),
                             rows(w["L0_attn_b_W_o"])], 1)

    arrays["wqkv"] = rows(w["L1_attn_a_w_qkv"])
    arrays["wout"] = rows(w["L1_attn_a_w_out"])

    arrays["w13"] = np.stack([rows(w["L1_ffn_W1"].T), rows(w["L1_ffn_W3"].T)], 1)
    arrays["w2f"] = w["L1_ffn_W2"].T.reshape(NFF, P, D).transpose(1, 0, 2)
    had = np.ones((1, 1), np.float32)
    while had.shape[0] < P:
        had = np.block([[had, had], [had, -had]])
    arrays["had"] = had

    chunks = lambda a: a.reshape(KD, P, -1).transpose(1, 0, 2)
    arrays["wuvg"] = rows(cat([w["L1_attn_b_Wu"].T, w["L1_attn_b_Wv"].T, w["L1_attn_b_Wg1"].T], 1))
    arrays["wg2"] = w["L1_attn_b_Wg2"].T
    arrays["wu"] = rows(w["L1_attn_b_Wu"].T)
    arrays["bias3"] = np.stack([chunks(w[f"L1_attn_b_{n}"])[:, :, 0] for n in ("bu", "bv", "bg2")], 1)
    arrays["bg1"] = w["L1_attn_b_bg1"].reshape(-1, 1)
    arrays["taps"] = cat([chunks(w["L1_attn_b_conv_w"].reshape(D, 3)), chunks(w["L1_attn_b_conv_b"])], 2)

    cos, sin = _rope_tables(np)
    scale = np.float32((DN + DR) ** -0.5)
    arrays["cos_k"], arrays["sin_k"] = cos, sin
    arrays["cos_q"], arrays["sin_q"] = cos * scale, sin * scale
    arrays["ident"] = np.eye(P, dtype=np.float32)
    arrays["ident_b"] = np.eye(P, dtype=ml_dtypes.bfloat16)
    arrays["causal"] = np.where(np.tri(P, dtype=bool), 0.0, -3e38).astype(ml_dtypes.bfloat16)

    nc = bacc.Bacc("TRN2", target_bir_lowering=False, num_devices=1)
    dram = {}
    for name, a in arrays.items():
        a = arrays[name] = np.ascontiguousarray(a)
        dram[name] = nc.dram_tensor(name, a.shape, mybir.dt.from_np(a.dtype), kind="ExternalInput").ap()
    out = nc.dram_tensor("out", (P, NT, D), F32, kind="ExternalOutput").ap()
    build(nc, dram, out)
    r = run_bass_kernel_spmd(nc, [arrays], core_ids=[0])
    got = r.results[0]["out"]
    return np.ascontiguousarray(np.asarray(got).transpose(1, 0, 2)).reshape(1, T, D)
```

```python
from contextlib import ExitStack

import concourse.bass as bass
from concourse import mybir

ALU = mybir.AluOpType
ACT = mybir.ActivationFunctionType
AX = mybir.AxisListType.X
F32 = mybir.dt.float32
F32R = mybir.dt.float32r
BF16 = mybir.dt.bfloat16

P = 128
T, D = 1024, 256
NT = T // P
KD = D // P
LN_EPS = 1e-5

H = 16
NP = H // 2
QL, KL, DR, DN = 192, 64, 64, 128
QR1 = QL - P
WA_N = QL + KL + DR
RMS_EPS = 1e-6
WH_N = QL + KL + KL + D

NE, FI = 8, 176
BLK = 2 * FI
W1_N = (NE + 1) * BLK + NE
FH = (NE + 1) * FI
NF = (FH + P - 1) // P
FTAIL = FH - (NF - 1) * P

HD = D // H
FF = 1024
NFF = FF // P


def ds(start, size):
    return bass.ds(start, size)


class Bufs:

    def __init__(self, nc, ctx, tag):
        self.nc, self.ctx, self.tag = nc, ctx, tag

    def sb(self, name, shape, dt=F32):
        return self.ctx.enter_context(self.nc.sbuf_tensor(f"{self.tag}_{name}", shape, dt))

    def ps(self, name, shape, dt=F32):
        return self.ctx.enter_context(self.nc.psum_tensor(f"{self.tag}_{name}", shape, dt))

    def sem(self, name):
        return self.ctx.enter_context(self.nc.semaphore(f"{self.tag}_{name}"))


def split3(pe, out, lhs, rhs, start, stop):
    (lh, ll), (rh, rl) = lhs, rhs
    pe.matmul(out, lh, rh, start=start, stop=False)
    pe.matmul(out, lh, rl, start=False, stop=False)
    return pe.matmul(out, ll, rh, start=False, stop=stop)


def staged(stages, eng, step):
    for i in range(stages):
        step(i, *[s <= i for s in range(stages)], i)
    with eng.Fori(stages, NT - 1) as i:
        step(i, *[True] * stages, stages)
    for i in range(NT - 1, NT + stages - 1):
        step(i, *[s > i - NT for s in range(stages)], i)


def has_next(i):
    return not (isinstance(i, int) and i >= NT - 1)


class LayerNorm:

    def __init__(self, b, g):
        self.g = g
        self.stats = b.sb("ln_stats", [P, 6])
        self.mean_var = b.sb("ln_mean_var", [P, 2])
        self.var_eps = b.sb("ln_var_eps", [P, 1])
        self.rstd = b.sb("ln_rstd", [P, 1])
        self.xn = b.sb("ln_xn", [P, D])
        self.waiter = b.sb("ln_waiter", [1, 1])
        self.stats_done = b.sem("ln_stats_done")
        self.aggr_done = b.sem("ln_aggr_done")
        self.var_done = b.sem("ln_var_done")
        self.rstd_done = b.sem("ln_rstd_done")
        self.xn_done = b.sem("ln_xn_done")
        self.xn_read = b.sem("ln_xn_read")

    def vector_stats(self, v, t, n):
        v.bn_stats(self.stats[:], self.g.X[:, ds(t * D, D)]).then_inc(self.stats_done, 1)
        v.wait_ge(self.stats_done, n + 1)
        v.memset(self.waiter[:], 0.0)
        v.bn_aggr(self.mean_var[:], self.stats[:]).then_inc(self.aggr_done, 1)
        v.wait_ge(self.aggr_done, n + 1)
        v.tensor_scalar(self.var_eps[:], self.mean_var[:, 1:2], LN_EPS, None, ALU.add).then_inc(self.var_done, 1)

    def gpsimd_power(self, pool, n):
        pool.wait_ge(self.var_done, n + 1)
        pool.tensor_tensor(self.rstd[:], self.var_eps[:], self.g.neg_half[:, 0:1], ALU.pow).then_inc(self.rstd_done, 1)

    def vector_scale(self, v, t, n, first):
        v.wait_ge(self.rstd_done, n + 1)
        if not first:
            v.wait_ge(self.xn_read, n)
        v.tensor_scalar(self.xn[:], self.g.X[:, ds(t * D, D)], self.mean_var[:, 0:1], self.rstd[:, 0:1],
                        ALU.subtract, ALU.mult).then_inc(self.xn_done, 1)

    def tensor_transpose(self, pe, out, n):
        pe.wait_ge(self.xn_done, n + 1)
        for c in range(KD):
            mm = pe.transpose(out[:, c * P:(c + 1) * P], self.xn[:, c * P:(c + 1) * P], self.g.ident[:])
        mm.then_inc(self.xn_read, 1)


def latent_projections(nc, g, dram):
    with ExitStack() as ctx:
        b = Bufs(nc, ctx, "a1")
        ln = LayerNorm(b, g)
        wa_h = b.sb("wa_h", [P, KD, WA_N], F32R)
        wa_l = b.sb("wa_l", [P, KD, WA_N], F32R)
        xt_h = b.sb("xt_h", [P, KD * P], F32R)
        xt_l = b.sb("xt_l", [P, KD * P], F32R)
        square = b.sb("square", [P, QL])
        sumsq = b.sb("sumsq", [P, 2])
        meansq = b.sb("meansq", [P, 2])
        rrms = b.sb("rrms", [P, 2])
        qa = b.sb("qa", [P, QL])
        kck = b.sb("kck", [P, 3, DR])
        krc = b.sb("krc", [P, DR])
        krs = b.sb("krs", [P, DR])
        qat0 = b.sb("qat0", [P, P])
        qat1 = b.sb("qat1", [QR1, P])
        rot = g.u_space[:, 2048:3072].rearrange("p (h c) -> p h c", c=DR)
        rot_s = g.u_space[:, 3072:4096].rearrange("p (h c) -> p h c", c=DR)
        qr = b.sb("qr", [P, H * DR])
        rot_c = qr[:].rearrange("p (h c) -> p h c", c=DR)
        ps_x = b.ps("ps_x", [P, 512])
        ps_a = b.ps("ps_a", [P, 512])
        ps_t = b.ps("ps_t", [P, 512])
        ps_r = b.ps("ps_r", [P, 2, 512])
        ps_q = b.ps("ps_q", [P, 2, 512])
        ps_w = b.ps("ps_w", [P, 512])
        wh = b.sb("wh", [P, 2, WH_N])
        wh_loaded = b.sem("wh_loaded")
        w_done = b.sem("w_done")
        w_evac = b.sem("w_evac")
        wa_split = b.sem("wa_split")
        wr_scaled = b.sem("wr_scaled")
        xt_hi = b.sem("xt_hi")
        xt_lo = b.sem("xt_lo")
        proj_done = b.sem("proj_done")
        sumsq_done = b.sem("sumsq_done")
        meansq_done = b.sem("meansq_done")
        rrms_done = b.sem("rrms_done")
        kr_parts = b.sem("kr_parts")
        kr_done = b.sem("kr_done")
        latents_done = b.sem("latents_done")
        key_copied = b.sem("key_copied")
        lat_t_done = b.sem("lat_t_done")
        lat_evac = b.sem("lat_evac")
        key_lo = b.sem("key_lo")
        qat_kept = b.sem("qat_kept")
        rope_mm = b.sem("rope_mm")
        rot_copied = b.sem("rot_copied")
        rot_s_done = b.sem("rot_s_done")
        rot_c_done = b.sem("rot_c_done")
        qr_done = b.sem("qr_done")
        qr_t_done = b.sem("qr_t_done")
        qr_evac = b.sem("qr_evac")
        block = ctx.enter_context(nc.Block())

        @block.sync
        def _(sp):
            def load(p, first):
                if not first:
                    sp.wait_ge(w_done, p)
                sp.dma_start(wh[:], dram["wh"][ds(p, 1)].squeeze(0)).then_inc(wh_loaded, 16)
            load(0, True)
            with sp.Fori(1, NP) as p:
                load(p, False)


        @block.tensor
        def _(pe):
            def step(i, one, two, three, four, least):
                if two:
                    t = i - 1
                    pe.wait_ge(xt_hi, t + 1)
                    pe.wait_ge(xt_lo, t + 1)
                    if least == 1:
                        pe.wait_ge(wa_split, 2)
                    if least >= 2:
                        pe.wait_ge(latents_done, 2 * t)
                        pe.wait_ge(kr_parts, 2 * t)
                    for c in range(KD):
                        cs = slice(c * P, (c + 1) * P)
                        mm = split3(pe, ps_a[:, 0:WA_N], (xt_h[:, cs], xt_l[:, cs]), (wa_h[:, c, :], wa_l[:, c, :]),
                                    c == 0, c == KD - 1)
                    mm.then_inc(proj_done, 1)
                if three:
                    t = i - 2
                    pe.wait_ge(latents_done, 2 * t + 2)
                    pe.wait_ge(key_copied, t + 1)
                    if least >= 3:
                        pe.wait_ge(lat_evac, 3 * t)
                        pe.wait_ge(key_lo, t)
                    pe.transpose(ps_t[:, 0:P], qa[:, 0:P], g.ident[:])
                    pe.transpose(ps_t[0:QR1, P:2 * P], qa[:, P:QL], g.ident[:])
                    pe.transpose(ps_t[:, 2 * P:3 * P], kck[:, 0:2, :], g.ident[:])
                    pe.transpose(ps_t[:, 3 * P:4 * P], kck[:, 1:3, :], g.ident[:]).then_inc(lat_t_done, 1)
                if two:
                    t = i - 1
                    pe.wait_ge(wh_loaded, 16 * t + 16)
                    if least >= 2:
                        pe.wait_ge(w_evac, 3 * t)
                    for head in range(2):
                        c = (1 - head) * KL
                        pe.matmul(ps_w[:, c:c + KL], wh[:, head, 0:P], wh[:, head, QL:QL + KL], start=True, stop=True)
                        pe.matmul(ps_w[0:QR1, P + c:P + c + KL], wh[:, head, P:QL], wh[:, head, QL:QL + KL],
                                  start=True, stop=True)
                    for head in range(2):
                        mm = pe.matmul(ps_w[head * KL:(head + 1) * KL, 2 * P:512], wh[:, head, QL + KL:QL + 2 * KL],
                                       wh[:, head, QL + 2 * KL:WH_N], start=True, stop=True)
                    mm.then_inc(w_done, 1)
                if one:
                    if least >= 1:
                        pe.wait_ge(xt_hi, i)
                        pe.wait_ge(xt_lo, i)
                    ln.tensor_transpose(pe, ps_x, i)
                if three:
                    t = i - 2
                    pe.wait_ge(lat_evac, 3 * t + 2)
                    if least >= 3:
                        pe.wait_ge(rot_copied, t)
                        pe.wait_ge(rot_c_done, t)
                    if least == 2:
                        pe.wait_ge(wr_scaled, 2)
                    for n in range(2):
                        pe.matmul(ps_r[:, n, :], qat0[:], g.wr0[:, n * 512:(n + 1) * 512], start=True, stop=False)
                        mm = pe.matmul(ps_r[:, n, :], qat1[:], g.wr1[:, n * 512:(n + 1) * 512], start=False, stop=True)
                    mm.then_inc(rope_mm, 1)
                if four:
                    t = i - 3
                    pe.wait_ge(qr_done, t + 1)
                    if least >= 4:
                        pe.wait_ge(qr_evac, 2 * t)
                    for c in range(NP):
                        mm = pe.transpose(ps_q[:, c // 4, (c % 4) * P:(c % 4 + 1) * P], qr[:, c * P:(c + 1) * P],
                                          g.ident[:])
                    mm.then_inc(qr_t_done, 1)

            pe.wait_ge(g.loaded_ident, 16)
            staged(4, pe, step)

        @block.scalar
        def _(act):
            def step(i, one, two, three, four, least):
                if two:
                    t = i - 1
                    act.wait_ge(proj_done, t + 1)
                    if least >= 2:
                        act.wait_ge(meansq_done, 2 * t)
                    act.activation(square[:], ps_a[:, 0:QL], ACT.Square,
                                   accum_out=sumsq[:, 0:1]).then_inc(sumsq_done, 1)
                    act.wait_ge(sumsq_done, 2 * t + 1)
                    act.activation(square[:, 0:KL], ps_a[:, QL:QL + KL], ACT.Square,
                                   accum_out=sumsq[:, 1:2]).then_inc(sumsq_done, 1)
                if three:
                    t = i - 2
                    act.wait_ge(lat_t_done, t + 1)
                    if least >= 3:
                        act.wait_ge(rope_mm, t)
                        act.wait_ge(qat_kept, 2 * t)
                    act.activation(qat0[:], ps_t[:, 0:P], ACT.Copy).then_inc(lat_evac, 1)
                    act.activation(qat1[:], ps_t[0:QR1, P:2 * P], ACT.Copy).then_inc(lat_evac, 1)
                    act.activation(g.kt_h[:, :, ds(t * P, P)], ps_t[:, 2 * P:4 * P].rearrange("p (a c) -> p a c", a=2),
                                   ACT.Copy).then_inc(lat_evac, 1)
                if two:
                    t = i - 1
                    if least == 1:
                        act.wait_ge(g.loaded_wr, 16 * 5)
                        act.activation(g.wr0, g.wr0, ACT.Copy, scale=g.qnw0[:, 0:1]).then_inc(wr_scaled, 1)
                        act.activation(g.wr1, g.wr1, ACT.Copy, scale=g.qnw1[:, 0:1]).then_inc(wr_scaled, 1)
                    act.wait_ge(w_done, t + 1)
                    act.activation(g.wq[:, ds(t, 1), 0:P].squeeze(1), ps_w[:, 0:P], ACT.Copy,
                                   scale=g.qnw0[:, 0:1]).then_inc(w_evac, 1)
                    act.activation(g.wq[0:QR1, ds(t, 1), P:2 * P].squeeze(1), ps_w[0:QR1, P:2 * P], ACT.Copy,
                                   scale=g.qnw1[:, 0:1]).then_inc(w_evac, 1)
                    act.activation(g.wvo[:, ds(t, 1), :].squeeze(1), ps_w[:, 2 * P:512], ACT.Copy,
                                   scale=g.kvw[:, 0:1]).then_inc(w_evac, 1)
                if one:
                    act.wait_ge(ln.xn_read, i + 1)
                    if least >= 1:
                        act.wait_ge(proj_done, i)
                    act.activation(xt_h[:], ps_x[:, 0:KD * P], ACT.Copy).then_inc(xt_hi, 1)
                if two:
                    t = i - 1
                    act.wait_ge(kr_done, t + 1)
                    act.activation(kck[:, 2, :], kck[:, 0, :], ACT.Copy).then_inc(key_copied, 1)
                if three:
                    t = i - 2
                    act.wait_ge(rope_mm, t + 1)
                    if least >= 3:
                        act.wait_ge(rot_s_done, t)
                    act.activation(rot, ps_r[:].rearrange("p a (h c) -> p (a h) c", c=DR),
                                   ACT.Copy).then_inc(rot_copied, 1)
                if four:
                    t = i - 3
                    act.wait_ge(qr_t_done, t + 1)
                    act.activation(g.qrt[:, 0:4, ds(t * P, P)], ps_q[:, 0, :].rearrange("p (a c) -> p a c", a=4),
                                   ACT.Copy).then_inc(qr_evac, 1)
            act.wait_ge(g.loaded_wa, 16)
            act.activation(wa_h[:], g.wa[:], ACT.Copy).then_inc(wa_split, 1)
            staged(4, act, step)

        @block.vector
        def _(v):
            def step(i, one, two, three, four, least):
                if least == 0:
                    ln.vector_stats(v, i, i)
                if one:
                    ln.vector_scale(v, i, i, least == 0)
                    if has_next(i):
                        ln.vector_stats(v, i + 1, i + 1)
                if four:
                    t = i - 3
                    v.wait_ge(rot_c_done, t + 1)
                    v.wait_ge(rot_s_done, t + 1)
                    v.tensor_tensor(qr[:].rearrange("p (h c) -> p h c", c=DR), rot_c, rot_s,
                                    ALU.add).then_inc(qr_done, 1)
                if two and least == 1:
                    v.wait_ge(wa_split, 1)
                    v.tensor_tensor(wa_l[:], g.wa[:], wa_h[:].bitcast(F32), ALU.subtract).then_inc(wa_split, 1)
                if two:
                    t = i - 1
                    v.wait_ge(sumsq_done, 2 * t + 2)
                    v.tensor_scalar(meansq[:, 0:1], sumsq[:, 0:1], 1.0 / QL, RMS_EPS, ALU.mult,
                                    ALU.add).then_inc(meansq_done, 1)
                    v.tensor_scalar(meansq[:, 1:2], sumsq[:, 1:2], 1.0 / KL, RMS_EPS, ALU.mult,
                                    ALU.add).then_inc(meansq_done, 1)
                if two:
                    t = i - 1
                    if least == 1:
                        v.wait_ge(g.loaded_const, 16 * g.N_CONST)
                    key = ps_a[:, QL + KL:WA_N]
                    v.tensor_tensor(krc[:], key, g.cos_k[:, ds(t, 1), :].squeeze(1), ALU.mult).then_inc(kr_parts, 1)
                    swapped = key.rearrange("p (a c) -> p a c", a=2)[:, ::-1, :]
                    v.tensor_tensor(krs[:].rearrange("p (a c) -> p a c", a=2), swapped,
                                    g.sin_k[:, ds(t, 1), :].rearrange("p o (a c) -> p (o a) c", a=2),
                                    ALU.mult).then_inc(kr_parts, 1)
                    if least >= 2:
                        v.wait_ge(lat_t_done, t)
                        v.wait_ge(key_copied, t)
                        v.wait_ge(g.vext_done, t)
                    v.wait_ge(kr_parts, 2 * t + 2)
                    v.tensor_tensor(kck[:, 0, :], krc[:], krs[:], ALU.add).then_inc(kr_done, 1)
                    v.wait_ge(rrms_done, t + 1)
                    v.tensor_scalar(qa[:], ps_a[:, 0:QL], rrms[:, 0:1], None, ALU.mult).then_inc(latents_done, 1)
                    v.tensor_scalar(kck[:, 1, :], ps_a[:, QL:QL + KL], rrms[:, 1:2], None,
                                    ALU.mult).then_inc(latents_done, 1)
                if three:
                    t = i - 2
                    v.wait_ge(lat_evac, 3 * t + 3)
                    v.tensor_tensor(g.kt_l[:, :, ds(t * P, P)], ps_t[:, 2 * P:4 * P].rearrange("p (a c) -> p a c", a=2),
                                    g.kt_h[:, :, ds(t * P, P)].bitcast(F32), ALU.subtract).then_inc(key_lo, 1)
                if one:
                    v.wait_ge(ln.xn_read, i + 1)
                    v.wait_ge(xt_hi, i + 1)
                    if least >= 1:
                        v.wait_ge(proj_done, i)
                    v.tensor_tensor(xt_l[:], ps_x[:, 0:KD * P], xt_h[:].bitcast(F32), ALU.subtract).then_inc(xt_lo, 1)
                if four:
                    t = i - 3
                    v.wait_ge(qr_t_done, t + 1)
                    v.tensor_copy(g.qrt[:, 4:8, ds(t * P, P)],
                                  ps_q[:, 1, :].rearrange("p (a c) -> p a c", a=4)).then_inc(qr_evac, 1)
                if three:
                    t = i - 2
                    v.wait_ge(rope_mm, t + 1)
                    v.wait_ge(rot_copied, t + 1)
                    if least >= 3:
                        v.wait_ge(qr_t_done, t)
                    v.tensor_tensor(rot_c, ps_r[:].rearrange("p a (h c) -> p (a h) c", c=DR),
                                    g.cos_q[:, ds(t, 1), :].broadcast_to([P, H, DR]), ALU.mult).then_inc(rot_c_done, 1)
            v.wait_ge(g.loaded_x, 16)
            staged(4, v, step)

        @block.gpsimd
        def _(pool):
            pool.wait_ge(g.neg_half_set, 1)

            def step(i, one, two, three, four, least):
                if least == 0:
                    ln.gpsimd_power(pool, i)
                if one and has_next(i):
                    ln.gpsimd_power(pool, i + 1)
                if two:
                    t = i - 1
                    pool.wait_ge(meansq_done, 2 * t + 2)
                    if least >= 2:
                        pool.wait_ge(latents_done, 2 * t)
                    pool.tensor_tensor(rrms[:], meansq[:], g.neg_half[:, 0:2], ALU.pow).then_inc(rrms_done, 1)
                if three:
                    t = i - 2
                    pool.wait_ge(lat_evac, 3 * t + 2)
                    pool.tensor_copy(g.qat0[:, ds(t * P, P)], qat0[:]).then_inc(qat_kept, 1)
                    pool.tensor_copy(g.qat1[:, ds(t * P, P)], qat1[:]).then_inc(qat_kept, 1)
                if two:
                    t = i - 1
                    pool.wait_ge(latents_done, 2 * t + 2)
                    pool.tensor_copy(g.vext[:, ds(t, 1), 0:KL].squeeze(1), kck[:, 1, :]).then_inc(g.vext_done, 1)
                if three:
                    t = i - 2
                    pool.wait_ge(rot_copied, t + 1)
                    if least >= 3:
                        pool.wait_ge(qr_done, t)
                    pool.tensor_tensor(rot_s.rearrange("p h (a c) -> p h a c", a=2),
                                       rot.rearrange("p h (a c) -> p h a c", a=2)[:, :, ::-1, :],
                                       g.sin_q[:, ds(t, 1), :].rearrange("p o (a c) -> p o a c", a=2).broadcast_to([P, H, 2, DR // 2]),
                                       ALU.mult).then_inc(rot_s_done, 1)
            staged(4, pool, step)
            pool.wait_ge(g.loaded_wr, 16 * 5)
            pool.tensor_scalar(g.kvw_s[:], g.kvw[:], float((DN + DR) ** -0.5), None, ALU.mult).then_inc(g.kvw_scaled, 1)


class CausalHeads:

    UNITS = [(head, block) for head in range(2) for block in range(NT // 4)]
    NU = len(UNITS)
    S_JOBS = [[(q, k, min(k + 4, q + 1)) for q in range(4 * blk, 4 * blk + 4) for k in range(0, q + 1, 4)]
              for _, blk in UNITS]
    T_JOBS = [[(k, max(k, 4 * blk)) for k in range(4 * blk + 4)] for _, blk in UNITS]
    SLOTS_S, SLOTS_T = 2, 3
    AHEAD = 0.6
    BEHIND = 0.2
    EARLY = 0

    def __init__(self, b, g, width, space=None):
        self.g, self.width = g, width
        self.s_off, self.t_off = [0], [0]
        for s_jobs, t_jobs in zip(self.S_JOBS, self.T_JOBS):
            self.s_off.append(self.s_off[-1] + len(s_jobs))
            self.t_off.append(self.t_off[-1] + len(t_jobs))
        assert [blk for _, blk in self.UNITS] == [0, 1, 0, 1]
        self.NS, self.NTR = self.s_off[-1], self.t_off[-1]
        assert self.NS % self.SLOTS_S == 0 and self.NTR % self.SLOTS_T == 0
        rows = self.t_off[2]
        self.p = b.sb("p", [P, rows, 4 * P]) if space is None else \
            space[:, 0:rows * 4 * P].rearrange("p (k q) -> p k q", q=4 * P)
        self.p_row = [self.t_off[blk] for _, blk in self.UNITS]
        self.part = b.sb("part", [P, 4, 2])
        self.negmax = b.sb("negmax", [P, 2, 4])
        self.diag = b.sb("diag", [P, 2, 4, P], F32R)
        self.ones = b.sb("ones", [P, P], F32R)
        self.ps_s = b.ps("ps_s", [P, self.SLOTS_S, 512])
        self.ps_t = b.ps("ps_t", [P, self.SLOTS_T, 512])
        self.ps_u = b.ps("ps_u", [P, 2, 512])
        self.ones_done = b.sem("ones_done")
        self.scores_done = b.sem("scores_done")
        self.max_done = b.sem("max_done")
        self.joined = b.sem("joined")
        self.diag_done = b.sem("diag_done")
        self.trans_done = b.sem("trans_done")
        self.exp_done = b.sem("exp_done")
        self.value_done = b.sem("value_done")
        self.u_read = b.sem("u_read")

    def score_jobs(self, n, s, u, has_next):
        def unit(ahead):
            return (n, s, u + ahead) if u + ahead < self.NU else (n + 1, 1 - s, u + ahead - self.NU)
        found = []
        for ahead in (1, 2):
            if u + ahead >= self.NU and not has_next:
                continue
            m, t, w = unit(ahead)
            early = self.EARLY if self.UNITS[w][1] else 0
            jobs = range(early, len(self.S_JOBS[w])) if ahead == 1 else range(early)
            found += [(m, t, w, i) for i in jobs]
        return [((k + 0.2) / len(found) * self.AHEAD,) + job for k, job in enumerate(found)]

    def make_ones(self, v):
        v.tensor_scalar(self.ones[:], self.g.ident[:], 0.0, 1.0, ALU.mult, ALU.add).then_inc(self.ones_done, 1)

    def scores(self, pe, n, s, u, i, product, first):
        head = self.UNITS[u][0]
        q, k0, k1 = self.S_JOBS[u][i]
        job = self.s_off[u] + i
        if not (first and job < self.SLOTS_S):
            pe.wait_ge(self.max_done, self.NS * n + job - self.SLOTS_S + 1)
        out = self.ps_s[:, job % self.SLOTS_S, 0:(k1 - k0) * P]
        masked = k1 == q + 1
        mm = product(pe, out, s, head, q, k0, k1, not masked)
        if masked:
            mm = pe.matmul(out[:, (q - k0) * P:(q - k0 + 1) * P], self.g.ident_b[:], self.g.causal[:],
                           start=False, stop=True)
        mm.then_inc(self.scores_done, 1)

    def transposed(self, pe, n, s, u, i, product_t, first):
        head, blk = self.UNITS[u]
        k, q0 = self.T_JOBS[u][i]
        job = self.t_off[u] + i
        if i == 0:
            pe.wait_ge(self.diag_done, self.NU * n + u + 1)
        if not (first and job < self.SLOTS_T):
            pe.wait_ge(self.exp_done, self.NTR * n + job - self.SLOTS_T + 1)
        out = self.ps_t[:, job % self.SLOTS_T, (q0 - 4 * blk) * P:4 * P]
        product_t(pe, out, s, head, k, q0, 4 * blk + 4)
        masked = k >= 4 * blk
        mm = pe.matmul(out, self.ones[:], self.diag[:, u % 2, q0 - 4 * blk:4, :], start=False, stop=not masked)
        if masked:
            mm = pe.matmul(out[:, 0:P], self.g.causal[:], self.g.ident_b[:], start=False, stop=True)
        mm.then_inc(self.trans_done, 1)

    def values(self, pe, n, s, u, j, value, first):
        head, blk = self.UNITS[u]
        q = 4 * blk + j
        if j == 0 and not (first and u < 2):
            pe.wait_ge(self.u_read, self.NU * n + u - 1)
        pe.wait_ge(self.exp_done, self.NTR * n + self.t_off[u] + q + 1)
        for k in range(q + 1):
            mm = pe.matmul(self.ps_u[:, u % 2, j * self.width:(j + 1) * self.width],
                           self.p[:, self.p_row[u] + k, j * P:(j + 1) * P], value(s, head, k), start=(k == 0), stop=(k == q))
        if j == 3:
            mm.then_inc(self.value_done, 1)

    def tensor_step(self, pe, n, s, u, product, product_t, value, has_prev, has_next, first, extra=None):
        jobs = [((i + 0.3) / len(self.T_JOBS[u]), 1, i) for i in range(len(self.T_JOBS[u]))]
        prev = (n, s, u - 1) if u > 0 else (n - 1, 1 - s, self.NU - 1)
        scores = self.score_jobs(n, s, u, has_next)
        jobs += [(job[0], 0, k) for k, job in enumerate(scores)]
        if u > 0 or has_prev:
            jobs += [(self.BEHIND + (i + 0.5) / 4 * (1 - self.BEHIND), 2, i) for i in range(4)]
        if extra is not None:
            jobs.append((0.45, 3, 0))
        for _, kind, i in sorted(jobs):
            if kind == 0:
                _, m, t, w, j = scores[i]
                self.scores(pe, m, t, w, j, product, first and w > u)
            elif kind == 1:
                self.transposed(pe, n, s, u, i, product_t, first)
            elif kind == 2:
                self.values(pe, *prev, i, value, first)
            else:
                extra()

    def exponential(self, act, n, u, i, first):
        blk = self.UNITS[u][1]
        k, q0 = self.T_JOBS[u][i]
        job = self.t_off[u] + i
        if i == 0 and not (first and u < 2):
            act.wait_ge(self.value_done, self.NU * n + u - 1)
        act.wait_ge(self.trans_done, self.NTR * n + job + 1)
        cols = slice((q0 - 4 * blk) * P, 4 * P)
        act.activation(self.p[:, self.p_row[u] + k, cols], self.ps_t[:, job % self.SLOTS_T, cols],
                       ACT.Exp).then_inc(self.exp_done, 1)

    def maxima(self, v, n, u, first, part="all"):
        early = self.EARLY if self.UNITS[u][1] else 0
        start = early if part == "rest" else 0
        head, blk = self.UNITS[u]
        halves = blk > 0
        if start == 0 and not (first and u < 2):
            v.wait_ge(self.diag_done, self.NU * n + u - 1)
        if start == 0 and halves and not (first and head == 0):
            v.wait_ge(self.joined, 2 * n + head)
        for i, (q, k0, k1) in enumerate(self.S_JOBS[u]):
            if i < start or (part == "early" and i >= early):
                continue
            job = self.s_off[u] + i
            j = q - 4 * blk
            out = self.part[:, j, k0 // 4:k0 // 4 + 1] if halves else self.negmax[:, u % 2, j:j + 1]
            v.wait_ge(self.scores_done, self.NS * n + job + 1)
            v.tensor_reduce(out, self.ps_s[:, job % self.SLOTS_S, 0:(k1 - k0) * P], AX, ALU.max,
                            negate=True).then_inc(self.max_done, 1)
        if part == "early":
            return
        v.wait_ge(self.max_done, self.NS * n + self.s_off[u + 1])
        if halves:
            v.tensor_reduce(self.negmax[:, u % 2, :], self.part[:], AX, ALU.min).then_inc(self.joined, 1)
            v.wait_ge(self.joined, 2 * n + head + 1)
        if not (first and u < 2):
            behind = self.t_off[u - 1] if u >= 2 else self.t_off[self.NU + u - 1] - self.NTR
            v.wait_ge(self.trans_done, self.NTR * n + behind)
        v.tensor_tensor(self.diag[:, u % 2], self.g.ident[:].unsqueeze(1).broadcast_to([P, 4, P]),
                        self.negmax[:, u % 2, :].unsqueeze(2).broadcast_to([P, 4, P]),
                        ALU.mult).then_inc(self.diag_done, 1)

    def result(self, v, n, u, out):
        head, blk = self.UNITS[u]
        v.wait_ge(self.value_done, self.NU * n + u + 1)
        v.tensor_copy(out(n, head, 4 * blk), self.ps_u[:, u % 2, 0:4 * self.width].rearrange("p (q c) -> p q c", q=4)
                      ).then_inc(self.u_read, 1)

    def vector_step(self, v, n, u, out, has_prev, has_next, first):
        if u >= 2:
            self.result(v, n, u - 2, out)
        elif has_prev:
            self.result(v, n - 1, self.NU + u - 2, out)
        if u + 1 < self.NU:
            self.maxima(v, n, u + 1, first)
        elif has_next:
            self.maxima(v, n + 1, 0, False)

    def vector_end(self, v, n, out):
        for u in (self.NU - 2, self.NU - 1):
            self.result(v, n, u, out)


class NarrowHeads(CausalHeads):

    AHEAD = 0.6
    BEHIND = 0.2
    EARLY = 2
    WIDE = 64

    def __init__(self, b, g, width, space=None):
        super().__init__(b, g, width, space)
        self.ot = b.sb("ot", [P, 2, 4 * P])
        self.ps_o = b.ps("ps_o", [P, 4, P])
        self.ot_zero = b.sem("ot_zero")
        self.back_done = b.sem("back_done")
        self.back_read = b.sem("back_read")

    def values(self, pe, n, s, u, j, value, first):
        head, blk = self.UNITS[u]
        if j == 0 and not (first and u < 2):
            pe.wait_ge(self.u_read, self.NU * n + u - 1)
        for k in range(j * (blk + 1), (j + 1) * (blk + 1)):
            q0 = self.T_JOBS[u][k][1] - 4 * blk
            pe.wait_ge(self.exp_done, self.NTR * n + self.t_off[u] + k + 1)
            rows = slice(head * self.WIDE, head * self.WIDE + self.width)
            mm = pe.matmul(self.ps_u[rows, u % 2, q0 * P:4 * P], value(s, head, k),
                           self.p[:, self.p_row[u] + k, q0 * P:4 * P], start=(k == 0), stop=(k == 4 * blk + 3))
        if j == 3:
            mm.then_inc(self.value_done, 1)

    def transpose_back(self, pe, n, blk, first):
        pe.wait_ge(self.u_read, self.NU * n + 2 + blk + 1)
        if not (first and blk == 0):
            pe.wait_ge(self.back_read, 2 * n + blk)
        for q in range(4):
            mm = pe.transpose(self.ps_o[:, q, :], self.ot[:, blk, q * P:(q + 1) * P], self.g.ident[:])
        mm.then_inc(self.back_done, 1)

    def keep(self, act, n, u, first):
        head, blk = self.UNITS[u]
        rows = slice(head * self.WIDE, head * self.WIDE + self.width)
        act.wait_ge(self.value_done, self.NU * n + u + 1)
        if not first:
            act.wait_ge(self.back_done, 2 * n - 1 + blk)
        act.activation(self.ot[rows, blk, :], self.ps_u[rows, u % 2, :], ACT.Copy).then_inc(self.u_read, 1)

    def result(self, v, n, blk, out):
        v.wait_ge(self.back_done, 2 * n + blk + 1)
        v.tensor_copy(out(n, 4 * blk), self.ps_o[:].rearrange("p q (h c) -> p q h c", h=2)[:, :, :, 0:self.width]
                      ).then_inc(self.back_read, 1)

    def vector_step(self, v, n, u, out, has_prev, has_next, first):
        for ahead, part in ((1, "rest"), (2, "early")):
            w = u + ahead
            if w < self.NU:
                if part == "rest" or self.UNITS[w][1]:
                    self.maxima(v, n, w, first, part)
            elif has_next and (part == "rest" or self.UNITS[w - self.NU][1]):
                self.maxima(v, n + 1, w - self.NU, False, part)
        if u < 2 and has_prev:
            self.result(v, n - 1, u, out)


def double_pairs(eng, body):
    for s in range(2):
        body(s, s, s == 0, False)
    with eng.Fori(1, NP // 2 - 1) as j:
        for s in range(2):
            body(2 * j + s, s, False, False)
    for s in range(2):
        body(NP - 2 + s, s, False, s == 1)


def latent_heads(nc, g, dram):
    with ExitStack() as ctx:
        b = Bufs(nc, ctx, "a2")
        att = CausalHeads(b, g, KL + 1)
        wq0 = b.sb("wq0", [P, P])
        wq1 = b.sb("wq1", [QR1, P])
        q_h = b.sb("q_h", [P, 2, 2, T], F32R)
        q_l = b.sb("q_l", [P, 2, 2, T], F32R)
        waiter = b.sb("waiter", [1, 1])
        ps_q = b.ps("ps_q", [P, 512])
        wq_loaded = b.sem("wq_loaded")
        qabs_done = b.sem("qabs_done")
        q_hi = b.sem("q_hi")
        q_lo = b.sem("q_lo")
        rope_hi = b.sem("rope_hi")
        rope_lo = b.sem("rope_lo")
        block = ctx.enter_context(nc.Block())

        @block.sync
        def _(sp):
            def load(p, first):
                if not first:
                    sp.wait_ge(qabs_done, 2 * p)
                sp.dma_start(wq0[:], g.wq[:, ds(p, 1), 0:P].squeeze(1)).then_inc(wq_loaded, 16)
                sp.dma_start(wq1[:], g.wq[0:QR1, ds(p, 1), P:2 * P].squeeze(1)).then_inc(wq_loaded, 16)
            load(0, True)
            load(1, False)
            sp.dma_start(g.w1_raw, dram["w1"]).then_inc(g.loaded_w1, 16)
            with sp.Fori(2, NP) as p:
                load(p, False)

        @block.tensor
        def _(pe):
            def product(pe, out, s, head, q, k0, k1, stop):
                return pe.matmul(out, q_h[:, s, head, q * P:(q + 1) * P], g.kt_h[:, head, k0 * P:k1 * P],
                                 start=True, stop=stop)

            def product_t(pe, out, s, head, k, q0, q1):
                keys, cols = slice(k * P, (k + 1) * P), slice(q0 * P, q1 * P)
                split3(pe, out, (g.kt_h[:, head, keys], g.kt_l[:, head, keys]),
                       (q_h[:, s, head, cols], q_l[:, s, head, cols]), True, False)

            def queries(p, half, first):
                if half == 0:
                    pe.wait_ge(wq_loaded, 32 * p + 32)
                if not (first and half == 0):
                    pe.wait_ge(q_lo, 4 * p + 2 * half)
                cols = slice(half * 512, (half + 1) * 512)
                pe.matmul(ps_q[:], wq0[:], g.qat0[:, cols], start=True, stop=False)
                pe.matmul(ps_q[:], wq1[:], g.qat1[:, cols], start=False, stop=True).then_inc(qabs_done, 1)

            def queries_ready(p, halves=2):
                pe.wait_ge(q_hi, 4 * p + 2 * halves)
                pe.wait_ge(q_lo, 4 * p + 2 * halves)
                pe.wait_ge(rope_hi, 2 * p + 2)
                pe.wait_ge(rope_lo, 2 * p + 2)

            def pair(n, s, first, last):
                for u in range(att.NU):
                    if u == att.NU - 1 and not last:
                        queries_ready(n + 1)
                    extra = (lambda: queries(n + 1, u // 2, False)) if u % 2 == 0 and not last else None
                    att.tensor_step(pe, n, s, u, product, product_t, lambda s, head, k: g.vext[:, k, :],
                                    not first, not last, first, extra)

            queries(0, 0, True)
            pe.wait_ge(g.loaded_const, 16 * g.N_CONST)
            pe.wait_ge(att.ones_done, 1)
            queries_ready(0, 1)
            for i in range(len(att.S_JOBS[0])):
                att.scores(pe, 0, 0, 0, i, product, True)
            queries(0, 1, True)
            queries_ready(0)
            double_pairs(pe, pair)
            for j in range(4):
                att.values(pe, NP - 1, 1, att.NU - 1, j, lambda s, head, k: g.vext[:, k, :], False)

        @block.scalar
        def _(act):
            def high(p, s, half, first):
                if half == 0 and not first:
                    act.wait_ge(att.trans_done, att.NTR * (p - 1))
                cols = slice(half * 512, (half + 1) * 512)
                act.wait_ge(qabs_done, 2 * p + half + 1)
                act.activation(q_h[KL:P, s, 0, cols], ps_q[KL:P, :], ACT.Copy,
                               scale=g.kvw_s[KL:P, 0:1]).then_inc(q_hi, 1)
                act.activation(q_h[0:KL, s, 1, cols], ps_q[0:KL, :], ACT.Copy,
                               scale=g.kvw_s[0:KL, 0:1]).then_inc(q_hi, 1)

            def pair(n, s, first, last):
                for u in range(att.NU):
                    jobs = len(att.T_JOBS[u])
                    for i in range(jobs):
                        if i == jobs - 2 and u % 2 == 0 and not last:
                            high(n + 1, 1 - s, u // 2, first)
                        att.exponential(act, n, u, i, first)
            for head, rows in ((0, slice(0, DR)), (1, slice(DR, P))):
                act.activation(q_h[rows, 0, head, :], g.qrt[rows, 0, :], ACT.Copy).then_inc(rope_hi, 1)
            act.wait_ge(g.kvw_scaled, 1)
            for half in range(2):
                high(0, 0, half, True)
            double_pairs(act, pair)

        @block.vector
        def _(v):
            def low(p, s, half):
                cols = slice(half * 512, (half + 1) * 512)
                v.wait_ge(q_hi, 4 * p + 2 * half + 2)
                v.scalar_tensor_tensor(q_l[KL:P, s, 0, cols], ps_q[KL:P, :], g.kvw_s[KL:P, 0:1],
                                       q_h[KL:P, s, 0, cols].bitcast(F32), ALU.mult, ALU.subtract).then_inc(q_lo, 1)
                v.scalar_tensor_tensor(q_l[0:KL, s, 1, cols], ps_q[0:KL, :], g.kvw_s[0:KL, 0:1],
                                       q_h[0:KL, s, 1, cols].bitcast(F32), ALU.mult, ALU.subtract).then_inc(q_lo, 1)

            def out(n, head, q0):
                return g.u[:, q0:q0 + 4, ds(2 * n + head, 1), :].squeeze(2)

            def pair(n, s, first, last):
                for u in range(att.NU):
                    att.vector_step(v, n, u, out, not first, not last, first)
                    if u % 2 == 0 and not last:
                        low(n + 1, 1 - s, u // 2)
            att.make_ones(v)
            v.wait_ge(rope_hi, 2)
            for head, rows in ((0, slice(0, DR)), (1, slice(DR, P))):
                v.tensor_tensor(q_l[rows, 0, head, :], g.qrt[rows, 0, :], q_h[rows, 0, head, :].bitcast(F32),
                                ALU.subtract).then_inc(rope_lo, 1)
            low(0, 0, 0)
            att.maxima(v, 0, 0, True)
            low(0, 0, 1)
            double_pairs(v, pair)
            att.vector_end(v, NP - 1, out)

        @block.gpsimd
        def _(pool):
            def rope_rows(p, s, first):
                if not first:
                    pool.wait_ge(att.trans_done, att.NTR * (p - 1))
                    pool.tensor_tensor(waiter[:], g.neg_half[0:1, 0:1], g.neg_half[0:1, 0:1], ALU.add)
                for head, rows in ((0, slice(0, DR)), (1, slice(DR, P))):
                    pool.tensor_copy(q_h[rows, s, head, :], g.qrt[rows, ds(p, 1), :].squeeze(1)).then_inc(rope_hi, 1)
                pool.wait_ge(rope_hi, 2 * p + 2)
                pool.tensor_tensor(waiter[:], g.neg_half[0:1, 0:1], g.neg_half[0:1, 0:1], ALU.add)
                for head, rows in ((0, slice(0, DR)), (1, slice(DR, P))):
                    pool.tensor_tensor(q_l[rows, s, head, :], g.qrt[rows, ds(p, 1), :].squeeze(1),
                                       q_h[rows, s, head, :].bitcast(F32), ALU.subtract).then_inc(rope_lo, 1)
            pool.wait_ge(rope_lo, 2)
            rope_rows(1, 1, True)
            with pool.Fori(1, NP // 2) as j:
                for s in range(2):
                    rope_rows(2 * j + s, s, False)


def latent_output(nc, g, dram, w2_raw):
    CH = W1_N // NT
    with ExitStack() as ctx:
        b = Bufs(nc, ctx, "a3")
        rden = b.sb("rden", [P, H])
        un = b.sb("un", [P, H * KL])
        ut = b.sb("ut", [P, NP, P])
        ps_t = b.ps("ps_t", [P, 2, 512])
        ps_y = b.ps("ps_y", [P, 512])
        rden_done = b.sem("rden_done")
        un_done = b.sem("un_done")
        un_t_done = b.sem("un_t_done")
        ut_by_scalar = b.sem("ut_by_scalar")
        ut_by_vector = b.sem("ut_by_vector")
        y_done = b.sem("y_done")
        y_added = b.sem("y_added")
        w1_hi = b.sem("w1_hi")
        w1_lo = b.sem("w1_lo")
        w2_hi = b.sem("w2_hi")
        w2_lo = b.sem("w2_lo")
        block = ctx.enter_context(nc.Block())

        @block.sync
        def _(sp):
            sp.dma_start(w2_raw[:, 0:NF - 1, :], dram["w2"][0:(NF - 1) * P, :]
                         .rearrange("(k p) d -> p k d", p=P)).then_inc(g.loaded_w2, 16)
            sp.dma_start(w2_raw[0:FTAIL, NF - 1, :], dram["w2"][(NF - 1) * P:FH, :]).then_inc(g.loaded_w2, 16)

        @block.gpsimd
        def _(pool):
            pool.wait_ge(g.loaded_w2, 32)
            parts = [(slice(0, P), slice(0, NF - 1)), (slice(0, FTAIL), slice(NF - 1, NF))]
            for n, (rows, ks) in enumerate(parts):
                pool.tensor_copy(g.w2_h[rows, ks, :], w2_raw[rows, ks, :]).then_inc(w2_hi, 1)
                pool.wait_ge(w2_hi, n + 1)
                pool.tensor_tensor(g.w2_l[rows, ks, :], w2_raw[rows, ks, :], g.w2_h[rows, ks, :].bitcast(F32),
                                   ALU.subtract).then_inc(w2_lo, 1)

        @block.tensor
        def _(pe):
            def step(i, one, two, least):
                if one:
                    pe.wait_ge(un_done, i + 1)
                    if least >= 1:
                        pe.wait_ge(ut_by_scalar, i)
                        pe.wait_ge(ut_by_vector, i)
                    for c in range(NP):
                        mm = pe.transpose(ps_t[:, c // 4, (c % 4) * P:(c % 4 + 1) * P], un[:, c * P:(c + 1) * P],
                                          g.ident[:])
                    mm.then_inc(un_t_done, 1)
                    pe.wait_ge(ut_by_scalar, i + 1)
                    pe.wait_ge(ut_by_vector, i + 1)
                    if least >= 1:
                        pe.wait_ge(y_added, i)
                    for c in range(NP):
                        mm = pe.matmul(ps_y[:, 0:D], ut[:, c, :], g.wvo[:, c, :], start=(c == 0), stop=(c == NP - 1))
                    mm.then_inc(y_done, 1)
            staged(2, pe, step)

        @block.scalar
        def _(act):
            def step(i, one, two, least):
                if one:
                    act.wait_ge(un_t_done, i + 1)
                    if least >= 1:
                        act.wait_ge(y_done, i)
                    act.activation(ut[:, 0:4, :], ps_t[:, 0, :].rearrange("p (k c) -> p k c", c=P),
                                   ACT.Copy).then_inc(ut_by_scalar, 1)
                    act.activation(g.w1_h[:, :, ds(i * CH, CH)], g.w1_raw[:, :, ds(i * CH, CH)], ACT.Copy).then_inc(w1_hi, 1)
            act.wait_ge(g.loaded_w1, 16)
            staged(2, act, step)

        @block.vector
        def _(v):
            def step(i, one, two, least):
                if one:
                    v.reciprocal(rden[:], g.u[:, ds(i, 1), :, KL].squeeze(1)).then_inc(rden_done, 1)
                    v.wait_ge(rden_done, i + 1)
                    if least >= 1:
                        v.wait_ge(un_t_done, i)
                    v.tensor_tensor(un[:].rearrange("p (h c) -> p h c", c=KL), g.u[:, ds(i, 1), :, 0:KL].squeeze(1),
                                    rden[:].unsqueeze(2).broadcast_to([P, H, KL]), ALU.mult).then_inc(un_done, 1)
                if two:
                    t = i - 1
                    v.wait_ge(y_done, t + 1)
                    v.tensor_tensor(g.X[:, ds(t * D, D)], g.X[:, ds(t * D, D)], ps_y[:, 0:D],
                                    ALU.add).then_inc(y_added, 1)
                if one:
                    v.wait_ge(un_t_done, i + 1)
                    v.tensor_copy(ut[:, 4:8, :], ps_t[:, 1, :].rearrange("p (k c) -> p k c", c=P))\
                        .then_inc(ut_by_vector, 1)
                    v.wait_ge(w1_hi, i + 1)
                    v.tensor_tensor(g.w1_l[:, :, ds(i * CH, CH)], g.w1_raw[:, :, ds(i * CH, CH)],
                                    g.w1_h[:, :, ds(i * CH, CH)].bitcast(F32), ALU.subtract).then_inc(w1_lo, 1)
            staged(2, v, step)


def experts(nc, g, tag, ahead=None):
    NBLK = NE + 1
    with ExitStack() as ctx:
        b = Bufs(nc, ctx, tag)
        ln = LayerNorm(b, g)
        xt_h = b.sb("xt_h", [P, KD * P], F32R)
        xt_l = b.sb("xt_l", [P, KD * P], F32R)
        silu = b.sb("silu", [P, 2, FI])
        hid = b.sb("hid", [P, FH])
        hid_h = b.sb("hid_h", [P, NF, P], F32R)
        hid_l = b.sb("hid_l", [P, NF, P], F32R)
        logits = b.sb("logits", [P, NE])
        top = b.sb("top", [P, 8])
        top_at = b.sb("top_at", [P, 8], mybir.dt.uint32)
        top_atf = b.sb("top_atf", [P, 2])
        neg_top = b.sb("neg_top", [P, 1])
        expert_no = b.sb("expert_no", [P, NE])
        expo = b.sb("expo", [P, NE])
        expo_sum = b.sb("expo_sum", [P, 1])
        first_w = b.sb("first_w", [P, NE])
        second_w = b.sb("second_w", [P, NE])
        both_w = b.sb("both_w", [P, NE])
        pair_sum = b.sb("pair_sum", [P, 1])
        den = b.sb("den", [P, 1])
        rden = b.sb("rden", [P, 1])
        comb = b.sb("comb", [P, NE])
        ps_b = b.ps("ps_b", [P, 4, 512])
        ps_x = b.ps("ps_x", [P, 512])
        ps_h = b.ps("ps_h", [P, 2, 512])
        ps_y = b.ps("ps_y", [P, 512])
        numbered = b.sem("numbered")
        xt_hi = b.sem("xt_hi")
        xt_lo = b.sem("xt_lo")
        block_done = b.sem("block_done")
        silu_done = b.sem("silu_done")
        hid_done = b.sem("hid_done")
        hid_t_done = b.sem("hid_t_done")
        hid_hi = b.sem("hid_hi")
        hid_lo = b.sem("hid_lo")
        y_done = b.sem("y_done")
        y_added = b.sem("y_added")
        logits_done = b.sem("logits_done")
        router = b.sem("router")
        expo_done = b.sem("expo_done")
        den_done = b.sem("den_done")
        comb_done = b.sem("comb_done")
        ROUTER = 8
        block = ctx.enter_context(nc.Block())
        col = lambda k: 0 if k == 0 else BLK + NE + (k - 1) * BLK
        wid = lambda k: BLK + NE if k == 0 else BLK
        groups = [(0, 4), (4, 8), (8, 11), (11, NF)]

        if ahead is not None:
            @block.sync
            def _(sp):
                ahead(sp)

        def slot_before(k, slots):
            if k >= slots:
                return k - slots
            return max(j for j in range(NBLK) if j % slots == k % slots) - NBLK

        def tiles(eng, step):
            step(0, True, False)
            with eng.Fori(1, NT - 1) as t:
                step(t, False, False)
            step(NT - 1, False, True)

        @block.tensor
        def _(pe):
            def transposed_input(t, first):
                if not first:
                    pe.wait_ge(xt_hi, t)
                    pe.wait_ge(xt_lo, t)
                ln.tensor_transpose(pe, ps_x, t)

            def transposes(t, n, first):
                k0, k1 = groups[n]
                need = min(NBLK, -(-k1 * P // FI))
                pe.wait_ge(hid_done, NBLK * t + need)
                if n >= 2 or not first:
                    pe.wait_ge(hid_lo, 4 * t + n - 1)
                for k in range(k0, k1):
                    m = min(P, FH - k * P)
                    mm = pe.transpose(ps_h[0:m, n % 2, (k - k0) * P:(k - k0 + 1) * P], hid[:, k * P:k * P + m], g.ident[:])
                mm.then_inc(hid_t_done, 1)

            def outputs(t, k0, k1):
                for k in range(k0, k1):
                    m = min(P, FH - k * P)
                    mm = split3(pe, ps_y[:, 0:D], (hid_h[0:m, k, :], hid_l[0:m, k, :]),
                                (g.w2_h[0:m, k, :], g.w2_l[0:m, k, :]), k == 0, k == NF - 1)
                return mm

            def last_outputs(t):
                pe.wait_ge(hid_lo, 4 * t + 4)
                outputs(t, 8, NF).then_inc(y_done, 1)

            def step(t, first, last):
                pe.wait_ge(xt_hi, t + 1)
                pe.wait_ge(xt_lo, t + 1)
                for k in range(NBLK):
                    if not (first and k < 4):
                        pe.wait_ge(hid_done, NBLK * t + slot_before(k, 4) + 1)
                    for c in range(KD):
                        cs, ws = slice(c * P, (c + 1) * P), slice(col(k), col(k) + wid(k))
                        mm = split3(pe, ps_b[:, k % 4, 0:wid(k)], (xt_h[:, cs], xt_l[:, cs]),
                                    (g.w1_h[:, c, ws], g.w1_l[:, c, ws]), c == 0, c == KD - 1)
                    mm.then_inc(block_done, 1)
                    if k == 2 and not first:
                        last_outputs(t - 1)
                    if k == 5:
                        transposes(t, 0, first)
                    if k == 7:
                        transposes(t, 1, first)
                if not last:
                    transposed_input(t + 1, False)
                if not first:
                    pe.wait_ge(y_added, t)
                transposes(t, 2, first)
                pe.wait_ge(hid_lo, 4 * t + 1)
                outputs(t, 0, 4)
                transposes(t, 3, first)
                pe.wait_ge(hid_lo, 4 * t + 2)
                outputs(t, 4, 8)
            transposed_input(0, True)
            tiles(pe, step)
            last_outputs(NT - 1)

        @block.scalar
        def _(act):
            def transposed_high(t, first):
                act.wait_ge(ln.xn_read, t + 1)
                if not first:
                    act.wait_ge(block_done, NBLK * t)
                act.activation(xt_h[:], ps_x[:, 0:KD * P], ACT.Copy).then_inc(xt_hi, 1)

            def high_group(t, n, first):
                k0, k1 = groups[n]
                act.wait_ge(hid_t_done, 4 * t + n + 1)
                if not first:
                    act.wait_ge(y_done, t)
                m = min(P, FH - k0 * P)
                act.activation(hid_h[0:m, k0:k1, :], ps_h[0:m, n % 2, 0:(k1 - k0) * P].rearrange("p (k c) -> p k c", c=P),
                               ACT.Copy).then_inc(hid_hi, 1)

            def step(t, first, last):
                for k in range(NBLK):
                    act.wait_ge(block_done, NBLK * t + k + 1)
                    if not (first and k < 2):
                        act.wait_ge(hid_done, NBLK * t + slot_before(k, 2) + 1)
                    act.activation(silu[:, k % 2, :], ps_b[:, k % 4, 0:FI], ACT.Silu).then_inc(silu_done, 1)
                    if k == 0:
                        act.wait_ge(router, ROUTER * t + 3)
                        if not first:
                            act.wait_ge(comb_done, t)
                        act.activation(expo[:], logits[:], ACT.Exp, bias=neg_top[:, 0:1],
                                       accum_out=expo_sum[:]).then_inc(expo_done, 1)
                    if k == 5:
                        high_group(t, 0, first)
                    if k == 7:
                        high_group(t, 1, first)
                if not last:
                    transposed_high(t + 1, False)
                high_group(t, 2, first)
                high_group(t, 3, first)
            transposed_high(0, True)
            tiles(act, step)

        @block.vector
        def _(v):
            def transposed_low(t, first):
                v.wait_ge(xt_hi, t + 1)
                v.tensor_tensor(xt_l[:], ps_x[:, 0:KD * P], xt_h[:].bitcast(F32), ALU.subtract).then_inc(xt_lo, 1)

            def gated(t, k, first):
                v.wait_ge(silu_done, NBLK * t + k + 1)
                if k == 0 and not first:
                    v.wait_ge(hid_t_done, 4 * t)
                out, up = hid[:, k * FI:(k + 1) * FI], ps_b[:, k % 4, FI:BLK]
                if k == 0:
                    v.tensor_tensor(out, up, silu[:, 0, :], ALU.mult).then_inc(hid_done, 1)
                else:
                    if k == 1:
                        v.wait_ge(comb_done, t + 1)
                    v.scalar_tensor_tensor(out, up, comb[:, k - 1:k], silu[:, k % 2, :], ALU.mult,
                                           ALU.mult).then_inc(hid_done, 1)

            def low_group(t, n, first):
                k0, k1 = groups[n]
                m = min(P, FH - k0 * P)
                v.wait_ge(hid_hi, 4 * t + n + 1)
                if not first:
                    v.wait_ge(y_done, t)
                v.tensor_tensor(hid_l[0:m, k0:k1, :], ps_h[0:m, n % 2, 0:(k1 - k0) * P].rearrange("p (k c) -> p k c", c=P),
                                hid_h[0:m, k0:k1, :].bitcast(F32), ALU.subtract).then_inc(hid_lo, 1)

            def route(t):
                def after(n):
                    v.wait_ge(router, ROUTER * t + n)
                v.wait_ge(logits_done, t + 1)
                v.memset(ln.waiter[:], 0.0)
                v.max(top[:], logits[:]).then_inc(router, 1)
                after(1)
                v.memset(ln.waiter[:], 0.0)
                v.max_index(top_at[:], top[:], logits[:]).then_inc(router, 1)
                v.tensor_scalar(neg_top[:], top[:, 0:1], -1.0, None, ALU.mult).then_inc(router, 1)
                after(2)
                v.tensor_copy(top_atf[:], top_at[:, 0:2]).then_inc(router, 1)
                after(4)
                v.wait_ge(expo_done, t + 1)
                v.scalar_tensor_tensor(first_w[:], expert_no[:], top_atf[:, 0:1], expo[:], ALU.is_equal,
                                       ALU.mult).then_inc(router, 1)
                v.scalar_tensor_tensor(second_w[:], expert_no[:], top_atf[:, 1:2], expo[:], ALU.is_equal,
                                       ALU.mult).then_inc(router, 1)
                after(6)
                v.tensor_tensor(both_w[:], first_w[:], second_w[:], ALU.add).then_inc(router, 1)
                after(7)
                v.tensor_reduce(pair_sum[:], both_w[:], AX, ALU.add).then_inc(router, 1)
                after(8)
                v.scalar_tensor_tensor(den[:], expo_sum[:], 1e-20, pair_sum[:], ALU.mult, ALU.add).then_inc(den_done, 1)
                v.wait_ge(den_done, 2 * t + 1)
                v.reciprocal(rden[:], den[:]).then_inc(den_done, 1)
                v.wait_ge(den_done, 2 * t + 2)
                v.tensor_scalar(comb[:], both_w[:], rden[:, 0:1], None, ALU.mult).then_inc(comb_done, 1)

            def step(t, first, last):
                v.wait_ge(block_done, NBLK * t + 1)
                v.wait_ge(silu_done, NBLK * t + 1)
                v.tensor_copy(logits[:], ps_b[:, 0, BLK:BLK + NE]).then_inc(logits_done, 1)
                gated(t, 0, first)
                route(t)
                for k in range(1, NBLK):
                    gated(t, k, first)
                    if not last and k == 2:
                        ln.vector_stats(v, t + 1, t + 1)
                    if not last and k == 4:
                        ln.vector_scale(v, t + 1, t + 1, False)
                    if k == 4 and not first:
                        add(t - 1)
                    if k == 6:
                        low_group(t, 0, first)
                low_group(t, 1, first)
                if not last:
                    transposed_low(t + 1, False)
                low_group(t, 2, first)
                low_group(t, 3, first)

            def add(t):
                v.wait_ge(y_done, t + 1)
                v.tensor_tensor(g.X[:, ds(t * D, D)], g.X[:, ds(t * D, D)], ps_y[:, 0:D], ALU.add).then_inc(y_added, 1)

            v.wait_ge(numbered, 1)
            ln.vector_stats(v, 0, 0)
            ln.vector_scale(v, 0, 0, True)
            transposed_low(0, True)
            tiles(v, step)
            add(NT - 1)

        @block.gpsimd
        def _(pool):
            pool.iota(expert_no[:], pattern=[[1, NE]], base=0, channel_multiplier=0,
                      allow_small_or_imprecise_dtypes=True).then_inc(numbered, 1)
            ln.gpsimd_power(pool, 0)
            with pool.Fori(1, NT) as t:
                ln.gpsimd_power(pool, t)


def plain_attention(nc, g, dram):
    with ExitStack() as ctx:
        b = Bufs(nc, ctx, "b")
        xt_h = b.sb("xt_h", [P, KD, T], F32R)
        xt_l = b.sb("xt_l", [P, KD, T], F32R)
        wqk_h = b.sb("wqk_h", [P, KD, D], F32R)
        wqk_l = b.sb("wqk_l", [P, KD, D], F32R)
        wvo_h = b.sb("wvo_h", [P, KD, D], F32R)
        wvo_l = b.sb("wvo_l", [P, KD, D], F32R)
        vo = b.sb("vo", [P, NT, D])
        keys_and_values(nc, g, dram, xt_h, xt_l, wqk_h, wqk_l, wvo_h, wvo_l, vo)
        plain_queries(nc, g, xt_h, xt_l, wqk_h, wqk_l, vo)


def keys_and_values(nc, g, dram, xt_h, xt_l, wqk_h, wqk_l, wvo_h, wvo_l, vo):
    with ExitStack() as ctx:
        b = Bufs(nc, ctx, "bk")
        ln = LayerNorm(b, g)
        w = g.wb
        xs_h = b.sb("xs_h", [P, KD, P], F32R)
        xs_l = b.sb("xs_l", [P, KD, P], F32R)
        ps_w = b.ps("ps_w", [P, 2, 512])
        ps_x = b.ps("ps_x", [P, 512])
        ps_v = b.ps("ps_v", [P, 512])
        w_done = b.sem("w_done")
        w_hi = b.sem("w_hi")
        w_lo = b.sem("w_lo")
        xt_hi = b.sem("xt_hi")
        xt_lo = b.sem("xt_lo")
        xt_kept = b.sem("xt_kept")
        vo_done = b.sem("vo_done")
        vo_copied = b.sem("vo_copied")
        block = ctx.enter_context(nc.Block())

        @block.tensor
        def _(pe):
            pe.wait_ge(g.loaded_wb, 16)
            for n, (left, right) in enumerate(((0, 1), (2, 3))):
                for m in range(KD):
                    for c in range(KD):
                        mm = pe.matmul(ps_w[:, n, m * D:(m + 1) * D], w[:, left, c, m * P:(m + 1) * P],
                                       w[:, right, c, :], start=(c == 0), stop=(c == KD - 1))
                mm.then_inc(w_done, 1)

            def step(t, one, least):
                if least >= 1:
                    pe.wait_ge(xt_lo, t)
                ln.tensor_transpose(pe, ps_x, t)
                pe.wait_ge(xt_hi, t + 1)
                pe.wait_ge(xt_lo, t + 1)
                if least == 0:
                    pe.wait_ge(w_lo, 2)
                else:
                    pe.wait_ge(vo_copied, t)
                for c in range(KD):
                    mm = split3(pe, ps_v[:, 0:D], (xs_h[:, c, :], xs_l[:, c, :]), (wvo_h[:, c, :], wvo_l[:, c, :]),
                                c == 0, c == KD - 1)
                mm.then_inc(vo_done, 1)
            staged(1, pe, step)

        @block.scalar
        def _(act):
            for n, (hi, scale) in enumerate(((wqk_h, D ** -0.5), (wvo_h, 1.0))):
                act.wait_ge(w_done, n + 1)
                act.activation(hi[:], ps_w[:, n, :].rearrange("p (m c) -> p m c", m=KD), ACT.Copy,
                               scale=scale).then_inc(w_hi, 1)

            def step(t, one, least):
                act.wait_ge(ln.xn_read, t + 1)
                if least >= 1:
                    act.wait_ge(vo_done, t)
                    act.wait_ge(xt_kept, 2 * t)
                act.activation(xs_h[:], ps_x[:, 0:KD * P].rearrange("p (m c) -> p m c", m=KD),
                               ACT.Copy).then_inc(xt_hi, 1)
                act.wait_ge(vo_done, t + 1)
                act.activation(vo[:, ds(t, 1), :].squeeze(1), ps_v[:, 0:D], ACT.Copy).then_inc(vo_copied, 1)
            staged(1, act, step)

        @block.vector
        def _(v):
            ln.vector_stats(v, 0, 0)
            ln.vector_scale(v, 0, 0, True)
            for n, (hi, lo, scale) in enumerate(((wqk_h, wqk_l, D ** -0.5), (wvo_h, wvo_l, 1.0))):
                v.wait_ge(w_hi, n + 1)
                v.scalar_tensor_tensor(lo[:], ps_w[:, n, :].rearrange("p (m c) -> p m c", m=KD), scale,
                                       hi[:].bitcast(F32), ALU.mult, ALU.subtract).then_inc(w_lo, 1)

            def low(t):
                v.wait_ge(xt_hi, t + 1)
                v.tensor_tensor(xs_l[:], ps_x[:, 0:KD * P].rearrange("p (m c) -> p m c", m=KD),
                                xs_h[:].bitcast(F32), ALU.subtract).then_inc(xt_lo, 1)

            def step(t):
                ln.vector_stats(v, t + 1, t + 1)
                low(t)
                ln.vector_scale(v, t + 1, t + 1, False)
            step(0)
            with v.Fori(1, NT - 1) as t:
                step(t)
            low(NT - 1)

        @block.gpsimd
        def _(pool):
            def step(t, one, least):
                if least == 0:
                    ln.gpsimd_power(pool, 0)
                    ln.gpsimd_power(pool, 1)
                pool.wait_ge(xt_lo, t + 1)
                pool.tensor_copy(xt_h[:, :, ds(t * P, P)], xs_h[:]).then_inc(xt_kept, 1)
                pool.tensor_copy(xt_l[:, :, ds(t * P, P)], xs_l[:]).then_inc(xt_kept, 1)
            step(0, True, 0)
            with pool.Fori(1, NT - 1) as t:
                ln.gpsimd_power(pool, t + 1)
                step(t, True, 1)
            step(NT - 1, True, 1)


def plain_queries(nc, g, xt_h, xt_l, wqk_h, wqk_l, vo):
    with ExitStack() as ctx:
        b = Bufs(nc, ctx, "bq")
        qt_h = b.sb("qt_h", [P, KD, P], F32R)
        qt_l = b.sb("qt_l", [P, KD, P], F32R)
        negmax = b.sb("negmax", [P, 1])
        wsum = b.sb("wsum", [P, 1])
        rsum = b.sb("rsum", [P, 1])
        p = b.sb("p", [P, T])
        pt = b.sb("pt", [P, NT, P])
        ps_q = b.ps("ps_q", [P, 512])
        ps_s = b.ps("ps_s", [P, 2, 512])
        ps_t = b.ps("ps_t", [P, 2, 512])
        ps_y = b.ps("ps_y", [P, 512])
        q_done = b.sem("q_done")
        q_hi = b.sem("q_hi")
        q_lo = b.sem("q_lo")
        scores_done = b.sem("scores_done")
        max_done = b.sem("max_done")
        exp_done = b.sem("exp_done")
        rsum_done = b.sem("rsum_done")
        p_t_done = b.sem("p_t_done")
        pt_by_scalar = b.sem("pt_by_scalar")
        pt_by_vector = b.sem("pt_by_vector")
        y_done = b.sem("y_done")
        y_added = b.sem("y_added")
        block = ctx.enter_context(nc.Block())

        @block.tensor
        def _(pe):
            def step(i, one, two, least):
                if one:
                    if least >= 1:
                        pe.wait_ge(q_lo, i)
                    for m in range(KD):
                        for c in range(KD):
                            tokens = ds(i * P, P)
                            mm = split3(pe, ps_q[:, m * P:(m + 1) * P],
                                        (wqk_h[:, c, m * P:(m + 1) * P], wqk_l[:, c, m * P:(m + 1) * P]),
                                        (xt_h[:, c, tokens], xt_l[:, c, tokens]), c == 0, c == KD - 1)
                    mm.then_inc(q_done, 1)
                if two:
                    t = i - 1
                    pe.wait_ge(exp_done, t + 1)
                    if least >= 2:
                        pe.wait_ge(pt_by_scalar, t)
                        pe.wait_ge(pt_by_vector, t)
                    for k in range(NT):
                        mm = pe.transpose(ps_t[:, k // 4, (k % 4) * P:(k % 4 + 1) * P], p[:, k * P:(k + 1) * P],
                                          g.ident[:])
                    mm.then_inc(p_t_done, 1)
                if one:
                    pe.wait_ge(q_hi, i + 1)
                    pe.wait_ge(q_lo, i + 1)
                    for n in range(2):
                        cols = slice(n * 512, (n + 1) * 512)
                        for c in range(KD):
                            mm = split3(pe, ps_s[:, n, :], (qt_h[:, c, :], qt_l[:, c, :]),
                                        (xt_h[:, c, cols], xt_l[:, c, cols]), c == 0, c == KD - 1)
                    mm.then_inc(scores_done, 1)
                if two:
                    t = i - 1
                    pe.wait_ge(pt_by_scalar, t + 1)
                    pe.wait_ge(pt_by_vector, t + 1)
                    if least >= 2:
                        pe.wait_ge(y_added, t)
                    for k in range(NT):
                        mm = pe.matmul(ps_y[:, 0:D], pt[:, k, :], vo[:, k, :], start=(k == 0), stop=(k == NT - 1))
                    mm.then_inc(y_done, 1)
            staged(2, pe, step)

        @block.scalar
        def _(act):
            def step(i, one, two, least):
                if one:
                    act.wait_ge(q_done, i + 1)
                    if least >= 1:
                        act.wait_ge(scores_done, i)
                    act.activation(qt_h[:], ps_q[:, 0:KD * P].rearrange("p (m c) -> p m c", m=KD),
                                   ACT.Copy).then_inc(q_hi, 1)
                if two:
                    t = i - 1
                    act.wait_ge(p_t_done, t + 1)
                    if least >= 2:
                        act.wait_ge(y_done, t)
                    act.activation(pt[:, 0:4, :], ps_t[:, 0, :].rearrange("p (k c) -> p k c", c=P),
                                   ACT.Copy).then_inc(pt_by_scalar, 1)
                if one:
                    act.wait_ge(max_done, i + 1)
                    if least >= 1:
                        act.wait_ge(rsum_done, i)
                    act.activation(p[:], ps_s[:].rearrange("p a c -> p (a c)"), ACT.Exp, bias=negmax[:, 0:1],
                                   accum_out=wsum[:]).then_inc(exp_done, 1)
            staged(2, act, step)

        @block.vector
        def _(v):
            def step(i, one, two, least):
                if one:
                    v.wait_ge(q_hi, i + 1)
                    v.tensor_tensor(qt_l[:], ps_q[:, 0:KD * P].rearrange("p (m c) -> p m c", m=KD),
                                    qt_h[:].bitcast(F32), ALU.subtract).then_inc(q_lo, 1)
                if two:
                    t = i - 1
                    v.wait_ge(p_t_done, t + 1)
                    if least >= 2:
                        v.wait_ge(y_done, t)
                    v.tensor_copy(pt[:, 4:8, :], ps_t[:, 1, :].rearrange("p (k c) -> p k c", c=P))\
                        .then_inc(pt_by_vector, 1)
                if one:
                    v.wait_ge(scores_done, i + 1)
                    v.tensor_reduce(negmax[:], ps_s[:].rearrange("p a c -> p (a c)"), AX, ALU.max,
                                    negate=True).then_inc(max_done, 1)
                if two:
                    t = i - 1
                    v.wait_ge(y_done, t + 1)
                    v.scalar_tensor_tensor(g.X[:, ds(t * D, D)], ps_y[:, 0:D], rsum[:, 0:1], g.X[:, ds(t * D, D)],
                                           ALU.mult, ALU.add).then_inc(y_added, 1)
                if one:
                    v.wait_ge(exp_done, i + 1)
                    if least >= 1:
                        v.wait_ge(y_added, i)
                    v.reciprocal(rsum[:], wsum[:]).then_inc(rsum_done, 1)
            staged(2, v, step)


def experts_and_middle(nc, g, dram):
    with ExitStack() as ctx:
        b = Bufs(nc, ctx, "m")
        g.w1_h = b.sb("w1_h", [P, KD, W1_N], F32R)
        g.w1_l = b.sb("w1_l", [P, KD, W1_N], F32R)
        g.w2_h = b.sb("w2_h", [P, NF, D], F32R)
        g.w2_l = b.sb("w2_l", [P, NF, D], F32R)
        with ExitStack() as rctx:
            w2_raw = Bufs(nc, rctx, "mr").sb("w2_raw", [P, NF, D])
            latent_output(nc, g, dram, w2_raw)
            experts(nc, g, "m1", lambda sp: sp.dma_start(g.wb, dram["wb"]).then_inc(g.loaded_wb, 16))
        plain_attention(nc, g, dram)
        experts(nc, g, "m2", lambda sp: sp.dma_start(g.wqkv, dram["wqkv"]).then_inc(g.loaded_wqkv, 16))


def heads_projections(nc, g, dram):
    with ExitStack() as ctx:
        b = Bufs(nc, ctx, "c1")
        ln = LayerNorm(b, g)
        w = g.wqkv
        w_h = b.sb("w_h", [P, KD, 3 * D], F32R)
        w_l = b.sb("w_l", [P, KD, 3 * D], F32R)
        xt_h = b.sb("xt_h", [P, KD * P], F32R)
        xt_l = b.sb("xt_l", [P, KD * P], F32R)
        st = b.sb("st", [P, 2, H, 4, HD], F32R)
        ps_x = b.ps("ps_x", [P, 512])
        ps_qk = b.ps("ps_qk", [P, 512])
        ps_v = b.ps("ps_v", [P, 512])
        ps_t = b.ps("ps_t", [P, 4, 512])
        w_hi = b.sem("w_hi")
        w_lo = b.sem("w_lo")
        xt_hi = b.sem("xt_hi")
        xt_lo = b.sem("xt_lo")
        qk_done = b.sem("qk_done")
        v_done = b.sem("v_done")
        st_hi = b.sem("st_hi")
        st_lo = b.sem("st_lo")
        v_kept = b.sem("v_kept")
        st_t_done = b.sem("st_t_done")
        by_scalar = b.sem("by_scalar")
        by_vector = b.sem("by_vector")
        block = ctx.enter_context(nc.Block())
        qk = ps_qk[:].rearrange("p (a h c) -> p a h c", a=2, c=HD)
        HIGH = (st[:, 0, :, 0:2, :], st[:, 1, :, 0:4:2, :])
        LOW = (st[:, 0, :, 2:4, :], st[:, 1, :, 1:4:2, :])
        twice = [qk[:, a].unsqueeze(2).broadcast_to([P, H, 2, HD]) for a in range(2)]
        parts = ((slice(0, D), HD ** -0.5), (slice(D, 3 * D), 1.0))

        @block.sync
        def _(sp):
            sp.dma_start(g.had[:], dram["had"]).then_inc(g.ffn_loaded, 16)
            sp.dma_start(g.w2f[:], dram["w2f"]).then_inc(g.ffn_loaded, 16)
            sp.dma_start(g.w13_raw[:], dram["w13"]).then_inc(g.ffn_loaded, 16)


        @block.tensor
        def _(pe):
            def step(i, one, two, three, least):
                if three:
                    t = i - 2
                    pe.wait_ge(st_lo, 2 * t + 2)
                    if least >= 3:
                        pe.wait_ge(by_scalar, 2 * t)
                        pe.wait_ge(by_vector, 2 * t)
                    flat = st[:].rearrange("p a h s c -> p (a h s c)").bitcast(F32)
                    for c in range(2 * NP):
                        mm = pe.transpose(ps_t[:, c // 4, (c % 4) * P:(c % 4 + 1) * P], flat[:, c * P:(c + 1) * P],
                                          g.ident[:])
                    mm.then_inc(st_t_done, 1)
                if two:
                    t = i - 1
                    pe.wait_ge(xt_hi, t + 1)
                    pe.wait_ge(xt_lo, t + 1)
                    if least == 1:
                        pe.wait_ge(w_lo, 2)
                    else:
                        pe.wait_ge(st_lo, 2 * t)
                        pe.wait_ge(v_kept, t)
                    for out, cols, sem in ((ps_qk[:], slice(0, 2 * D), qk_done), (ps_v[:, 0:D], slice(2 * D, 3 * D), v_done)):
                        for c in range(KD):
                            cs = slice(c * P, (c + 1) * P)
                            mm = split3(pe, out, (xt_h[:, cs], xt_l[:, cs]), (w_h[:, c, cols], w_l[:, c, cols]),
                                        c == 0, c == KD - 1)
                        mm.then_inc(sem, 1)
                if one:
                    if least >= 1:
                        pe.wait_ge(xt_lo, i)
                    ln.tensor_transpose(pe, ps_x, i)
            staged(3, pe, step)

        @block.scalar
        def _(act):
            act.wait_ge(g.loaded_wqkv, 16)
            for cols, scale in parts:
                act.activation(w_h[:, :, cols], w[:, :, cols], ACT.Copy, scale=scale).then_inc(w_hi, 1)

            def step(i, one, two, three, least):
                if three:
                    t = i - 2
                    act.wait_ge(st_t_done, t + 1)
                    for n in range(2):
                        act.activation(g.qks[:, 4 * n:4 * n + 4, ds(t * P, P)],
                                       ps_t[:, n, :].rearrange("p (k c) -> p k c", c=P), ACT.Copy).then_inc(by_scalar, 1)
                if two:
                    t = i - 1
                    act.wait_ge(qk_done, t + 1)
                    if least >= 2:
                        act.wait_ge(st_t_done, t)
                    for a in range(2):
                        act.activation(HIGH[a], twice[a], ACT.Copy).then_inc(st_hi, 1)
                    act.wait_ge(v_done, t + 1)
                    act.activation(g.vh[:, :, ds(t, 1), :, 0:HD].squeeze(2), ps_v[:, 0:D].rearrange("p (n h c) -> p n h c", h=2, c=HD),
                                   ACT.Copy).then_inc(v_kept, 1)
                if one:
                    act.wait_ge(ln.xn_read, i + 1)
                    if least >= 1:
                        act.wait_ge(v_done, i)
                    act.activation(xt_h[:], ps_x[:, 0:KD * P], ACT.Copy).then_inc(xt_hi, 1)
            staged(3, act, step)

        @block.vector
        def _(v):
            def step(i, one, two, three, least):
                if least == 0:
                    ln.vector_stats(v, i, i)
                if one:
                    ln.vector_scale(v, i, i, least == 0)
                    if has_next(i):
                        ln.vector_stats(v, i + 1, i + 1)
                if least == 0:
                    for n, (cols, scale) in enumerate(parts):
                        v.wait_ge(w_hi, n + 1)
                        v.scalar_tensor_tensor(w_l[:, :, cols], w[:, :, cols], scale, w_h[:, :, cols].bitcast(F32),
                                               ALU.mult, ALU.subtract).then_inc(w_lo, 1)
                if three:
                    t = i - 2
                    v.wait_ge(st_t_done, t + 1)
                    for n in range(2, 4):
                        v.tensor_copy(g.qks[:, 4 * n:4 * n + 4, ds(t * P, P)],
                                      ps_t[:, n, :].rearrange("p (k c) -> p k c", c=P)).then_inc(by_vector, 1)
                if two:
                    t = i - 1
                    v.wait_ge(st_hi, 2 * t + 2)
                    for a in range(2):
                        v.tensor_tensor(LOW[a], twice[a], HIGH[a].bitcast(F32), ALU.subtract).then_inc(st_lo, 1)
                if one:
                    v.wait_ge(xt_hi, i + 1)
                    if least >= 1:
                        v.wait_ge(v_done, i)
                    v.tensor_tensor(xt_l[:], ps_x[:, 0:KD * P], xt_h[:].bitcast(F32), ALU.subtract).then_inc(xt_lo, 1)
            staged(3, v, step)

        @block.gpsimd
        def _(pool):
            pool.memset(g.vh[:, :, :, :, HD:HD + 1], 1.0).then_inc(g.ones_set, 1)
            pool.wait_ge(g.ones_set, 2)

            def step(i, one, least):
                if least == 0:
                    ln.gpsimd_power(pool, i)
                if has_next(i):
                    ln.gpsimd_power(pool, i + 1)
            staged(1, pool, step)


def head_pairs(nc, g):
    with ExitStack() as ctx:
        b = Bufs(nc, ctx, "c2")
        att = NarrowHeads(b, g, HD + 1, g.space)
        q_s = b.sb("q_s", [P, 2, T], F32R)
        k_s = b.sb("k_s", [P, 2, T], F32R)
        v_s = b.sb("v_s", [P, 2, NT, 2, HD + 1])
        slot_loaded = [b.sem(f"slot{s}_loaded") for s in range(2)]
        block = ctx.enter_context(nc.Block())

        @block.sync
        def _(sp):
            def load(j, s, first):
                pair = 2 * j + s
                if not first:
                    sp.wait_ge(att.value_done, att.NU * (pair - 1))
                sp.dma_start(q_s[:, s].bitcast(F32), g.qks[:, ds(pair, 1), :].squeeze(1).bitcast(F32)).then_inc(slot_loaded[s], 16)
                sp.dma_start(k_s[:, s].bitcast(F32), g.qks[:, ds(pair + NP, 1), :].squeeze(1).bitcast(F32)).then_inc(slot_loaded[s], 16)
                sp.dma_start(v_s[:, s], g.vh[:, ds(pair, 1)].squeeze(1)).then_inc(slot_loaded[s], 16)
            for s in range(2):
                load(0, s, True)
            with sp.Fori(1, NP // 2) as j:
                for s in range(2):
                    load(j, s, False)

        @block.tensor
        def _(pe):
            def product(pe, out, s, head, q, k0, k1, stop):
                rows = slice(head * 64, head * 64 + 64)
                return pe.matmul(out, q_s[rows, s, q * P:(q + 1) * P], k_s[rows, s, k0 * P:k1 * P],
                                 start=True, stop=stop)

            def product_t(pe, out, s, head, k, q0, q1):
                rows = slice(head * 64, head * 64 + 64)
                pe.matmul(out, k_s[rows, s, k * P:(k + 1) * P], q_s[rows, s, q0 * P:q1 * P], start=True, stop=False)

            def value(s, head, k):
                return v_s[:, s, k, head, :]

            def pair(n, s, first, last):
                one = isinstance(n, int) and n == 1
                for u in range(att.NU):
                    if u == att.NU - 1 and not last:
                        pe.wait_ge(slot_loaded[1 - s], 24 * (n + 1 - (1 - s)) + 48)
                    back = (lambda: att.transpose_back(pe, n - 1, u, one)) if u < 2 and not first else None
                    att.tensor_step(pe, n, s, u, product, product_t, value, not first, not last, first, back)
            pe.wait_ge(slot_loaded[0], 48)
            pe.wait_ge(att.ones_done, 1)
            for i in range(len(att.S_JOBS[0])):
                att.scores(pe, 0, 0, 0, i, product, True)
            for i in range(att.EARLY):
                att.scores(pe, 0, 0, 1, i, product, True)
            double_pairs(pe, pair)
            for j in range(4):
                att.values(pe, NP - 1, 1, att.NU - 1, j, value, False)
            for blk in range(2):
                att.transpose_back(pe, NP - 1, blk, False)

        @block.scalar
        def _(act):
            def pair(n, s, first, last):
                one = isinstance(n, int) and n == 1
                for u in range(att.NU):
                    if u >= 2:
                        att.keep(act, n, u - 2, first)
                    elif not first:
                        att.keep(act, n - 1, u + 2, one)
                    for i in range(len(att.T_JOBS[u])):
                        att.exponential(act, n, u, i, first)
            act.wait_ge(att.ot_zero, 1)
            double_pairs(act, pair)
            for u in (2, 3):
                att.keep(act, NP - 1, u, False)

        @block.vector
        def _(v):
            def out(n, q0):
                return g.o[:, q0:q0 + 4, ds(2 * n, 2), :]

            def pair(n, s, first, last):
                for u in range(att.NU):
                    att.vector_step(v, n, u, out, not first, not last, first)
            att.make_ones(v)
            v.memset(att.ot[:], 0.0).then_inc(att.ot_zero, 1)
            att.maxima(v, 0, 0, True)
            att.maxima(v, 0, 1, True, "early")
            double_pairs(v, pair)
            for blk in range(2):
                att.result(v, NP - 1, blk, out)


def heads_output(nc, g, dram):
    CH = FF // NT
    with ExitStack() as ctx:
        b = Bufs(nc, ctx, "c3")
        w = b.sb("w", [P, KD, D])
        rden = b.sb("rden", [P, H])
        on = b.sb("on", [P, D])
        ot = b.sb("ot", [P, KD, P])
        fly = b.sb("fly", [P, 2, NFF, D])
        ps_f = b.ps("ps_f", [P, NFF, D])
        had_done = b.sem("had_done")
        fly_start = b.sem("fly_start")
        fly_done = b.sem("fly_done")
        w13_hi = b.sem("w13_hi")
        w13_lo = b.sem("w13_lo")
        ps_t = b.ps("ps_t", [P, 512])
        ps_y = b.ps("ps_y", [P, 512])
        w_loaded = b.sem("w_loaded")
        rden_done = b.sem("rden_done")
        on_done = b.sem("on_done")
        on_t_done = b.sem("on_t_done")
        ot_copied = b.sem("ot_copied")
        y_done = b.sem("y_done")
        y_added = b.sem("y_added")
        block = ctx.enter_context(nc.Block())

        @block.sync
        def _(sp):
            sp.dma_start(w[:], dram["wout"]).then_inc(w_loaded, 16)

        @block.tensor
        def _(pe):
            pe.wait_ge(g.ffn_loaded, 48)
            for k in range(0, NFF, 2):
                for j in range(k, k + 2):
                    mm = pe.matmul(ps_f[:, j, :], g.had[:], g.w2f[:, j, :], start=True, stop=True)
                mm.then_inc(had_done, 1)
            pe.wait_ge(w_loaded, 16)

            def step(i, one, least):
                pe.wait_ge(on_done, i + 1)
                if least >= 1:
                    pe.wait_ge(ot_copied, i)
                for c in range(KD):
                    mm = pe.transpose(ps_t[:, c * P:(c + 1) * P], on[:, c * P:(c + 1) * P], g.ident[:])
                mm.then_inc(on_t_done, 1)
                pe.wait_ge(ot_copied, i + 1)
                if least >= 1:
                    pe.wait_ge(y_added, i)
                for c in range(KD):
                    mm = pe.matmul(ps_y[:, 0:D], ot[:, c, :], w[:, c, :], start=(c == 0), stop=(c == KD - 1))
                mm.then_inc(y_done, 1)
            staged(1, pe, step)

        @block.scalar
        def _(act):
            for k in range(0, NFF, 2):
                act.wait_ge(had_done, k // 2 + 1)
                act.activation(fly[:, 0, k:k + 2, :], ps_f[:, k:k + 2, :], ACT.Copy, scale=FF ** -0.5).then_inc(fly_start, 1)
            act.wait_ge(g.ffn_loaded, 48)

            def step(i, one, least):
                act.wait_ge(on_t_done, i + 1)
                if least >= 1:
                    act.wait_ge(y_done, i)
                act.activation(ot[:], ps_t[:, 0:D].rearrange("p (k c) -> p k c", c=P), ACT.Copy).then_inc(ot_copied, 1)
                cols = ds(i * CH, CH)
                act.activation(g.w13_h[:, :, :, cols], g.w13_raw[:, :, :, cols], ACT.Copy).then_inc(w13_hi, 1)
            staged(1, act, step)

        @block.vector
        def _(v):
            def step(i, one, two, least):
                if one:
                    if least >= 1:
                        v.wait_ge(on_t_done, i)
                    v.reciprocal(rden[:], g.o[:, ds(i, 1), :, HD].squeeze(1)).then_inc(rden_done, 1)
                    v.wait_ge(rden_done, i + 1)
                    v.tensor_tensor(on[:].rearrange("p (h c) -> p h c", c=HD), g.o[:, ds(i, 1), :, 0:HD].squeeze(1),
                                    rden[:].unsqueeze(2).broadcast_to([P, H, HD]), ALU.mult).then_inc(on_done, 1)
                if two:
                    t = i - 1
                    cols = ds(t * CH, CH)
                    v.wait_ge(w13_hi, t + 1)
                    v.tensor_tensor(g.w13_l[:, :, :, cols], g.w13_raw[:, :, :, cols], g.w13_h[:, :, :, cols].bitcast(F32),
                                    ALU.subtract).then_inc(w13_lo, 1)
                    v.wait_ge(y_done, t + 1)
                    v.tensor_tensor(g.X[:, ds(t * D, D)], g.X[:, ds(t * D, D)], ps_y[:, 0:D],
                                    ALU.add).then_inc(y_added, 1)
            staged(2, v, step)

        @block.gpsimd
        def _(pool):
            pool.wait_ge(fly_start, NFF // 2)
            done = 0
            for stage in range(3):
                src = fly[:, stage % 2].rearrange("p (a two j) d -> p a two j d", two=2, j=1 << stage)
                dst = (g.w2f[:] if stage == 2 else fly[:, 1 - stage % 2])\
                    .rearrange("p (a two j) d -> p a two j d", two=2, j=1 << stage)
                if stage:
                    pool.wait_ge(fly_done, done)
                for a in range(src.shape[1]):
                    pool.tensor_tensor(dst[:, a, 0], src[:, a, 0], src[:, a, 1], ALU.add).then_inc(fly_done, 1)
                    pool.tensor_tensor(dst[:, a, 1], src[:, a, 0], src[:, a, 1], ALU.subtract).then_inc(fly_done, 1)
                    done += 2


def many_head_attention(nc, g, dram):
    with ExitStack() as ctx:
        b = Bufs(nc, ctx, "c")
        g.o = b.sb("o", [P, NT, H, HD + 1])
        g.had = b.sb("had", [P, P])
        g.w13_raw = b.sb("w13_raw", [P, 2, KD, FF])
        g.ffn_loaded = b.sem("ffn_loaded")
        with ExitStack() as hctx:
            h = Bufs(nc, hctx, "ch")
            g.qks = h.sb("qks", [P, 2 * NP, T], F32R)
            g.vh = h.sb("vh", [P, NP, NT, 2, HD + 1])
            heads_projections(nc, g, dram)
            head_pairs(nc, g)
        heads_output(nc, g, dram)


HALF = T // 2
HT = NT // 2


def feed_forward(nc, g, tag, split):
    with ExitStack() as ctx:
        b = Bufs(nc, ctx, tag)
        ln = LayerNorm(b, g)
        xt_h = b.sb("xt_h", [P, 2, KD, HALF], F32R)
        xt_l = b.sb("xt_l", [P, 2, KD, HALF], F32R)
        silu = b.sb("silu", [P, 2, HALF])
        full = b.sb("full", [P, 2, HALF])
        hid_h = b.sb("hid_h", [P, NFF, HALF], F32R)
        hid_l = b.sb("hid_l", [P, NFF, HALF], F32R)
        ps_x = b.ps("ps_x", [P, 512])
        ps_g = b.ps("ps_g", [P, 2, 512])
        ps_u = b.ps("ps_u", [P, 2, 512])
        ps_y = b.ps("ps_y", [P, 2, 512])
        xt_hi = b.sem("xt_hi")
        xt_lo = b.sem("xt_lo")
        gate_done = b.sem("gate_done")
        up_done = b.sem("up_done")
        silu_done = b.sem("silu_done")
        full_done = b.sem("full_done")
        hid_hi = b.sem("hid_hi")
        hid_lo = b.sem("hid_lo")
        w2_hi = b.sem("w2_hi")
        w2_lo = b.sem("w2_lo")
        y_done = b.sem("y_done")
        y_added = b.sem("y_added")
        block = ctx.enter_context(nc.Block())

        @block.tensor
        def _(pe):
            def input_tile(t):
                if t:
                    pe.wait_ge(xt_lo, t)
                ln.tensor_transpose(pe, ps_x, t)

            def features(s):
                half, f = divmod(s, NFF)
                fs = slice(f * P, (f + 1) * P)
                for n, (ps, sem) in enumerate(((ps_g, gate_done), (ps_u, up_done))):
                    if s >= 2:
                        pe.wait_ge(full_done, s - 1)
                    for c in range(KD):
                        mm = split3(pe, ps[:, s % 2, :], (g.w13_h[:, n, c, fs], g.w13_l[:, n, c, fs]),
                                    (xt_h[:, half, c, :], xt_l[:, half, c, :]), c == 0, c == KD - 1)
                    mm.then_inc(sem, 1)

            def output(t):
                cols = slice(t % HT * P, (t % HT + 1) * P)
                if t >= 2:
                    pe.wait_ge(y_added, t - 1)
                for f in range(NFF):
                    if t % HT == 0:
                        pe.wait_ge(hid_lo, t // HT * NFF + f + 1)
                    mm = split3(pe, ps_y[:, t % 2, 0:D], (hid_h[:, f, cols], hid_l[:, f, cols]),
                                (g.w2f_h[:, f, :], g.w2f_l[:, f, :]), f == 0, f == NFF - 1)
                mm.then_inc(y_done, 1)

            for t in range(HT):
                input_tile(t)
            pe.wait_ge(xt_hi, HT)
            pe.wait_ge(xt_lo, HT)
            for f in range(NFF):
                features(f)
                if f % 2:
                    input_tile(HT + f // 2)
            if split:
                pe.wait_ge(w2_lo, 1)
            for t in range(HT):
                output(t)
            pe.wait_ge(xt_hi, NT)
            pe.wait_ge(xt_lo, NT)
            for f in range(NFF):
                features(NFF + f)
            for t in range(HT, NT):
                output(t)

        @block.scalar
        def _(act):
            def high(t):
                act.wait_ge(ln.xn_read, t + 1)
                act.activation(xt_h[:, t // HT, :, t % HT * P:(t % HT + 1) * P],
                               ps_x[:, 0:D].rearrange("p (c q) -> p c q", c=KD), ACT.Copy).then_inc(xt_hi, 1)

            def gate(s):
                act.wait_ge(gate_done, s + 1)
                if s >= 2:
                    act.wait_ge(full_done, s - 1)
                act.activation(silu[:, s % 2, :], ps_g[:, s % 2, :], ACT.Silu).then_inc(silu_done, 1)

            def hidden_high(s):
                act.wait_ge(full_done, s + 1)
                if s >= NFF:
                    act.wait_ge(y_done, HT)
                act.activation(hid_h[:, s % NFF, :], full[:, s % 2, :], ACT.Copy).then_inc(hid_hi, 1)

            for t in range(HT):
                high(t)
            if split:
                act.activation(g.w2f_h[:], g.w2f[:], ACT.Copy).then_inc(w2_hi, 1)
            for s in range(2 * NFF):
                gate(s)
                if s < NFF and s % 2:
                    high(HT + s // 2)
                if s % NFF:
                    hidden_high(s - 1)
                if s % NFF == NFF - 1:
                    hidden_high(s)

        @block.vector
        def _(v):
            def low(t):
                v.wait_ge(xt_hi, t + 1)
                half, cols = t // HT, slice(t % HT * P, (t % HT + 1) * P)
                v.tensor_tensor(xt_l[:, half, :, cols], ps_x[:, 0:D].rearrange("p (c q) -> p c q", c=KD),
                                xt_h[:, half, :, cols].bitcast(F32), ALU.subtract).then_inc(xt_lo, 1)

            def norm(t):
                ln.vector_stats(v, t, t)
                ln.vector_scale(v, t, t, t == 0)

            def hidden(s):
                v.wait_ge(silu_done, s + 1)
                v.wait_ge(up_done, s + 1)
                if s >= 2:
                    v.wait_ge(hid_hi, s - 1)
                    v.wait_ge(hid_lo, s - 1)
                v.tensor_tensor(full[:, s % 2, :], ps_u[:, s % 2, :], silu[:, s % 2, :], ALU.mult).then_inc(full_done, 1)

            def add(t):
                v.wait_ge(y_done, t + 1)
                v.tensor_tensor(g.X[:, ds(t * D, D)], g.X[:, ds(t * D, D)], ps_y[:, t % 2, 0:D],
                                ALU.add).then_inc(y_added, 1)

            norm(0)
            for t in range(HT):
                norm(t + 1)
                low(t)
            for f in range(NFF):
                hidden(f)
                if f % 2:
                    t = HT + f // 2
                    low(t)
                    if t + 1 < NT:
                        norm(t + 1)
            for t in range(HT):
                add(t)
            for f in range(NFF):
                hidden(NFF + f)
            for t in range(HT, NT):
                add(t)

        @block.gpsimd
        def _(pool):
            def hidden_low(s):
                pool.wait_ge(hid_hi, s + 1)
                if s >= NFF:
                    pool.wait_ge(y_done, HT)
                pool.tensor_tensor(hid_l[:, s % NFF, :], full[:, s % 2, :], hid_h[:, s % NFF, :].bitcast(F32),
                                   ALU.subtract).then_inc(hid_lo, 1)

            for t in range(HT + 1):
                ln.gpsimd_power(pool, t)
            if split:
                pool.wait_ge(w2_hi, 1)
                pool.tensor_tensor(g.w2f_l[:], g.w2f[:], g.w2f_h[:].bitcast(F32), ALU.subtract).then_inc(w2_lo, 1)
            for s in range(2 * NFF):
                hidden_low(s)
                if s < NFF and s % 2 and HT + s // 2 + 1 < NT:
                    ln.gpsimd_power(pool, HT + s // 2 + 1)


def gated_cumsum(nc, g, dram):
    M = KD
    GH = D // 4
    with ExitStack() as ctx:
        b = Bufs(nc, ctx, "d")
        ln = LayerNorm(b, g)
        w = b.sb("w", [P, KD, 2 * D + GH])
        w_h = b.sb("w_h", [P, KD, 2 * D + GH], F32R)
        w_l = b.sb("w_l", [P, KD, 2 * D + GH], F32R)
        wg2 = b.sb("wg2", [GH, D])
        wu = b.sb("wu", [P, M, D])
        bias = b.sb("bias", [P, 3, M])
        bg1 = b.sb("bg1", [GH, 1])
        taps = b.sb("taps", [P, KD, 4])
        xt = b.sb("xt", [P, KD, T + 2])
        xt_h = b.sb("xt_h", [P, KD, T], F32R)
        xt_l = b.sb("xt_l", [P, KD, T], F32R)
        hidden = b.sb("hidden", [GH, T])
        gates = b.sb("gates", [P, M, T])
        ones = b.sb("ones", [P, T])
        ug = b.sb("ug", [P, M, T])
        vg = b.sb("vg", [P, M, T])
        run = b.sb("run", [P, M, T])
        conv = b.sb("conv", [P, KD, T])
        ps_x = b.ps("ps_x", [P, 512])
        ps_h = b.ps("ps_h", [P, 2, 512])
        ps_uv = b.ps("ps_uv", [P, 2, 512])
        ps_y = b.ps("ps_y", [P, 2, 512])
        loaded = b.sem("loaded")
        small_loaded = b.sem("small_loaded")
        ones_set = b.sem("ones_set")
        w_hi = b.sem("w_hi")
        w_lo = b.sem("w_lo")
        xt_full = b.sem("xt_full")
        xt_hi = b.sem("xt_hi")
        xt_lo = b.sem("xt_lo")
        h_done = b.sem("h_done")
        relu_done = b.sem("relu_done")
        g_done = b.sem("g_done")
        gates_done = b.sem("gates_done")
        uv_done = b.sem("uv_done")
        uv_gated = b.sem("uv_gated")
        run_done = b.sem("run_done")
        out_done = b.sem("out_done")
        conv_done = b.sem("conv_done")
        y_done = b.sem("y_done")
        y_added = b.sem("y_added")
        block = ctx.enter_context(nc.Block())
        halves = [slice(n * HALF, (n + 1) * HALF) for n in range(2)]
        jobs = [(a, m, n) for m in range(M) for a in range(2) for n in range(2)]

        @block.sync
        def _(sp):
            sp.dma_start(w[:], dram["wuvg"]).then_inc(loaded, 16)
            sp.dma_start(wg2[:], dram["wg2"]).then_inc(small_loaded, 16)
            sp.dma_start(wu[:], dram["wu"]).then_inc(small_loaded, 16)
            sp.dma_start(bias[:], dram["bias3"]).then_inc(small_loaded, 16)
            sp.dma_start(bg1[:], dram["bg1"]).then_inc(small_loaded, 16)
            sp.dma_start(taps[:], dram["taps"]).then_inc(small_loaded, 16)

        @block.tensor
        def _(pe):
            def input_tile(t, least):
                if least:
                    pe.wait_ge(xt_full, t)
                    pe.wait_ge(xt_hi, t)
                ln.tensor_transpose(pe, ps_x, t)
            input_tile(0, 0)
            with pe.Fori(1, NT) as t:
                input_tile(t, 1)
            pe.wait_ge(xt_lo, NT)
            pe.wait_ge(w_lo, 1)

            def product(out, cols, n):
                for c in range(KD):
                    mm = split3(pe, out, (w_h[:, c, cols], w_l[:, c, cols]), (xt_h[:, c, halves[n]], xt_l[:, c, halves[n]]),
                                c == 0, c == KD - 1)
                return mm
            for n in range(2):
                product(ps_h[0:GH, n, :], slice(2 * D, 2 * D + GH), n).then_inc(h_done, 1)
            pe.wait_ge(small_loaded, 16 * 5)

            def gate(m):
                for n in range(2):
                    if m == 0:
                        pe.wait_ge(relu_done, n + 1)
                    else:
                        pe.wait_ge(gates_done, n + 1)
                    pe.matmul(ps_h[:, n, :], wg2[:, m * P:(m + 1) * P], hidden[:, halves[n]], start=True,
                              stop=True).then_inc(g_done, 1)

            def uv(j):
                a, m, n = jobs[j]
                if j >= 2:
                    pe.wait_ge(uv_gated, j - 1)
                product(ps_uv[:, j % 2, :], slice(a * D + m * P, a * D + (m + 1) * P), n).then_inc(uv_done, 1)
            pe.wait_ge(relu_done, 2)
            gate(0)
            for j in range(4):
                uv(j)
            gate(1)
            for j in range(4, 8):
                uv(j)
            pe.wait_ge(conv_done, 3 * KD)
            for t in range(NT):
                tokens = slice(t * P, (t + 1) * P)
                if t == 0:
                    pe.wait_ge(out_done, M)
                if t >= 2:
                    pe.wait_ge(y_added, t - 1)
                for m in range(M):
                    pe.matmul(ps_y[:, t % 2, 0:D], run[:, m, tokens], wu[:, m, :], start=(m == 0), stop=False)
                for c in range(KD):
                    mm = pe.matmul(ps_y[:, t % 2, c * P:(c + 1) * P], conv[:, c, tokens], g.ident[:], start=False,
                                   stop=(c == KD - 1))
                mm.then_inc(y_done, 1)

        @block.scalar
        def _(act):
            act.wait_ge(loaded, 16)
            act.activation(w_h[:], w[:], ACT.Copy).then_inc(w_hi, 1)

            def full(t):
                act.wait_ge(ln.xn_read, t + 1)
                act.activation(xt[:, :, ds(t * P + 1, P)], ps_x[:, 0:D].rearrange("p (c q) -> p c q", c=KD),
                               ACT.Copy).then_inc(xt_full, 1)
            full(0)
            with act.Fori(1, NT) as t:
                full(t)
            act.wait_ge(small_loaded, 16 * 5)
            for n in range(2):
                act.wait_ge(h_done, n + 1)
                act.activation(hidden[:, halves[n]], ps_h[0:GH, n, :], ACT.Relu, bias=bg1[:, 0:1]).then_inc(relu_done, 1)
            for m in range(M):
                for n in range(2):
                    act.wait_ge(g_done, 2 * m + n + 1)
                    act.activation(gates[:, m, halves[n]], ps_h[:, n, :], ACT.Sigmoid,
                                   bias=bias[:, 2, m:m + 1]).then_inc(gates_done, 1)

        @block.vector
        def _(v):
            ln.vector_stats(v, 0, 0)
            ln.vector_scale(v, 0, 0, True)
            v.wait_ge(w_hi, 1)
            v.tensor_tensor(w_l[:], w[:], w_h[:].bitcast(F32), ALU.subtract).then_inc(w_lo, 1)

            def high(t):
                v.wait_ge(xt_full, t + 1)
                v.tensor_copy(xt_h[:, :, ds(t * P, P)], ps_x[:, 0:D].rearrange("p (c q) -> p c q", c=KD)).then_inc(xt_hi, 1)

            def step(t):
                ln.vector_stats(v, t + 1, t + 1)
                high(t)
                ln.vector_scale(v, t + 1, t + 1, False)
            step(0)
            with v.Fori(1, NT - 1) as t:
                step(t)
            high(NT - 1)
            v.wait_ge(small_loaded, 16 * 5)

            def gated(j):
                a, m, n = jobs[j]
                v.wait_ge(uv_done, j + 1)
                v.wait_ge(gates_done, 2 * m + n + 1)
                v.scalar_tensor_tensor((ug, vg)[a][:, m, halves[n]], ps_uv[:, j % 2, :], bias[:, a, m:m + 1],
                                       gates[:, m, halves[n]], ALU.add, ALU.mult).then_inc(uv_gated, 1)

            def convolve(c):
                v.wait_ge(ones_set, 2)
                v.tensor_scalar(conv[:, c, :], xt[:, c, 1:T + 1], taps[:, c, 1:2], taps[:, c, 3:4], ALU.mult,
                                ALU.add).then_inc(conv_done, 1)
                for n, tap in enumerate((0, 2)):
                    v.wait_ge(conv_done, 3 * c + n + 1)
                    v.scalar_tensor_tensor(conv[:, c, :], xt[:, c, tap:tap + T], taps[:, c, tap:tap + 1], conv[:, c, :],
                                           ALU.mult, ALU.add).then_inc(conv_done, 1)
            convolve(0)
            for m in range(M):
                for j in range(4 * m, 4 * m + 4):
                    gated(j)
                if m == 0:
                    convolve(1)
                v.wait_ge(uv_gated, 4 * m + 2)
                v.tensor_tensor_scan(run[:, m, :], ones[:], ug[:, m, :], 0.0, ALU.mult, ALU.add).then_inc(run_done, 1)
                v.wait_ge(run_done, m + 1)
                v.wait_ge(uv_gated, 4 * m + 4)
                v.tensor_tensor(run[:, m, :], run[:, m, :], vg[:, m, :], ALU.mult).then_inc(out_done, 1)
            for t in range(NT):
                v.wait_ge(y_done, t + 1)
                v.tensor_tensor(g.X[:, ds(t * D, D)], g.X[:, ds(t * D, D)], ps_y[:, t % 2, 0:D],
                                ALU.add).then_inc(y_added, 1)

        @block.gpsimd
        def _(pool):
            pool.memset(ones[:], 1.0).then_inc(ones_set, 1)
            pool.memset(xt[:, :, 0:T + 2:T + 1], 0.0).then_inc(ones_set, 1)
            ln.gpsimd_power(pool, 0)

            def low(t):
                tokens = ds(t * P, P)
                pool.wait_ge(xt_hi, t + 1)
                pool.tensor_tensor(xt_l[:, :, tokens], xt[:, :, ds(t * P + 1, P)], xt_h[:, :, tokens].bitcast(F32),
                                   ALU.subtract).then_inc(xt_lo, 1)

            def step(t):
                ln.gpsimd_power(pool, t + 1)
                low(t)
            step(0)
            with pool.Fori(1, NT - 1) as t:
                step(t)
            low(NT - 1)


class Persistent:
    pass


def clear_released_semaphores(nc):
    done = sorted(nc.released_uncleared_semaphores)
    runs = []
    for n in done:
        if runs and runs[-1][1] == n:
            runs[-1][1] = n + 1
        else:
            runs.append([n, n + 1])
    with nc.Block() as block:
        @block.gpsimd
        def _(pool):
            for start, end in runs:
                pool.sem_clear(range(start, end))


def build(nc, dram, out):
    with ExitStack() as ctx:
        g = Persistent()
        b = Bufs(nc, ctx, "g")
        X = b.sb("X", [P, NT * D])
        g.X = X
        g.ident = b.sb("ident", [P, P])
        g.ident_b = b.sb("ident_b", [P, P], BF16)
        g.causal = b.sb("causal", [P, P], BF16)
        g.neg_half = b.sb("neg_half", [P, 8])
        g.qnw0 = b.sb("qnw0", [P, 1])
        g.qnw1 = b.sb("qnw1", [QR1, 1])
        g.kvw = b.sb("kvw", [P, 1])
        g.kvw_s = b.sb("kvw_s", [P, 1])
        g.space = b.sb("space", [P, KD * W1_N])
        g.wqkv = g.space[:, 0:KD * 3 * D].rearrange("p (k c) -> p k c", k=KD)
        g.wb = g.space[:, KD * 3 * D:KD * 3 * D + 4 * KD * D].rearrange("p (n k c) -> p n k c", n=4, k=KD)
        g.w1_raw = g.space[:].rearrange("p (k c) -> p k c", k=KD)
        g.loaded_x = b.sem("loaded_x")
        g.loaded_ident = b.sem("loaded_ident")
        g.loaded_const = b.sem("loaded_const")
        g.loaded_wa = b.sem("loaded_wa")
        g.loaded_wr = b.sem("loaded_wr")
        g.loaded_w1 = b.sem("loaded_w1")
        g.loaded_w2 = b.sem("loaded_w2")
        g.loaded_wb = b.sem("loaded_wb")
        g.loaded_wqkv = b.sem("loaded_wqkv")
        g.neg_half_set = b.sem("neg_half_set")
        g.vext_done = b.sem("vext_done")
        g.kvw_scaled = b.sem("kvw_scaled")
        g.ones_set = b.sem("ones_set")
        stored = b.sem("stored")
        g.N_CONST = 6

        with ExitStack() as actx:
            a = Bufs(nc, actx, "a")
            g.wvo = a.sb("wvo", [P, NP, D])
            g.u_space = a.sb("u", [P, NT * H * (KL + 1)])
            g.u = g.u_space[:].rearrange("p (t h c) -> p t h c", h=H, c=KL + 1)
            with ExitStack() as hctx:
                h = Bufs(nc, hctx, "h")
                g.kt_h = h.sb("kt_h", [P, 2, T], F32R)
                g.kt_l = h.sb("kt_l", [P, 2, T], F32R)
                g.vext = h.sb("vext", [P, NT, KL + 1])
                g.qrt = h.sb("qrt", [P, NP, T])
                g.qat0 = h.sb("qat0", [P, T])
                g.qat1 = h.sb("qat1", [QR1, T])
                g.wq = h.sb("wq", [P, NP, 2 * P])
                with ExitStack() as wctx:
                    w = Bufs(nc, wctx, "w")
                    g.cos_q = w.sb("cos_q", [P, NT, DR])
                    g.sin_q = w.sb("sin_q", [P, NT, DR])
                    g.cos_k = w.sb("cos_k", [P, NT, DR])
                    g.sin_k = w.sb("sin_k", [P, NT, DR])
                    g.wa = w.sb("wa", [P, KD, WA_N])
                    g.wr0 = g.u_space[:, 0:H * DR]
                    g.wr1 = g.u_space[0:QR1, H * DR:2 * H * DR]
                    with nc.Block() as block:
                        @block.sync
                        def _(sp):
                            sp.dma_start(X[:].rearrange("p (t d) -> p t d", d=D), dram["x"]).then_inc(g.loaded_x, 16)
                            sp.dma_start(g.wr0, dram["wr"][0:P, :]).then_inc(g.loaded_wr, 16)
                            sp.dma_start(g.wr1, dram["wr"][P:QL, :]).then_inc(g.loaded_wr, 16)
                            sp.dma_start(g.cos_q[:], dram["cos_q"]).then_inc(g.loaded_const, 16)
                            sp.dma_start(g.sin_q[:], dram["sin_q"]).then_inc(g.loaded_const, 16)

                        @block.scalar
                        def _(act):
                            act.dma_start(g.ident[:], dram["ident"]).then_inc(g.loaded_ident, 16)
                            act.dma_start(g.wa[:], dram["wa"]).then_inc(g.loaded_wa, 16)
                            act.dma_start(g.cos_k[:], dram["cos_k"]).then_inc(g.loaded_const, 16)
                            act.dma_start(g.sin_k[:], dram["sin_k"]).then_inc(g.loaded_const, 16)
                            act.dma_start(g.qnw0[:], dram["qnw"][0:P, :]).then_inc(g.loaded_wr, 16)
                            act.dma_start(g.qnw1[:], dram["qnw"][P:QL, :]).then_inc(g.loaded_wr, 16)
                            act.dma_start(g.kvw[:], dram["kvw"]).then_inc(g.loaded_wr, 16)
                            act.dma_start(g.causal[:], dram["causal"]).then_inc(g.loaded_const, 16)
                            act.dma_start(g.ident_b[:], dram["ident_b"]).then_inc(g.loaded_const, 16)

                        @block.gpsimd
                        def _(pool):
                            pool.memset(g.neg_half[:], -0.5).then_inc(g.neg_half_set, 1)
                            pool.memset(g.vext[:], 1.0).then_inc(g.ones_set, 1)
                            pool.wait_ge(g.ones_set, 1)
                    latent_projections(nc, g, dram)
                latent_heads(nc, g, dram)
            experts_and_middle(nc, g, dram)
        clear_released_semaphores(nc)
        f = Bufs(nc, ctx, "f")
        g.w13_h = f.sb("w13_h", [P, 2, KD, FF], F32R)
        g.w13_l = f.sb("w13_l", [P, 2, KD, FF], F32R)
        g.w2f = f.sb("w2f", [P, NFF, D])
        many_head_attention(nc, g, dram)
        g.w2f_h = f.sb("w2f_h", [P, NFF, D], F32R)
        g.w2f_l = f.sb("w2f_l", [P, NFF, D], F32R)
        feed_forward(nc, g, "f1", True)
        gated_cumsum(nc, g, dram)
        feed_forward(nc, g, "f2", False)

        with nc.Block() as block:
            @block.sync
            def _(sp):
                sp.wait_ge(g.loaded_const, 16 * g.N_CONST)
                sp.dma_start(out, X[:].rearrange("p (t d) -> p t d", d=D)).then_inc(stored, 16)
                sp.wait_ge(stored, 16)


def _rope_tables(np):
    inv = np.float32(1.0) / np.float32(10000.0) ** (np.arange(0, DR, 2, dtype=np.float32) / np.float32(DR))
    freqs = np.outer(np.arange(T, dtype=np.float32), inv.astype(np.float32)).astype(np.float32)
    cos, sin = np.cos(freqs), np.sin(freqs)
    lay = lambda a: np.ascontiguousarray(a.reshape(NT, P, DR).transpose(1, 0, 2).astype(np.float32))
    return lay(np.concatenate([cos, cos], 1)), lay(np.concatenate([-sin, sin], 1))


def kernel(**inputs):
    import ml_dtypes
    import numpy as np
    import concourse.bacc as bacc
    from concourse.bass_utils import run_bass_kernel_spmd

    w = {k: np.asarray(v) for k, v in inputs.items()}
    rows = lambda a: np.ascontiguousarray(a.reshape(KD, P, -1).transpose(1, 0, 2))
    cat = np.concatenate
    arrays = {}
    arrays["x"] = np.ascontiguousarray(w["L0_attn_a_hidden_states"][0].reshape(NT, P, D).transpose(1, 0, 2))

    wq_b = w["L0_attn_a_Wq_b"].reshape(QL, H, DN + DR)
    wkv_b = w["L0_attn_a_Wkv_b"].reshape(KL, H, 2 * DN)
    wo = w["L0_attn_a_Wo"].reshape(H, DN, D)
    arrays["wa"] = rows(cat([w["L0_attn_a_Wq_a"], w["L0_attn_a_Wkv_a"], w["L0_attn_a_Wk_rope"]], 1))
    arrays["wr"] = np.ascontiguousarray(wq_b[:, :, DN:]).reshape(QL, H * DR)
    heads = cat([wq_b[:, :, :DN].transpose(1, 2, 0), wkv_b[:, :, :DN].transpose(1, 2, 0),
                 wkv_b[:, :, DN:].transpose(1, 2, 0), wo], 2)
    arrays["wh"] = np.ascontiguousarray(heads.reshape(NP, 2, P, WH_N).transpose(0, 2, 1, 3))
    arrays["qnw"] = w["L0_attn_a_q_norm_w"].reshape(QL, 1)
    arrays["kvw"] = cat([w["L0_attn_a_kv_norm_w"]] * 2).reshape(P, 1)

    w1 = [w["L0_ffn_sw1"].T, w["L0_ffn_sw2"].T, w["L0_ffn_gate_w"].T] + list(w["L0_ffn_w1"])
    arrays["w1"] = rows(cat(w1, 1))
    arrays["w2"] = cat([w["L0_ffn_sw3"].T, w["L0_ffn_w2"].reshape(NE * FI, D)], 0)

    arrays["wb"] = np.stack([rows(w["L0_attn_b_W_q"].T), rows(w["L0_attn_b_W_k"].T), rows(w["L0_attn_b_W_v"].T),
                             rows(w["L0_attn_b_W_o"])], 1)

    arrays["wqkv"] = rows(w["L1_attn_a_w_qkv"])
    arrays["wout"] = rows(w["L1_attn_a_w_out"])

    arrays["w13"] = np.stack([rows(w["L1_ffn_W1"].T), rows(w["L1_ffn_W3"].T)], 1)
    arrays["w2f"] = w["L1_ffn_W2"].T.reshape(NFF, P, D).transpose(1, 0, 2)
    had = np.ones((1, 1), np.float32)
    while had.shape[0] < P:
        had = np.block([[had, had], [had, -had]])
    arrays["had"] = had

    chunks = lambda a: a.reshape(KD, P, -1).transpose(1, 0, 2)
    arrays["wuvg"] = rows(cat([w["L1_attn_b_Wu"].T, w["L1_attn_b_Wv"].T, w["L1_attn_b_Wg1"].T], 1))
    arrays["wg2"] = w["L1_attn_b_Wg2"].T
    arrays["wu"] = rows(w["L1_attn_b_Wu"].T)
    arrays["bias3"] = np.stack([chunks(w[f"L1_attn_b_{n}"])[:, :, 0] for n in ("bu", "bv", "bg2")], 1)
    arrays["bg1"] = w["L1_attn_b_bg1"].reshape(-1, 1)
    arrays["taps"] = cat([chunks(w["L1_attn_b_conv_w"].reshape(D, 3)), chunks(w["L1_attn_b_conv_b"])], 2)

    cos, sin = _rope_tables(np)
    scale = np.float32((DN + DR) ** -0.5)
    arrays["cos_k"], arrays["sin_k"] = cos, sin
    arrays["cos_q"], arrays["sin_q"] = cos * scale, sin * scale
    arrays["ident"] = np.eye(P, dtype=np.float32)
    arrays["ident_b"] = np.eye(P, dtype=ml_dtypes.bfloat16)
    arrays["causal"] = np.where(np.tri(P, dtype=bool), 0.0, -3e38).astype(ml_dtypes.bfloat16)

    nc = bacc.Bacc("TRN2", target_bir_lowering=False, num_devices=1)
    dram = {}
    for name, a in arrays.items():
        a = arrays[name] = np.ascontiguousarray(a)
        dram[name] = nc.dram_tensor(name, a.shape, mybir.dt.from_np(a.dtype), kind="ExternalInput").ap()
    out = nc.dram_tensor("out", (P, NT, D), F32, kind="ExternalOutput").ap()
    build(nc, dram, out)
    r = run_bass_kernel_spmd(nc, [arrays], core_ids=[0])
    got = r.results[0]["out"]
    return np.ascontiguousarray(np.asarray(got).transpose(1, 0, 2)).reshape(1, T, D)
```
